# Optimizing a Trainium2 kernel written in Bass

```python
import numpy as np
import jax
import jax.numpy as jnp

def _softmax(x, axis=-1):
    return jax.nn.softmax(x, axis=axis)

def _gelu(x):
    return jax.nn.gelu(x, approximate=True)

def _silu(x):
    return jax.nn.silu(x)

def _sigmoid(x):
    return jax.nn.sigmoid(x)

def _layernorm(x, axis=-1, eps=1e-05):
    m = jnp.mean(x, axis=axis, keepdims=True)
    v = jnp.var(x, axis=axis, keepdims=True)
    return (x - m) / jnp.sqrt(v + eps)

def _scatter_add(tgt, idx, src, axis=0):
    return tgt.at[idx].add(src)

def _segment_sum(src, seg, n):
    return jax.ops.segment_sum(src, seg, n)
kernel_name = 'mk_vit_tower_cls_d1_tok_img256_r4_dfe823'

def setup_inputs(seed: int=0):
    np.random.seed(seed)
    _w = jnp.asarray

    def _rec_inputs():
        import jax
        import jax.numpy as jnp
        _rk = jax.random.key(seed)
        x = -0.000392918 + 0.999932 * jax.random.normal(jax.random.fold_in(_rk, 1), (4, 64, 64, 64), jnp.float32)
        cls_tok = 0.02 * jax.random.normal(jax.random.fold_in(_rk, 5), (1, 1, 64), jnp.float32)
        return (x, cls_tok)
    x, cls_tok = _rec_inputs()

    def _L0_tok_setup():
        import jax, jax.numpy as jnp
        import numpy as np
        from jax import lax
        BN_EPS = 1e-05
        key = jax.random.key(seed)
        ks = jax.random.split(key, 9)
        B, H, W, C = (16, 64, 64, 64)
        return {'x': jax.random.normal(ks[0], (B, H, W, C), dtype=jnp.float32), 'bn_gamma': jax.random.uniform(ks[1], (C,), dtype=jnp.float32, minval=0.5, maxval=1.5), 'bn_beta': jax.random.normal(ks[2], (C,), dtype=jnp.float32) * 0.1, 'bn_mean': jax.random.normal(ks[3], (C,), dtype=jnp.float32) * 0.1, 'bn_var': jax.random.uniform(ks[4], (C,), dtype=jnp.float32, minval=0.5, maxval=1.5), 'conv_w': jax.random.normal(ks[5], (C, 1, 3, 3), dtype=jnp.float32) * (1.0 / 3.0), 'conv_b': jax.random.normal(ks[6], (C,), dtype=jnp.float32) * 0.1, 'lin_w': jax.random.normal(ks[7], (C, C), dtype=jnp.float32) * (1.0 / np.sqrt(C)), 'lin_b': jax.random.normal(ks[8], (C,), dtype=jnp.float32) * 0.1}
    _L0_tok_all = _L0_tok_setup()
    _L0_tok_in = {k: v for k, v in _L0_tok_all.items() if k in ('bn_gamma', 'bn_beta', 'bn_mean', 'bn_var', 'conv_w', 'conv_b', 'lin_w', 'lin_b')}
    del _L0_tok_all

    def _L0_attn_setup():
        import jax, jax.numpy as jnp
        import numpy as np
        EMBED_DIM = 64
        SEQ_LEN = 1024
        BATCH = 8
        ALPHA = 0.99
        key = jax.random.key(seed)
        k_x, k_w, k_b = jax.random.split(key, 3)
        x = jax.random.normal(k_x, (BATCH, SEQ_LEN, EMBED_DIM), dtype=jnp.float32)
        Wqkv = jax.random.normal(k_w, (EMBED_DIM, 3 * EMBED_DIM), dtype=jnp.float32) * EMBED_DIM ** (-0.5)
        bqkv = jax.random.normal(k_b, (3 * EMBED_DIM,), dtype=jnp.float32) * 0.02
        return {'x': x, 'Wqkv': Wqkv, 'bqkv': bqkv}
    _L0_attn_all = _L0_attn_setup()
    _L0_attn_in = {k: v for k, v in _L0_attn_all.items() if k in ('Wqkv', 'bqkv')}
    del _L0_attn_all

    def _L0_ffn_setup():
        import jax, jax.numpy as jnp
        import numpy as np
        D_IN, D_HID, D_OUT = (64, 128, 64)
        N_EXPERTS, TOP_K = (64, 2)
        B, S = (8, 1024)
        key = jax.random.key(seed)
        ks = jax.random.split(key, 8)
        scale_in = 1.0 / np.sqrt(D_IN)
        scale_hid = 1.0 / np.sqrt(D_HID)
        return {'x': jax.random.normal(ks[0], (B, S, D_IN), dtype=jnp.float32), 'Wr': jax.random.uniform(ks[1], (D_IN, N_EXPERTS), jnp.float32, -scale_in, scale_in), 'br': jax.random.uniform(ks[2], (N_EXPERTS,), jnp.float32, -scale_in, scale_in), 'W1': jax.random.uniform(ks[3], (N_EXPERTS, D_IN, D_HID), jnp.float32, -scale_in, scale_in), 'b1': jax.random.uniform(ks[4], (N_EXPERTS, D_HID), jnp.float32, -scale_in, scale_in), 'W2': jax.random.uniform(ks[5], (N_EXPERTS, D_HID, D_OUT), jnp.float32, -scale_hid, scale_hid), 'b2': jax.random.uniform(ks[6], (N_EXPERTS, D_OUT), jnp.float32, -scale_hid, scale_hid)}
    _L0_ffn_all = _L0_ffn_setup()
    _L0_ffn_in = {k: v for k, v in _L0_ffn_all.items() if k in ('Wr', 'br', 'W1', 'b1', 'W2', 'b2')}
    del _L0_ffn_all
    return {'x': x, 'cls_tok': cls_tok, 'L0_tok_bn_gamma': _L0_tok_in['bn_gamma'], 'L0_tok_bn_beta': _L0_tok_in['bn_beta'], 'L0_tok_bn_mean': _L0_tok_in['bn_mean'], 'L0_tok_bn_var': _L0_tok_in['bn_var'], 'L0_tok_conv_w': _L0_tok_in['conv_w'], 'L0_tok_conv_b': _L0_tok_in['conv_b'], 'L0_tok_lin_w': _L0_tok_in['lin_w'], 'L0_tok_lin_b': _L0_tok_in['lin_b'], 'L0_attn_Wqkv': _L0_attn_in['Wqkv'], 'L0_attn_bqkv': _L0_attn_in['bqkv'], 'L0_ffn_Wr': _L0_ffn_in['Wr'], 'L0_ffn_br': _L0_ffn_in['br'], 'L0_ffn_W1': _L0_ffn_in['W1'], 'L0_ffn_b1': _L0_ffn_in['b1'], 'L0_ffn_W2': _L0_ffn_in['W2'], 'L0_ffn_b2': _L0_ffn_in['b2']}

def reference(x, cls_tok, L0_tok_bn_gamma, L0_tok_bn_beta, L0_tok_bn_mean, L0_tok_bn_var, L0_tok_conv_w, L0_tok_conv_b, L0_tok_lin_w, L0_tok_lin_b, L0_attn_Wqkv, L0_attn_bqkv, L0_ffn_Wr, L0_ffn_br, L0_ffn_W1, L0_ffn_b1, L0_ffn_W2, L0_ffn_b2):
    import jax
    import jax.numpy as jnp

    def _L0_tok_ref(x, bn_gamma, bn_beta, bn_mean, bn_var, conv_w, conv_b, lin_w, lin_b):
        import jax, jax.numpy as jnp
        import numpy as np
        from jax import lax
        BN_EPS = 1e-05
        x = jnp.transpose(x, (0, 3, 1, 2))
        B, C, H, W = x.shape
        scale = bn_gamma / jnp.sqrt(bn_var + BN_EPS)
        shift = bn_beta - bn_mean * scale
        xn = x * scale[None, :, None, None] + shift[None, :, None, None]
        y = lax.conv_general_dilated(xn, conv_w, window_strides=(1, 1), padding='SAME', feature_group_count=C, dimension_numbers=('NCHW', 'OIHW', 'NCHW')) + conv_b[None, :, None, None]
        y = jnp.transpose(y.reshape(B, C, H * W), (0, 2, 1))
        return jnp.einsum('bnc,dc->bnd', y, lin_w) + lin_b

    def _L0_attn_ref(x, Wqkv, bqkv):
        import jax, jax.numpy as jnp
        import numpy as np
        EMBED_DIM = 64
        SEQ_LEN = 1024
        BATCH = 8
        ALPHA = 0.99
        bs, sl, d = x.shape
        qkv = x @ Wqkv + bqkv
        q, k, v = jnp.split(qkv, 3, axis=-1)
        i = jnp.arange(sl, dtype=jnp.float32)
        M = jnp.where(i[:, None] >= i[None, :], jnp.power(jnp.float32(ALPHA), i[:, None] - i[None, :]), 0.0)
        scores = jnp.einsum('bqd,bkd->bqk', q, k) / jnp.sqrt(jnp.float32(d))
        out = jnp.einsum('bqk,bkd->bqd', scores * M, v)
        return out

    def _L0_ffn_ref(x, Wr, br, W1, b1, W2, b2):
        import jax, jax.numpy as jnp
        import numpy as np
        D_IN, D_HID, D_OUT = (64, 128, 64)
        N_EXPERTS, TOP_K = (64, 2)
        B, S = (8, 1024)
        Bx, Sx, D = x.shape
        xf = x.reshape(-1, D)
        T = xf.shape[0]
        E = Wr.shape[1]
        logits = xf @ Wr + br
        topk_logits, topk_idx = jax.lax.top_k(logits, TOP_K)
        gates = jax.nn.softmax(topk_logits, axis=1)
        combine = jnp.zeros((T, E), xf.dtype).at[jnp.arange(T)[:, None], topk_idx].add(gates)
        out = jnp.zeros((T, W2.shape[-1]), xf.dtype)
        for e in range(E):
            h = jax.nn.relu(xf @ W1[e] + b1[e])
            y = h @ W2[e] + b2[e]
            out = out + combine[:, e:e + 1] * y
        return out.reshape(Bx, Sx, -1)
    h = _L0_tok_ref(x, L0_tok_bn_gamma, L0_tok_bn_beta, L0_tok_bn_mean, L0_tok_bn_var, L0_tok_conv_w, L0_tok_conv_b, L0_tok_lin_w, L0_tok_lin_b)
    h = jnp.concatenate([jnp.broadcast_to(cls_tok, (h.shape[0], 1, h.shape[2])), h], axis=1)
    h = h + _L0_attn_ref(_layernorm(h, axis=-1), L0_attn_Wqkv, L0_attn_bqkv)
    h = h + _L0_ffn_ref(_layernorm(h, axis=-1), L0_ffn_Wr, L0_ffn_br, L0_ffn_W1, L0_ffn_b1, L0_ffn_W2, L0_ffn_b2)
    return h

_drawn_inputs = setup_inputs


def setup_inputs(seed=0):
    import zlib

    import numpy as np

    out = dict(_drawn_inputs(seed))
    spreads = {}
    factors = {'cls_tok': 8.0,
     'L0_ffn_Wr': 7.336,
     'L0_ffn_br': 8.0,
     'L0_ffn_W1': 8.0,
     'L0_ffn_b1': 8.0,
     'L0_ffn_W2': 7.364,
     'L0_ffn_b2': 33.048}
    for name, (base, spread) in spreads.items():
        noise = np.random.default_rng([zlib.crc32(name.encode()), seed]).standard_normal(out[name].shape)
        drawn = base * np.exp(spread * noise) if base else spread * noise
        out[name] = jnp.asarray(drawn.astype(out[name].dtype))
    for name, factor in factors.items():
        out[name] = (out[name] * factor).astype(out[name].dtype)
    return out
```

```python
from contextlib import ExitStack

import numpy as np

import concourse.bass as bass
from concourse import mybir

ALU = mybir.AluOpType
ACT = mybir.ActivationFunctionType
AX = mybir.AxisListType
F32 = mybir.dt.float32
BF16 = mybir.dt.bfloat16
U32 = mybir.dt.uint32
I32 = mybir.dt.int32

P = 128
B, IMG, C = 4, 64, 64
NPIX = IMG * IMG
PAD = IMG + 2
PAIRS = B // 2
STEPS = 4
TILES = 2 * STEPS
W = STEPS * P
GROUPS = PAIRS * NPIX // W
GPP = GROUPS // PAIRS
ROWS_G = W // IMG
NT = GROUPS * TILES
E, HID = 64, 128
K2 = 2
TAPS = 9
ALPHA = float(np.float32(0.99))
DECAY = ALPHA ** P
EPS = 1e-5
ROW = C + 4
ONE, GAP, DEST = C, C + 1, C + 2
PICKS = K2 * (B * NPIX + 1)
NBLK = (PICKS + E * (P - 1)) // P
NBLK = -(-NBLK // 16) * 16
SLOTS = NBLK * P
YROWS = K2 * P * NT + K2
ROUND = float(2 ** 23)
FAR = 1000000.0
WCOLS = HID + C
UB = 4
UNITS = NBLK // UB
RING = 4
LAPS = UNITS // RING
FILL = 10

K_ID, K_MASK, K_QDEC, K_TRI = 0, P, 2 * P, 3 * P
K_FIRST, K_KEEP = 4 * P, 4 * P + GROUPS
K_IOTA = K_KEEP + GROUPS
K_DEST = K_IOTA + E
K_VDEC = K_DEST + K2 * NT
K_ROW1 = K_VDEC + 1
K_CDEST = K_ROW1 + 1
K_BLK = K_CDEST + K2
K_SEL = K_BLK + UB
K_EPS = K_SEL + P
K_COLS = K_EPS + 1


def constants():
    k = np.zeros((P, K_COLS), np.float64)
    i = np.arange(P)
    k[:, K_ID:K_ID + P] = np.eye(P)
    k[:, K_MASK:K_MASK + P] = (i[:, None] <= i[None, :]) / DECAY
    k[:, K_QDEC:K_QDEC + P] = ALPHA ** i[None, :] * DECAY / np.sqrt(C)
    k[:, K_TRI:K_TRI + P] = i[:, None] < i[None, :]
    k[:, K_FIRST:K_FIRST + GROUPS] = np.arange(GROUPS) % GPP == 0
    k[:, K_KEEP:K_KEEP + GROUPS] = np.arange(GROUPS) % GPP != 0
    k[:, K_IOTA:K_IOTA + E] = np.arange(E)
    k[:, K_DEST:K_DEST + K2 * NT] = (np.arange(K2)[:, None] * P * NT + np.arange(NT)).reshape(1, -1) + i[:, None] * NT
    k[:, K_VDEC] = ALPHA ** -i.astype(np.float64)
    k[:, K_ROW1] = FAR * (i > 0)
    k[:, K_CDEST:K_CDEST + K2] = K2 * P * NT + np.arange(K2)
    k[:, K_BLK:K_BLK + UB] = (UB * i[:, None] + np.arange(UB)) * P
    k[96, K_SEL:K_SEL + P] = 1
    k[:, K_EPS] = EPS
    return k.astype(np.float32)


CLS = ("mean xc sq ss std rstd hn turned hnT qkv qkvb qk dot att h2 kk vv outer state0 state1 "
       "mean2 xc2 sq2 ss2 std2 rstd2 hn2 turned2 hn2T logit logitb top topi topf hot0 hot1 hots "
       "gap0 gap1 rows dests ceil lim nb incl excl offb pos0s pos1s pos posi").split()


def tower(nc, x, cls_rows, consts, bn, conv_w, conv_b, lin_w, lin_b, wqkv, bqkv_col, bqkv_row,
          wr, br_row, experts, out):
    with ExitStack() as ctx:
        def sb(name, shape, dt=F32):
            return ctx.enter_context(nc.sbuf_tensor(name, shape, dt))

        def psum(name):
            return ctx.enter_context(nc.psum_tensor(name, [P, 512], F32))

        def sem(name):
            return ctx.enter_context(nc.semaphore(name))

        slots = nc.dram_tensor("slot_rows", [SLOTS, ROW], F32, kind="Internal").ap()
        ybuf = nc.dram_tensor("gated_results", [YROWS, C], F32, kind="Internal").ap()

        blk_dram = nc.dram_tensor("block_experts", [P, UB], I32, kind="Internal").ap()

        ps_conv = psum("ps_conv")
        ps_tok = psum("ps_tok")
        ps_turn = psum("ps_turn")
        ps_q = psum("ps_q")
        ps_k = psum("ps_k")
        ps_v = psum("ps_v")
        ps_p = psum("ps_p")
        ps_o = psum("ps_o")

        kc = sb("kc", [P, K_COLS])
        wall = sb("wall", [P, E * WCOLS])
        xs = wall[:, 0:PAIRS * 32 * P].rearrange("p (q j c) -> p q j c", q=PAIRS, j=32)
        img = sb("img", [P, PAIRS, PAD, PAD])
        h2 = sb("h2", [P, NT, C])
        bn_s = sb("bn_s", [P, 8])
        cw = sb("cw", [P, TAPS + 1])
        linT = sb("linT", [P, P])
        lb = sb("lb", [P, 2])
        wtap = sb("wtap", [P, TAPS, P])
        wq = sb("wq", [P, 3, P])
        bq = sb("bq", [P, 3])
        bqr = sb("bqr", [P, 3 * C])
        wrs = sb("wrs", [P, P])
        brr = sb("brr", [P, E])
        tri = sb("tri", [P, P], BF16)
        ones = sb("ones", [P, P], BF16)
        empty = sb("empty", [P, FILL, ROW])
        hT = sb("hT", [P, W])
        h = sb("h", [P, TILES, C])
        xc = sb("xc", [P, TILES, C])
        sq = sb("sq", [P, TILES, C])
        hn = sb("hn", [P, TILES, C])
        xc2 = sb("xc2", [P, TILES, C])
        sq2 = sb("sq2", [P, TILES, C])
        hn2 = sb("hn2", [P, TILES, C])
        hn2r = sb("hn2r", [P, TILES, C])
        ssum = sb("ssum", [P, 3, TILES])
        ssum2 = sb("ssum2", [P, 3, TILES])
        hnT = sb("hnT", [P, W])
        hn2T = sb("hn2T", [P, W])
        qT = sb("qT", [P, W])
        kT = sb("kT", [P, W])
        vT = sb("vT", [P, W])
        ktok = sb("ktok", [P, W])
        vtok = sb("vtok", [P, W])
        am = sb("am", [P, 2, W])
        state = sb("state", [P, STEPS + 1, P])
        state0 = sb("state0", [P, P])
        st_in = sb("st_in", [P, P])
        logit = sb("logit", [P, TILES, E])
        top = sb("top", [P, TILES, 8])
        topi = sb("topi", [P, TILES, 8], U32)
        topf = sb("topf", [P, K2, TILES])
        hot = sb("hot", [P, K2, TILES, E], BF16)
        hots = sb("hots", [P, TILES, E], BF16)
        tail = sb("tail", [P, K2, TILES, 4])
        rank = sb("rank", [P, TILES, E])
        pick = sb("pick", [P, K2, TILES, E])
        past = pick[:, 0]
        posf = sb("posf", [P, K2, TILES])
        posi = sb("posi", [P, K2 * TILES], U32)
        rows = sb("rows", [P, K2, TILES, ROW])
        cnt = sb("cnt", [P, E])
        lim = sb("lim", [P, E])
        offa = sb("offa", [P, E])
        small = sb("small", [P, 10, E])
        zero = sb("zero", [P, E])
        first_all = sb("first_all", [P, GROUPS + 1, E])
        end_all = sb("end_all", [P, GROUPS + 1, E])
        cl = sb("cl", [P, C])
        ch2 = sb("ch2", [P, C])
        cb = sb("cb", [P, 17, C])
        crow = sb("crow", [P, K2, ROW])
        ctop = sb("ctop", [P, 8])
        ctopi = sb("ctopi", [P, 8], U32)
        cs = sb("cs", [P, 16])
        cposi = sb("cposi", [P, K2], U32)
        chots = sb("chots", [P, E])
        ck2 = sb("ck2", [P, 2, P])
        blk_f = sb("blk_f", [P, UB])
        blk_i = sb("blk_i", [P, UB], I32)
        blk_row = sb("blk_row", [1, P * UB], I32)
        spare = img[:, :, :, :].rearrange("p a b c -> p (a b c)")
        at = [0]

        def reuse(n):
            at[0] += n
            return spare[:, at[0] - n:at[0]]
        xin = [reuse(UB * ROW).rearrange("p (k c) -> p k c", k=UB) for _ in range(RING)]
        ysb = [reuse(UB * C).rearrange("p (k c) -> p k c", k=UB) for _ in range(RING)]
        xT = [reuse(W) for _ in range(2)]
        hid = [reuse(W) for _ in range(2)]
        stage = [reuse(UB * WCOLS).rearrange("p (k c) -> p k c", k=UB) for _ in range(2)]
        blk_in = reuse((GROUPS + 1) * E).rearrange("p (g e) -> p g e", e=E)
        gate = [[reuse(2 * UB).rearrange("p (a k) -> p a k", a=2) for _ in range(RING)] for _ in range(3)]
        ydst = [sb(f"ydst{r}", [P, UB], U32) for r in range(RING)]
        FT = 16
        yin = [wall[:, i * K2 * FT * C:(i + 1) * K2 * FT * C].rearrange("p (k t c) -> p k t c", k=K2, t=FT)
               for i in range(4)]
        ycls = sb("ycls", [1, K2, C])
        osb = sb("osb", [1, C])

        ident = kc[:, K_ID:K_ID + P]

        def wide(ap, n=TILES):
            return ap.unsqueeze(2).to_broadcast([P, n, C])

        def all_tiles(ap):
            return ap.unsqueeze(1).to_broadcast([P, TILES, E])

        consts_in = sem("consts_in")
        x_in = [sem(f"x_in{q}") for q in range(PAIRS)]
        setup_v = sem("setup_v")
        bn_std = sem("bn_std")
        zeroed = sem("zeroed")
        bias_mm = sem("bias_mm")
        bias_ok = sem("bias_ok")
        turned_x = sem("turned_x")
        img_ok = sem("img_ok")
        filled = sem("filled")
        weights_in = sem("weights_in")
        cls_step = sem("cls_step")
        cls_sent = sem("cls_sent")
        s_conv = sem("s_conv")
        s_hT = sem("s_hT")
        s_htok = sem("s_htok")
        s_h = sem("s_h")
        s_ln1 = sem("s_ln1")
        s_sq1 = sem("s_sq1")
        s_turn1 = sem("s_turn1")
        s_hnT = sem("s_hnT")
        s_qmm = sem("s_qmm")
        s_kmm = sem("s_kmm")
        s_vmm = sem("s_vmm")
        s_q = sem("s_q")
        s_k = sem("s_k")
        s_v = sem("s_v")
        s_kturn = sem("s_kturn")
        s_vturn = sem("s_vturn")
        s_ktok = sem("s_ktok")
        s_vtok = sem("s_vtok")
        s_score = sem("s_score")
        s_am = sem("s_am")
        s_pmm = sem("s_pmm")
        s_stin = sem("s_stin")
        s_state = sem("s_state")
        s_omm = sem("s_omm")
        s_h2 = sem("s_h2")
        s_ln2 = sem("s_ln2")
        s_sq2 = sem("s_sq2")
        s_turn2 = sem("s_turn2")
        s_hn2T = sem("s_hn2T")
        s_hn2r = sem("s_hn2r")
        s_lmm = sem("s_lmm")
        s_logit = sem("s_logit")
        s_top = sem("s_top")
        s_topi = sem("s_topi")
        s_hot = sem("s_hot")
        s_tail = sem("s_tail")
        s_rank = sem("s_rank")
        s_alloc = sem("s_alloc")
        s_pos = sem("s_pos")
        s_rows = sem("s_rows")
        s_sent = [sem(f"s_sent{s}") for s in range(STEPS)]
        s_blk = sem("s_blk")
        blk_out = sem("blk_out")
        blk_in_row = sem("blk_in_row")
        u_in = [sem(f"u_in{r}") for r in range(RING)]
        u_stage = sem("u_stage")
        u_turn = sem("u_turn")
        u_xT = sem("u_xT")
        u_hmm = sem("u_hmm")
        u_hid = sem("u_hid")
        u_ymm = sem("u_ymm")
        u_y = sem("u_y")
        u_dst = sem("u_dst")
        u_gap = sem("u_gap")
        u_exp = sem("u_exp")
        u_gate = sem("u_gate")
        u_sent = [sem(f"u_sent{r}") for r in range(RING)]
        y_in = [sem(f"y_in{r}") for r in range(4)]
        y_sum = sem("y_sum")
        cls_y = sem("cls_y")
        out_done = sem("out_done")

        ALLOC, POS, LN, TAIL = 15, 7, 5, 3
        SETUP_V = 5 + TAPS

        def later(g):
            return not (isinstance(g, int) and g == 0)

        def pipeline(eng, *stages):
            depth = max(lag for lag, _ in stages)
            for i in range(MAX_LAG + 1):
                for lag, f in stages:
                    if i >= lag:
                        f(i - lag)
            with eng.Fori(MAX_LAG + 1, GROUPS) as i:
                for lag, f in stages:
                    f(i - lag)
            for i in range(GROUPS, GROUPS + MAX_LAG):
                for lag, f in stages:
                    if i - lag < GROUPS:
                        f(i - lag)

        MAX_LAG = 3

        def unit(n, r):
            return n * RING + r

        def older(n, r):
            return not isinstance(n, int) or unit(n, r) >= 2

        def cls_after(eng, *names):
            eng.wait_ge(cls_step, max(CLS.index(n) for n in names) + 1)

        block = ctx.enter_context(nc.Block())

        @block.sync
        def _(sp):
            loads = [(kc[:], consts), (cl[:], cls_rows), (bn_s[:, 0:4], bn), (cw[:, 0:TAPS], conv_w),
                     (cw[:, TAPS:TAPS + 1], conv_b), (linT[:], lin_w), (lb[:, 0:1], lin_b),
                     (wq[:], wqkv), (bq[:], bqkv_col), (bqr[:], bqkv_row), (wrs[:], wr), (brr[:], br_row)]
            for q in range(PAIRS):
                for b in range(2):
                    sp.dma_start(xs[:, q, :, b * C:(b + 1) * C],
                                 x[2 * q + b].rearrange("(p j) c -> p j c", p=P)).then_inc(x_in[q], 16)
                if q == 0:
                    for dst, src in loads:
                        sp.dma_start(dst, src).then_inc(consts_in, 16)
            sp.wait_ge(zeroed, 4)
            fill = slots.rearrange("(p n f) c -> n p f c", p=P, f=FILL)
            for n in range(NBLK // FILL):
                sp.dma_start(fill[n], empty[:]).then_inc(filled, 16)
            sp.wait_ge(turned_x, PAIRS * 8)
            sp.dma_start(wall[:], experts).then_inc(weights_in, 16)

            sp.wait_ge(s_blk, 3 * UB + 1)
            sp.dma_start(blk_dram, blk_i[:]).then_inc(blk_out, 16)
            sp.wait_ge(blk_out, 16)
            sp.dma_start(blk_row[:], blk_dram.rearrange("p (o k) -> o (p k)", o=1)).then_inc(blk_in_row, 16)
            sp.wait_ge(cls_sent, 32)
            for s in range(STEPS):
                sp.wait_ge(s_sent[s], GROUPS * 64)
            by_unit = slots.rearrange("(u k p) c -> u p k c", k=UB, p=P)
            sp.wait_ge(weights_in, 16)

            def load_unit(n, r, old):
                u = unit(n, r)
                if old:
                    before = sp.snap(u - RING + 1)
                    sp.wait_ge(u_turn, before)
                    sp.wait_ge(u_dst, before)
                    sp.wait_ge(u_exp, before)
                sp.dma_start(xin[r], by_unit[bass.ds(u, 1)].rearrange("o p k c -> p (o k) c")).then_inc(u_in[r], 16)
            for r in range(RING):
                load_unit(0, r, False)
            with sp.Fori(1, LAPS) as n:
                for r in range(RING):
                    load_unit(n, r, True)
            for r in range(RING):
                sp.wait_ge(u_sent[r], UNITS // RING * UB * 16)
            by_tile = ybuf[0:K2 * P * NT].rearrange("(k p t) c -> p k t c", k=K2, p=P)
            sp.dma_start(ycls[:], ybuf[K2 * P * NT:YROWS].unsqueeze(0)).then_inc(cls_y, 16)
            for n in range(NT // FT):
                if n >= 4:
                    sp.wait_ge(y_sum, 2 * (n - 3))
                sp.dma_start(yin[n % 4], by_tile[:, :, n * FT:(n + 1) * FT, :]).then_inc(y_in[n % 4], 16)
            sp.wait_ge(out_done, 16 * (B * NT // FT // 2 + B))

        @block.gpsimd
        def _(pool):
            pool.wait_ge(filled, 16 * (NBLK // FILL))
            cls_after(pool, "posi")
            for k in range(K2):
                nc.gpsimd.indirect_dma_start(slots, bass.IndirectOffsetOnAxis(cposi[0:2, k:k + 1], 0),
                                             crow[0:2, k, :], None, bounds_check=SLOTS - 1,
                                             oob_is_err=False).then_inc(cls_sent, 16)

            last_y = pool.alloc_register("last_y")
            pool.reg_mov(last_y, YROWS - 1)
            rows_wanted = pool.alloc_register("rows_wanted")
            pool.reg_mov(rows_wanted, 2)
            y_wanted = pool.alloc_register("y_wanted")
            pool.reg_mov(y_wanted, 1)

            def scatter(g):
                for s in range(STEPS):
                    wanted = pool.snap(rows_wanted)
                    if s == 0:
                        pool.wait_ge(s_pos, POS * (g + 1))
                    pool.wait_ge(s_rows, wanted)
                    pool.reg_add(rows_wanted, rows_wanted, 2)
                    for k in range(K2):
                        for b in range(2):
                            t = 2 * s + b
                            nc.gpsimd.indirect_dma_start(
                                slots, bass.IndirectOffsetOnAxis(posi[:, k * TILES + t:k * TILES + t + 1], 0),
                                rows[:, k, t, :], None).then_inc(s_sent[s], 16)

            with pool.Fori(0, GROUPS) as g:
                scatter(g)
            with pool.Fori(0, LAPS) as n:
                for r in range(RING):
                    wanted = pool.snap(y_wanted)
                    pool.wait_ge(u_dst, n * RING + r + 1)
                    pool.wait_ge(u_y, wanted)
                    pool.reg_add(y_wanted, y_wanted, 1)
                    for k in range(UB):
                        nc.gpsimd.indirect_dma_start(
                            ybuf, bass.IndirectOffsetOnAxis(ydst[r][:, k:k + 1], 0), ysb[r][:, k, :], None,
                            bounds_check=last_y, oob_is_err=False).then_inc(u_sent[r], 16)

        @block.tensor
        def _(pe):
            pe.wait_ge(consts_in, 12 * 16)
            pe.matmul(ps_o[:, 0:1], linT[:], cw[:, TAPS:TAPS + 1], start=True, stop=True).then_inc(bias_mm, 1)
            banks = [ps_conv, ps_tok]
            for q in range(PAIRS):
                pe.wait_ge(x_in[q], 32)
                for n in range(8):
                    i = 8 * q + n
                    if i >= 2:
                        pe.wait_ge(img_ok, i - 1)
                    for j in range(4):
                        m = pe.transpose(banks[i % 2][:, j * P:(j + 1) * P], xs[:, q, 4 * n + j, :], ident)
                    m.then_inc(turned_x, 1)

            cls_after(pe, "hn")
            pe.transpose(ps_turn[0:C, 0:P], cb[:, 3, :], ident).then_inc(cls_step, 1)
            cls_after(pe, "hnT")
            pe.matmul(ps_q[:, 0:3 * C], ck2[0:C, 0, :], wq[0:C, :, 0:C], start=True, stop=True
                      ).then_inc(cls_step, 1)
            cls_after(pe, "kk", "vv")
            pe.matmul(ps_k[:, 0:P], ck2[0:1, 0, :], ck2[0:1, 1, :], start=True, stop=True
                      ).then_inc(cls_step, 1)
            cls_after(pe, "hn2")
            pe.transpose(ps_turn[0:C, 0:P], cb[:, 11, :], ident).then_inc(cls_step, 1)
            cls_after(pe, "hn2T")
            pe.matmul(ps_q[:, 0:E], ck2[0:C, 0, :], wrs[0:C, 0:E], start=True, stop=True
                      ).then_inc(cls_step, 1)
            cls_after(pe, "posi")

            def taps(g, lo, hi):
                if lo == 0:
                    if later(g):
                        pe.wait_ge(s_hT, g)
                pair, y0 = (g // GPP, g % GPP * ROWS_G)
                for tap in range(lo, hi):
                    dy, dx = divmod(tap, 3)
                    if isinstance(g, int):
                        view = img[:, pair, y0 + dy:y0 + dy + ROWS_G, dx:dx + IMG]
                    else:
                        row = pair * PAD + y0 + dy
                        view = img[:, :, :, :].rearrange("p a b c -> p (a b) c")[:, bass.ds(row, ROWS_G), dx:dx + IMG]
                    m = pe.matmul(ps_conv[:, :], wtap[:, tap, :], view, start=tap == 0, stop=tap == TAPS - 1,
                                  skip_group_check=True)
                if hi == TAPS:
                    m.then_inc(s_conv, 1)

            def turn_hn(g):
                pe.wait_ge(s_ln1, LN * (g + 1))
                if isinstance(g, int):
                    if g >= 2:
                        pe.wait_ge(s_hn2T, g - 1)
                else:
                    pe.wait_ge(s_hn2T, g - 1)
                for s in range(STEPS):
                    m = pe.transpose(ps_turn[:, s * P:(s + 1) * P],
                                     hn[:, 2 * s:2 * s + 2, :].rearrange("p t c -> p (t c)"), ident)
                m.then_inc(s_turn1, 1)

            def ranks(g):
                pe.wait_ge(s_hot, 3 * (g + 1))
                late = g + 1
                pe.wait_ge(s_state, 2 * STEPS * min_groups(g, 2))
                flat = hots[:].rearrange("p t e -> p (t e)")
                pe.matmul(ps_p[:, :], tri[:], flat, start=True, stop=False, skip_group_check=True)
                for k in range(1, TILES):
                    m = pe.matmul(ps_p[:, k * E:], ones[:], flat[:, 0:(TILES - k) * E], start=False,
                                  stop=k == TILES - 1, skip_group_check=True)
                pe.wait_ge(s_h2, min_groups(g, 2))
                for t in range(TILES):
                    m = pe.matmul(ps_o[:, 0:E], ones[:], hots[:, t, :], start=t == 0, stop=t == TILES - 1,
                                  skip_group_check=True)
                m.then_inc(s_rank, 1)

            def qkv(g):
                pe.wait_ge(s_hnT, g + 1)
                if not isinstance(g, int) or g >= 2:
                    pe.wait_ge(s_logit, g - 1)
                if later(g):
                    pe.wait_ge(s_am, 2 * g)
                    pe.wait_ge(s_vtok, g)
                for n, (bank, done) in enumerate(((ps_q, s_qmm), (ps_k, s_kmm), (ps_v, s_vmm))):
                    pe.matmul(bank[:, :], wq[:, n, :], hnT[:], start=True, stop=True).then_inc(done, 1)

            def turn_kv(g):
                pe.wait_ge(s_k, g + 1)
                pe.wait_ge(s_h, min_groups(g, 1))
                for s in range(STEPS):
                    m = pe.transpose(ps_tok[:, s * P:(s + 1) * P], kT[:, s * P:(s + 1) * P], ident)
                m.then_inc(s_kturn, 1)
                pe.wait_ge(s_v, g + 1)
                for s in range(STEPS):
                    m = pe.transpose(ps_v[:, s * P:(s + 1) * P], vT[:, s * P:(s + 1) * P], ident)
                m.then_inc(s_vturn, 1)

            def scores(g):
                pe.wait_ge(s_q, g + 1)
                for b, bank in ((0, ps_q), (1, ps_k)):
                    for s in range(STEPS):
                        m = pe.matmul(bank[:, s * P:(s + 1) * P], kT[b * C:(b + 1) * C, s * P:(s + 1) * P],
                                      qT[b * C:(b + 1) * C, s * P:(s + 1) * P], start=True, stop=True)
                    m.then_inc(s_score, 1)

            def products(g):
                pe.wait_ge(s_ktok, g + 1)
                pe.wait_ge(s_vtok, g + 1)
                if not isinstance(g, int) or g >= 2:
                    pe.wait_ge(s_pos, POS * (g - 2) + 1)
                for s in range(STEPS):
                    m = pe.matmul(ps_p[:, s * P:(s + 1) * P], ktok[:, s * P:(s + 1) * P],
                                  vtok[:, s * P:(s + 1) * P], start=True, stop=True)
                m.then_inc(s_pmm, 1)

            def attend(g):
                pe.wait_ge(s_state, 2 * STEPS * g + 2 * (STEPS - 1))
                pe.wait_ge(s_stin, 2 * (g + 1))
                pe.wait_ge(s_am, 2 * (g + 1))
                if not isinstance(g, int) or g >= 2:
                    pe.wait_ge(s_alloc, ALLOC * (g - 2) + 1)
                for s in range(STEPS):
                    c0 = s * P
                    pe.matmul(ps_o[:, c0:c0 + P], qT[:, c0:c0 + P], state[:, s, :], start=True, stop=False,
                              skip_group_check=True)
                    for b in range(2):
                        m = pe.matmul(ps_o[:, c0 + b * C:c0 + (b + 1) * C], am[:, b, c0:c0 + P],
                                      vtok[:, c0 + b * C:c0 + (b + 1) * C], start=False, stop=b == 1,
                                      skip_group_check=True)
                m.then_inc(s_omm, 1)

            def turn_hn2(g):
                pe.wait_ge(s_ln2, LN * (g + 1))
                pe.wait_ge(s_hnT, min_groups(g, 2))
                for s in range(STEPS):
                    m = pe.transpose(ps_turn[:, s * P:(s + 1) * P],
                                     hn2[:, 2 * s:2 * s + 2, :].rearrange("p t c -> p (t c)"), ident)
                m.then_inc(s_turn2, 1)

            def router(g):
                pe.wait_ge(s_hn2T, g + 1)
                pe.wait_ge(s_am, 2 * min_groups(g, 2))
                for s in range(STEPS):
                    m = pe.matmul(ps_q[:, s * P:(s + 1) * P], hn2T[:, s * P:(s + 1) * P], wrs[:],
                                  start=True, stop=True)
                m.then_inc(s_lmm, 1)

            def turn_h(g):
                pe.wait_ge(s_hT, g + 1)
                if later(g):
                    pe.wait_ge(s_ktok, g)
                for s in range(STEPS):
                    m = pe.transpose(ps_tok[:, s * P:(s + 1) * P], hT[:, s * P:(s + 1) * P], ident)
                m.then_inc(s_htok, 1)

            def min_groups(g, ahead):
                if isinstance(g, int):
                    return min(g + ahead, GROUPS) if ahead != 1 else min(g + 1, GROUPS)
                return g + ahead

            pe.wait_ge(bias_ok, 1)
            pe.wait_ge(img_ok, PAIRS * 8)
            pe.wait_ge(setup_v, SETUP_V)
            pipeline(pe,
                     (1, turn_hn), (3, ranks), (1, qkv),
                     (0, lambda g: taps(g, 0, 3)), (1, turn_kv), (1, scores), (0, lambda g: taps(g, 3, 5)),
                     (1, products), (2, turn_hn2), (2, router), (1, attend),
                     (0, lambda g: taps(g, 5, TAPS)), (0, turn_h))

            def unit_turn(n, r):
                u = unit(n, r)
                pe.wait_ge(u_in[r], 16 * (n + 1))
                if older(n, r):
                    pe.wait_ge(u_xT, u - 1)
                bank = (ps_conv, ps_tok)[r % 2]
                for k in range(UB):
                    m = pe.transpose(bank[0:ONE + 1, k * P:(k + 1) * P], xin[r][:, k, 0:ONE + 1], ident)
                m.then_inc(u_turn, 1)

            def unit_hidden(n, r):
                u = unit(n, r)
                pe.wait_ge(u_xT, u + 1)
                pe.wait_ge(u_stage, UB * (u + 1))
                if older(n, r):
                    pe.wait_ge(u_hid, u - 1)
                bank = (ps_q, ps_k)[r % 2]
                for k in range(UB):
                    m = pe.matmul(bank[:, k * P:(k + 1) * P], stage[r % 2][0:ONE + 1, k, 0:HID],
                                  xT[r % 2][0:ONE + 1, k * P:(k + 1) * P], start=True, stop=True)
                m.then_inc(u_hmm, 1)

            def unit_out(n, r):
                u = unit(n, r)
                pe.wait_ge(u_hid, u + 1)
                if older(n, r):
                    pe.wait_ge(u_y, u - 1)
                bank = (ps_v, ps_p)[r % 2]
                for k in range(UB):
                    pe.matmul(bank[:, k * C:(k + 1) * C], hid[r % 2][:, k * P:(k + 1) * P],
                              stage[r % 2][:, k, HID:WCOLS], start=True, stop=False, skip_group_check=True)
                    m = pe.matmul(bank[:, k * C:(k + 1) * C], kc[:, K_SEL:K_SEL + P], stage[r % 2][:, k, 0:C],
                                  start=False, stop=True, skip_group_check=True)
                m.then_inc(u_ymm, 1)

            def lap(n):
                for r in range(RING):
                    unit_turn(n, r)
                    unit_hidden(n, r)
                    if r:
                        unit_out(n, r - 1)
                    elif later(n):
                        unit_out(n - 1, RING - 1)

            lap(0)
            with pe.Fori(1, LAPS) as n:
                lap(n)
            unit_out(LAPS - 1, RING - 1)


        @block.vector
        def _(v):
            v.memset(img[:], 0.0).then_inc(zeroed, 1)
            v.memset(empty[:], 0.0).then_inc(zeroed, 1)
            v.wait_ge(zeroed, 2)
            v.memset(empty[:, :, DEST:DEST + 1], FAR).then_inc(zeroed, 1)
            v.memset(state[:], 0.0).then_inc(zeroed, 1)
            v.memset(state0[:], 0.0).then_inc(zeroed, 1)
            v.memset(ones[:], 1.0).then_inc(zeroed, 1)
            v.memset(zero[:], 0.0).then_inc(zeroed, 1)
            v.memset(offa[:], 0.0).then_inc(zeroed, 1)
            v.memset(tail[:], 0.0).then_inc(zeroed, 1)
            v.memset(crow[:], 0.0).then_inc(zeroed, 1)
            v.wait_ge(zeroed, 10)
            v.memset(tail[:, :, :, 0:1], 1.0).then_inc(zeroed, 1)
            v.memset(crow[:, :, ONE:ONE + 1], 1.0).then_inc(zeroed, 1)
            v.wait_ge(consts_in, 12 * 16)
            v.wait_ge(bn_std, 1)
            v.reciprocal(bn_s[:, 4:5], bn_s[:, 4:5]).then_inc(setup_v, 1)
            v.wait_ge(setup_v, 1)
            v.tensor_tensor(bn_s[:, 5:6], bn_s[:, 4:5], bn_s[:, 0:1], ALU.mult).then_inc(setup_v, 1)
            v.wait_ge(setup_v, 2)
            v.tensor_tensor(bn_s[:, 6:7], bn_s[:, 5:6], bn_s[:, 2:3], ALU.mult).then_inc(setup_v, 1)
            v.wait_ge(setup_v, 3)
            v.tensor_tensor(bn_s[:, 7:8], bn_s[:, 1:2], bn_s[:, 6:7], ALU.subtract).then_inc(setup_v, 1)
            v.tensor_copy(tri[:], kc[:, K_TRI:K_TRI + P]).then_inc(setup_v, 1)
            for tap in range(TAPS):
                v.tensor_scalar(wtap[:, tap, :], linT[:], cw[:, tap:tap + 1], None, ALU.mult).then_inc(setup_v, 1)
            v.wait_ge(bias_mm, 1)
            v.tensor_tensor(lb[:, 1:2], ps_o[:, 0:1], lb[:, 0:1], ALU.add).then_inc(bias_ok, 1)

            def done(ins, name):
                assert name in CLS
                ins.then_inc(cls_step, 1)

            def norm_cls(src, o, s, tag):
                v.tensor_reduce(cs[:, s:s + 1], src, AX.X, ALU.add).then_inc(cls_step, 1)
                cls_after(v, "mean" + tag)
                v.scalar_tensor_tensor(cb[:, o, :], cs[:, s:s + 1].to_broadcast([P, C]), -1.0 / C, src,
                                       ALU.mult, ALU.add).then_inc(cls_step, 1)
                cls_after(v, "xc" + tag)
                v.tensor_tensor(cb[:, o + 1, :], cb[:, o, :], cb[:, o, :], ALU.mult).then_inc(cls_step, 1)
                cls_after(v, "sq" + tag)
                v.tensor_reduce(cs[:, s + 1:s + 2], cb[:, o + 1, :], AX.X, ALU.add).then_inc(cls_step, 1)
                cls_after(v, "std" + tag)
                v.reciprocal(cs[:, s + 2:s + 3], cs[:, s + 2:s + 3]).then_inc(cls_step, 1)
                cls_after(v, "rstd" + tag)
                v.tensor_scalar(cb[:, o + 2, :], cb[:, o, :], cs[:, s + 2:s + 3], None, ALU.mult
                                ).then_inc(cls_step, 1)

            norm_cls(cl[:], 1, 0, "")
            cls_after(v, "turned")
            v.tensor_copy(ck2[0:C, 0, :], ps_turn[0:C, 0:P]).then_inc(cls_step, 1)
            cls_after(v, "qkv")
            qkv_c = cb[:, 4:7, :].rearrange("p n c -> p (n c)")
            v.tensor_tensor(qkv_c, ps_q[:, 0:3 * C], bqr[:], ALU.add).then_inc(cls_step, 1)
            cls_after(v, "qkvb")
            v.tensor_tensor(cb[:, 7, :], cb[:, 4, :], cb[:, 5, :], ALU.mult).then_inc(cls_step, 1)
            cls_after(v, "qk")
            v.tensor_reduce(cs[:, 3:4], cb[:, 7, :], AX.X, ALU.add).then_inc(cls_step, 1)
            cls_after(v, "dot")
            v.tensor_scalar(cb[:, 8, :], cb[:, 6, :], cs[:, 3:4], float(1 / np.sqrt(C)), ALU.mult, ALU.mult
                            ).then_inc(cls_step, 1)
            cls_after(v, "att")
            v.tensor_tensor(ch2[:], cb[:, 8, :], cl[:], ALU.add).then_inc(cls_step, 1)
            v.tensor_copy(ck2[:, 0, :].rearrange("p (a c) -> p a c", a=2),
                          cb[:, 5, :].unsqueeze(1).to_broadcast([P, 2, C])).then_inc(cls_step, 1)
            v.tensor_copy(ck2[:, 1, :].rearrange("p (a c) -> p a c", a=2),
                          cb[:, 6, :].unsqueeze(1).to_broadcast([P, 2, C])).then_inc(cls_step, 1)
            cls_after(v, "outer")
            for b in range(2):
                d = slice(b * C, (b + 1) * C)
                v.tensor_scalar(state0[d, d], ps_k[d, d], ALPHA / DECAY, None, ALU.mult
                                ).then_inc(cls_step, 1)
            norm_cls(ch2[:], 9, 4, "2")
            cls_after(v, "turned2")
            v.tensor_copy(ck2[0:C, 0, :], ps_turn[0:C, 0:P]).then_inc(cls_step, 1)
            cls_after(v, "logit")
            v.tensor_tensor(cb[:, 12, :], ps_q[:, 0:E], brr[:], ALU.add).then_inc(cls_step, 1)
            cls_after(v, "logitb")
            v.max(ctop[:], cb[:, 12, :]).then_inc(cls_step, 1)
            cls_after(v, "top")
            v.max_index(ctopi[:], ctop[:], cb[:, 12, :]).then_inc(cls_step, 1)
            cls_after(v, "topi")
            v.tensor_copy(cs[:, 8:10], ctopi[:, 0:2]).then_inc(cls_step, 1)
            cls_after(v, "topf")
            for k in range(K2):
                v.tensor_scalar(cb[:, 13 + k, :], kc[:, K_IOTA:K_IOTA + E], cs[:, 8 + k:9 + k], None,
                                ALU.is_equal).then_inc(cls_step, 1)
            cls_after(v, "hot1")
            v.tensor_tensor(chots[:], cb[:, 13, :], cb[:, 14, :], ALU.add).then_inc(cls_step, 1)
            for k in range(K2):
                v.tensor_tensor(crow[:, k, GAP:GAP + 1], ctop[:, 1 - k:2 - k], ctop[:, k:k + 1], ALU.subtract
                                ).then_inc(cls_step, 1)
            v.tensor_copy(crow[:, :, 0:C], cb[:, 11, :].unsqueeze(1).to_broadcast([P, K2, C])
                          ).then_inc(cls_step, 1)
            v.tensor_copy(crow[:, :, DEST:DEST + 1], kc[:, K_CDEST:K_CDEST + K2].unsqueeze(2)
                          ).then_inc(cls_step, 1)
            cls_after(v, "hots")
            v.tensor_scalar(small[:, 0, :], chots[:], float(P), None, ALU.mult).then_inc(cls_step, 1)
            cls_after(v, "ceil")
            v.tensor_copy(lim[:], small[:, 0, :]).then_inc(cls_step, 1)
            v.tensor_copy(cnt[:], chots[:]).then_inc(cls_step, 1)
            v.tensor_tensor_scan(end_all[:, 0, :], zero[:], small[:, 0, :], 0.0, ALU.add, ALU.add
                                 ).then_inc(cls_step, 1)
            cls_after(v, "incl")
            v.tensor_tensor(first_all[:, 0, :], end_all[:, 0, :], small[:, 0, :], ALU.subtract
                            ).then_inc(cls_step, 1)
            cls_after(v, "excl")
            v.tensor_copy(offa[:], first_all[:, 0, :]).then_inc(cls_step, 1)
            for k in range(K2):
                v.tensor_tensor(cb[:, 15 + k, :], cb[:, 13 + k, :], first_all[:, 0, :], ALU.mult
                                ).then_inc(cls_step, 1)
            cls_after(v, "pos1s")
            v.tensor_reduce(cs[:, 14:16], cb[:, 15:17, :], AX.X, ALU.add).then_inc(cls_step, 1)
            cls_after(v, "pos")
            v.tensor_scalar(cposi[:], cs[:, 14:16], kc[:, K_ROW1:K_ROW1 + 1], None, ALU.add
                            ).then_inc(cls_step, 1)
            cls_after(v, "posi")

            def slots_of(g):
                base = ALLOC * g

                def a(n):
                    v.wait_ge(s_alloc, base + n)
                new, rem, nlim, nb, offb, thr, bas, dif, gt = (small[:, n, :] for n in range(9))
                incl = end_all[:, bass.ds(g + 1, 1), :].rearrange("p o e -> p (o e)")
                excl = first_all[:, bass.ds(g + 1, 1), :].rearrange("p o e -> p (o e)")
                prev = end_all[:, bass.ds(g, 1), E - 1:E].rearrange("p o e -> p (o e)")
                v.wait_ge(s_rank, g + 1)
                if later(g):
                    v.wait_ge(s_pos, POS * g)
                    a(0)
                v.tensor_tensor(new, cnt[:], ps_o[:, 0:E], ALU.add).then_inc(s_alloc, 1)
                v.tensor_tensor(bas, cnt[:], offa[:], ALU.add).then_inc(s_alloc, 1)
                v.tensor_tensor(thr, lim[:], offa[:], ALU.add).then_inc(s_alloc, 1)
                a(2)
                v.tensor_tensor(rank[:], ps_p[:, :].rearrange("p (t e) -> p t e", e=E), all_tiles(bas),
                                ALU.add).then_inc(s_pos, 1)
                v.tensor_scalar(rem, new, 1.0 / P, 0.5 - 0.5 / P, ALU.mult, ALU.add).then_inc(s_alloc, 1)
                a(4)
                v.tensor_scalar(rem, rem, ROUND, None, ALU.add).then_inc(s_alloc, 1)
                a(5)
                v.tensor_scalar(nlim, rem, ROUND, float(P), ALU.subtract, ALU.mult).then_inc(s_alloc, 1)
                a(6)
                v.tensor_tensor(nb, nlim, lim[:], ALU.subtract).then_inc(s_alloc, 1)
                a(7)
                v.tensor_tensor_scan(incl, zero[:], nb, prev, ALU.add, ALU.add).then_inc(s_alloc, 1)
                v.tensor_scalar(gt, nb, 0.0, None, ALU.is_gt).then_inc(s_alloc, 1)
                a(8)
                v.tensor_tensor(excl, incl, nb, ALU.subtract).then_inc(s_alloc, 1)
                a(10)
                v.tensor_tensor(dif, excl, thr, ALU.subtract).then_inc(s_alloc, 1)
                a(11)
                v.tensor_tensor(rem, gt, dif, ALU.mult).then_inc(s_alloc, 1)
                a(12)
                v.tensor_tensor(offa[:], offa[:], rem, ALU.add).then_inc(s_alloc, 1)
                v.tensor_copy(cnt[:], new).then_inc(s_alloc, 1)
                v.tensor_copy(lim[:], nlim).then_inc(s_alloc, 1)

                def p(n):
                    v.wait_ge(s_pos, POS * g + n)
                p(1)
                v.tensor_tensor(past, rank[:], all_tiles(thr), ALU.is_ge).then_inc(s_pos, 1)
                p(2)
                v.tensor_tensor(past, past, all_tiles(dif), ALU.mult).then_inc(s_pos, 1)
                p(3)
                v.tensor_tensor(rank[:], rank[:], past, ALU.add).then_inc(s_pos, 1)
                p(4)
                v.tensor_tensor(pick[:], hot[:], rank[:].unsqueeze(1).to_broadcast([P, K2, TILES, E]),
                                ALU.mult).then_inc(s_pos, 1)
                p(5)
                v.tensor_reduce(posf[:], pick[:], AX.X, ALU.add).then_inc(s_pos, 1)
                p(6)
                if later(g):
                    for s in range(STEPS):
                        v.wait_ge(s_sent[s], 64 * g)
                v.tensor_copy(posi[:], posf[:].rearrange("p k t -> p (k t)")).then_inc(s_pos, 1)

            def q_scaled(g):
                v.wait_ge(s_qmm, g + 1)
                if later(g):
                    v.wait_ge(s_omm, g)
                v.scalar_tensor_tensor(qT[:].rearrange("p (s i) -> p s i", s=STEPS),
                                       ps_q[:, :].rearrange("p (s i) -> p s i", s=STEPS), bq[:, 0:1],
                                       kc[:, K_QDEC:K_QDEC + P].unsqueeze(1).to_broadcast([P, STEPS, P]),
                                       ALU.add, ALU.mult).then_inc(s_q, 1)

            def norm(g, src, xc_, sq_, out_, sums, s_ln, s_sq):
                def n(k):
                    v.wait_ge(s_ln, LN * g + k)
                v.tensor_reduce(sums[:, 0, :], src, AX.X, ALU.add).then_inc(s_ln, 1)
                n(1)
                v.scalar_tensor_tensor(xc_[:], wide(sums[:, 0, :]), -1.0 / C, src, ALU.mult, ALU.add
                                       ).then_inc(s_ln, 1)
                v.wait_ge(s_sq, 2 * g + 1)
                v.tensor_reduce(sums[:, 1, :], sq_[:], AX.X, ALU.add).then_inc(s_ln, 1)
                v.wait_ge(s_sq, 2 * g + 2)
                v.reciprocal(sums[:, 2, :], sums[:, 2, :]).then_inc(s_ln, 1)
                n(4)

            def norm2(g):
                src = h2[:, bass.ds(g * TILES, TILES), :]
                v.wait_ge(s_h2, g + 1)
                if later(g):
                    v.wait_ge(s_hn2r, g)
                norm(g, src, xc2, sq2, hn2, ssum2, s_ln2, s_sq2)
                if later(g):
                    v.wait_ge(s_turn2, g)
                v.tensor_tensor(hn2[:], xc2[:], wide(ssum2[:, 2, :]), ALU.mult).then_inc(s_ln2, 1)

            def masked(g):
                if later(g):
                    v.wait_ge(s_omm, g)
                for b, bank in ((0, ps_q), (1, ps_k)):
                    v.wait_ge(s_score, 2 * g + b + 1)
                    v.tensor_tensor(am[:, b, :].rearrange("p (s i) -> p s i", s=STEPS),
                                    bank[:, :].rearrange("p (s i) -> p s i", s=STEPS),
                                    kc[:, K_MASK:K_MASK + P].unsqueeze(1).to_broadcast([P, STEPS, P]),
                                    ALU.mult).then_inc(s_am, 1)

            def states(g):
                if later(g):
                    v.wait_ge(s_omm, g)
                    v.wait_ge(s_state, 2 * STEPS * g)
                col = (lambda o: kc[:, o + g:o + g + 1]) if isinstance(g, int) else \
                    (lambda o: kc[:, bass.ds(g + o, 1)])
                v.tensor_scalar(st_in[:], state0[:], col(K_FIRST), None, ALU.mult).then_inc(s_stin, 1)
                v.wait_ge(s_stin, 2 * g + 1)
                v.scalar_tensor_tensor(state[:, 0, :], state[:, STEPS, :], col(K_KEEP), st_in[:], ALU.mult,
                                       ALU.add).then_inc(s_stin, 1)
                v.wait_ge(s_stin, 2 * g + 2)
                v.wait_ge(s_pmm, g + 1)
                for s in range(STEPS):
                    if s:
                        v.wait_ge(s_state, 2 * STEPS * g + 2 * s)
                    for b in range(2):
                        d = slice(b * C, (b + 1) * C)
                        v.scalar_tensor_tensor(state[d, s + 1, d], state[d, s, d], DECAY,
                                               ps_p[d, s * P + b * C:s * P + (b + 1) * C], ALU.mult, ALU.add
                                               ).then_inc(s_state, 1)

            def choose(g):
                v.wait_ge(s_lmm, g + 1)
                if later(g):
                    v.wait_ge(s_topi, TILES * g)
                v.tensor_tensor(logit[:], ps_q[:, :].rearrange("p (t e) -> p t e", e=E), all_tiles(brr[:]),
                                ALU.add).then_inc(s_logit, 1)
                if later(g):
                    v.wait_ge(s_rows, 2 * STEPS * g)
                dest = kc[:, K_DEST:K_DEST + K2 * NT].rearrange("p (k t) -> p k t", k=K2)
                v.wait_ge(s_logit, g + 1)
                v.tensor_copy(tail[:, :, :, 2], dest[:, :, bass.ds(g * TILES, TILES)]).then_inc(s_tail, 1)
                for t in range(TILES):
                    v.max(top[:, t, :], logit[:, t, :]).then_inc(s_top, 1)
                v.wait_ge(s_top, TILES * (g + 1))
                for k in range(K2):
                    v.tensor_tensor(tail[:, k, :, 1:2], top[:, :, 1 - k:2 - k], top[:, :, k:k + 1], ALU.subtract
                                    ).then_inc(s_tail, 1)
                for t in range(TILES):
                    v.max_index(topi[:, t, :], top[:, t, :], logit[:, t, :]).then_inc(s_topi, 1)
                v.wait_ge(s_topi, TILES * (g + 1))
                v.tensor_copy(topf[:], topi[:, :, 0:K2].rearrange("p t k -> p k t")).then_inc(s_hot, 1)
                v.wait_ge(s_hot, 3 * g + 1)
                if later(g):
                    v.wait_ge(s_pos, POS * g)
                    v.wait_ge(s_rank, g)
                v.tensor_tensor(hot[:], kc[:, K_IOTA:K_IOTA + E].unsqueeze(1).unsqueeze(1).to_broadcast([P, K2, TILES, E]),
                                topf[:].unsqueeze(3).to_broadcast([P, K2, TILES, E]), ALU.is_equal
                                ).then_inc(s_hot, 1)
                v.wait_ge(s_hot, 3 * g + 2)
                v.tensor_tensor(hots[:], hot[:, 0], hot[:, 1], ALU.add).then_inc(s_hot, 1)

            def residual(g):
                v.wait_ge(s_omm, g + 1)
                v.tensor_tensor(h2[:, bass.ds(g * TILES, TILES), :], ps_o[:, :].rearrange("p (t c) -> p t c", c=C),
                                h[:], ALU.add).then_inc(s_h2, 1)

            def norm1(g):
                v.wait_ge(s_h, g + 1)
                if later(g):
                    v.wait_ge(s_ln1, LN * g)
                norm(g, h[:], xc, sq, hn, ssum, s_ln1, s_sq1)
                if later(g):
                    v.wait_ge(s_turn1, g)
                v.tensor_tensor(hn[:], xc[:], wide(ssum[:, 2, :]), ALU.mult).then_inc(s_ln1, 1)

            v.wait_ge(zeroed, 12)
            pipeline(v, (3, slots_of), (1, q_scaled), (2, norm2), (1, masked), (1, states), (2, choose),
                     (1, residual), (0, norm1))

            v.wait_ge(s_alloc, ALLOC * GROUPS)
            flat = blk_in.rearrange("p g e -> p (g e)")
            iota_g = kc[:, K_IOTA:K_IOTA + E].unsqueeze(1).to_broadcast([P, GROUPS + 1, E])
            for k in range(UB):
                if k:
                    v.wait_ge(s_blk, 3 * k)
                v.scalar_tensor_tensor(blk_in, first_all[:], kc[:, K_BLK + k:K_BLK + k + 1], iota_g,
                                       ALU.is_le, ALU.mult).then_inc(s_blk, 1)
                v.wait_ge(s_blk, 3 * k + 1)
                v.scalar_tensor_tensor(blk_in, end_all[:], kc[:, K_BLK + k:K_BLK + k + 1], blk_in,
                                       ALU.is_gt, ALU.mult).then_inc(s_blk, 1)
                v.wait_ge(s_blk, 3 * k + 2)
                v.tensor_reduce(blk_f[:, k:k + 1], flat, AX.X, ALU.add).then_inc(s_blk, 1)
            v.wait_ge(s_blk, 3 * UB)
            v.tensor_copy(blk_i[:], blk_f[:]).then_inc(s_blk, 1)
            v.wait_ge(blk_in_row, 16)
            v.wait_ge(weights_in, 16)

            regs = [v.alloc_register(f"expert{k}") for k in range(UB)]

            def stage_unit(n, r):
                u = unit(n, r)
                v.load(regs, blk_row[0:1, bass.ds(u * UB, UB)])
                if older(n, r):
                    v.wait_ge(u_ymm, u - 1)
                for k in range(UB):
                    e = v.snap(regs[k], min_val=0, max_val=E - 1)
                    v.tensor_copy(stage[r % 2][:, k, :], wall[:, bass.ds(e * WCOLS, WCOLS)]).then_inc(u_stage, 1)

            def dest_unit(n, r, old):
                v.wait_ge(u_in[r], 16 * (n + 1))
                if old:
                    v.wait_ge(u_sent[r], UB * 16 * n)
                v.tensor_copy(ydst[r][:].unsqueeze(2), xin[r][:, :, DEST:DEST + 1]).then_inc(u_dst, 1)
                d = xin[r][:, :, GAP]
                v.tensor_scalar(gate[0][r][:, 0, :], d, 0.0, -1.0, ALU.max, ALU.mult).then_inc(u_gap, 1)
                v.scalar_tensor_tensor(gate[0][r][:, 1, :], d, -1.0, d, ALU.mult, ALU.min).then_inc(u_gap, 1)

            def gated_unit(n, r):
                u = unit(n, r)
                v.wait_ge(u_exp, u + 1)
                g1, g2 = gate[1][r], gate[2][r]
                v.tensor_scalar(g2[:, 1, :], g1[:, 1, :], 1.0, None, ALU.add).then_inc(u_gate, 1)
                v.wait_ge(u_gate, 3 * u + 1)
                v.reciprocal(g2[:, 0, :], g2[:, 1, :]).then_inc(u_gate, 1)
                v.wait_ge(u_gate, 3 * u + 2)
                v.tensor_tensor(g1[:, 1, :], g2[:, 0, :], g1[:, 0, :], ALU.mult).then_inc(u_gate, 1)
                v.wait_ge(u_gate, 3 * u + 3)
                v.wait_ge(u_ymm, u + 1)
                v.tensor_tensor(ysb[r], (ps_v, ps_p)[r % 2][:, 0:UB * C].rearrange("p (k c) -> p k c", k=UB),
                                wide(g1[:, 1, :], UB), ALU.mult).then_inc(u_y, 1)

            def lap(n):
                for r in range(RING):
                    stage_unit(n, r)
                    dest_unit(n, r, later(n))
                    if r:
                        gated_unit(n, r - 1)
                    elif later(n):
                        gated_unit(n - 1, RING - 1)

            lap(0)
            with v.Fori(1, LAPS) as n:
                lap(n)
            gated_unit(LAPS - 1, RING - 1)

            v.wait_ge(cls_y, 16)
            v.tensor_tensor(osb[:], ch2[0:1, :], ycls[:, 0, :], ALU.add).then_inc(cls_y, 1)
            v.wait_ge(cls_y, 17)
            v.tensor_tensor(osb[:], osb[:], ycls[:, 1, :], ALU.add).then_inc(cls_y, 1)
            for n in range(NT // FT):
                v.wait_ge(y_in[n % 4], 16 * (n // 4 + 1))
                part = h2[:, n * FT:(n + 1) * FT, :]
                v.tensor_tensor(part, part, yin[n % 4][:, 0], ALU.add).then_inc(y_sum, 1)
                v.wait_ge(y_sum, 2 * n + 1)
                v.tensor_tensor(part, part, yin[n % 4][:, 1], ALU.add).then_inc(y_sum, 1)

        @block.scalar
        def _(act):
            act.wait_ge(consts_in, 12 * 16)
            act.activation(bn_s[:, 4:5], bn_s[:, 3:4], ACT.Sqrt, bias=kc[:, K_EPS:K_EPS + 1]).then_inc(bn_std, 1)
            act.wait_ge(zeroed, 1)
            act.wait_ge(setup_v, 4)
            banks = [ps_conv, ps_tok]
            for i in range(PAIRS * 8):
                q, n = divmod(i, 8)
                act.wait_ge(turned_x, i + 1)
                inner = img[:, q, 1:1 + IMG, 1:1 + IMG].rearrange("p y (x j) -> p y x j", j=32)
                for j in range(4):
                    a = act.activation(inner[:, :, :, 4 * n + j],
                                       banks[i % 2][:, j * P:(j + 1) * P].rearrange("p (y x) -> p y x", x=2),
                                       ACT.Identity, bias=bn_s[:, 7:8], scale=bn_s[:, 5:6])
                a.then_inc(img_ok, 1)
            for s, tag in ((0, ""), (4, "2")):
                cls_after(act, "ss" + tag)
                act.activation(cs[:, s + 2:s + 3], cs[:, s + 1:s + 2], ACT.Sqrt, scale=1.0 / C,
                               bias=kc[:, K_EPS:K_EPS + 1]).then_inc(cls_step, 1)
            cls_after(act, "posi")

            def hn_back(g):
                act.wait_ge(s_turn1, g + 1)
                if later(g):
                    act.wait_ge(s_vmm, g)
                act.copy(hnT[:], ps_turn[:, :]).then_inc(s_hnT, 1)

            def kv_bias(g):
                for n, bank, dst, mm, done in ((1, ps_k, kT, s_kmm, s_k), (2, ps_v, vT, s_vmm, s_v)):
                    act.wait_ge(mm, g + 1)
                    if later(g):
                        if n == 1:
                            act.wait_ge(s_score, 2 * g)
                        else:
                            act.wait_ge(s_vturn, g)
                    act.activation(dst[:], bank[:, :], ACT.Identity, bias=bq[:, n:n + 1]).then_inc(done, 1)

            def square2(g):
                act.wait_ge(s_ln2, LN * g + 2)
                act.activation(sq2[:], xc2[:], ACT.Square).then_inc(s_sq2, 1)
                act.wait_ge(s_ln2, LN * g + 3)
                act.activation(ssum2[:, 2, :], ssum2[:, 1, :], ACT.Sqrt, scale=1.0 / C,
                               bias=kc[:, K_EPS:K_EPS + 1]).then_inc(s_sq2, 1)

            def kv_tokens(g):
                if later(g):
                    act.wait_ge(s_omm, g)
                act.wait_ge(s_kturn, g + 1)
                act.copy(ktok[:], ps_tok[:, :]).then_inc(s_ktok, 1)
                act.wait_ge(s_vturn, g + 1)
                act.activation(vtok[:], ps_v[:, :], ACT.Identity, scale=kc[:, K_VDEC:K_VDEC + 1]
                               ).then_inc(s_vtok, 1)

            def hn2_back(g):
                act.wait_ge(s_turn2, g + 1)
                if later(g):
                    act.wait_ge(s_lmm, g)
                act.copy(hn2T[:], ps_turn[:, :]).then_inc(s_hn2T, 1)

            def hn2_keep(g):
                act.wait_ge(s_ln2, LN * (g + 1))
                if later(g):
                    act.wait_ge(s_rows, 2 * STEPS * g)
                act.copy(hn2r[:], hn2[:]).then_inc(s_hn2r, 1)

            def fill_rows(g):
                act.wait_ge(s_tail, TAIL * (g + 1))
                act.wait_ge(s_hn2r, g + 1)
                for s in range(STEPS):
                    if later(g):
                        act.wait_ge(s_sent[s], 64 * g)
                    t = slice(2 * s, 2 * s + 2)
                    act.copy(rows[:, :, t, 0:C], hn2r[:, t, :].unsqueeze(1).to_broadcast([P, K2, 2, C])
                             ).then_inc(s_rows, 1)
                    act.copy(rows[:, :, t, C:ROW], tail[:, :, t, :]).then_inc(s_rows, 1)

            def h_bias(g):
                act.wait_ge(s_conv, g + 1)
                if later(g):
                    act.wait_ge(s_htok, g)
                act.activation(hT[:], ps_conv[:, :], ACT.Identity, bias=lb[:, 1:2]).then_inc(s_hT, 1)
                act.wait_ge(s_htok, g + 1)
                if later(g):
                    act.wait_ge(s_h2, g)
                    act.wait_ge(s_ln1, LN * g)
                act.copy(h[:].rearrange("p t c -> p (t c)"), ps_tok[:, :]).then_inc(s_h, 1)

            def square1(g):
                act.wait_ge(s_ln1, LN * g + 2)
                act.activation(sq[:], xc[:], ACT.Square).then_inc(s_sq1, 1)
                act.wait_ge(s_ln1, LN * g + 3)
                act.activation(ssum[:, 2, :], ssum[:, 1, :], ACT.Sqrt, scale=1.0 / C,
                               bias=kc[:, K_EPS:K_EPS + 1]).then_inc(s_sq1, 1)

            act.wait_ge(bias_ok, 1)
            pipeline(act, (1, hn_back), (1, kv_bias), (3, fill_rows), (2, square2), (1, kv_tokens),
                     (2, hn2_back), (2, hn2_keep), (0, h_bias), (0, square1))

            def unit_back(n, r):
                u = unit(n, r)
                act.wait_ge(u_turn, u + 1)
                if older(n, r):
                    act.wait_ge(u_hmm, u - 1)
                act.wait_ge(u_gap, 2 * (u + 1))
                act.activation(gate[1][r], gate[0][r], ACT.Exp).then_inc(u_exp, 1)
                act.copy(xT[r % 2][0:ONE + 1, :], (ps_conv, ps_tok)[r % 2][0:ONE + 1, :]).then_inc(u_xT, 1)
                act.wait_ge(u_hmm, u + 1)
                if older(n, r):
                    act.wait_ge(u_ymm, u - 1)
                act.activation(hid[r % 2], (ps_q, ps_k)[r % 2][:, :], ACT.Relu).then_inc(u_hid, 1)

            for r in range(RING):
                unit_back(0, r)
            with act.Fori(1, LAPS) as n:
                for r in range(RING):
                    unit_back(n, r)

            act.wait_ge(cls_y, 18)
            for b in range(B):
                act.dma_start(out[b, 0:1, :], osb[:]).then_inc(out_done, 16)
            CH = FT // 2
            for n in range(NT // FT):
                act.wait_ge(y_sum, 2 * (n + 1))
                q, c0 = divmod(n * CH, NPIX // P)
                for b in range(2):
                    dst = out[2 * q + b, 1 + c0 * P:1 + (c0 + CH) * P, :].rearrange("(t p) c -> p t c", p=P)
                    src = h2[:, n * FT:(n + 1) * FT, :].rearrange("p (t b) c -> p t b c", b=2)[:, :, b, :]
                    act.dma_start(dst, src).then_inc(out_done, 16)


def kernel(**inputs):
    import concourse.bacc as bacc
    from concourse.bass_utils import run_bass_kernel_spmd

    a = {n: np.asarray(v) for n, v in inputs.items()}

    def twice(v):
        return np.ascontiguousarray(np.concatenate([v, v], 0))

    def rows(v):
        return np.ascontiguousarray(np.broadcast_to(v.reshape(1, -1), (P, v.size)))

    def blocks(m):
        d = np.zeros((P, P), m.dtype)
        d[:C, :C] = m
        d[C:, C:] = m
        return d

    wqkv = a["L0_attn_Wqkv"]
    pack = np.zeros((P, E, WCOLS), np.float32)
    pack[:C, :, :HID] = a["L0_ffn_W1"].transpose(1, 0, 2)
    pack[ONE, :, :HID] = a["L0_ffn_b1"]
    pack[96, :, :C] = a["L0_ffn_b2"]
    pack[:, :, HID:] = a["L0_ffn_W2"].transpose(1, 0, 2)
    arrays = {
        "x": a["x"].reshape(B, NPIX, C),
        "cls_rows": rows(a["cls_tok"]),
        "consts": constants(),
        "bn": twice(np.stack([a["L0_tok_bn_gamma"], a["L0_tok_bn_beta"], a["L0_tok_bn_mean"], a["L0_tok_bn_var"]], 1)),
        "conv_w": twice(a["L0_tok_conv_w"].reshape(C, TAPS)),
        "conv_b": twice(a["L0_tok_conv_b"].reshape(C, 1)),
        "lin_w": blocks(a["L0_tok_lin_w"].T),
        "lin_b": twice(a["L0_tok_lin_b"].reshape(C, 1)),
        "wqkv": np.stack([blocks(wqkv[:, n * C:(n + 1) * C]) for n in range(3)], 1),
        "bqkv_col": twice(a["L0_attn_bqkv"].reshape(3, C).T),
        "bqkv_row": rows(a["L0_attn_bqkv"]),
        "wr": blocks(a["L0_ffn_Wr"]),
        "br_row": rows(a["L0_ffn_br"]),
        "experts": pack.reshape(P, E * WCOLS),
    }
    nc = bacc.Bacc("TRN2", target_bir_lowering=False, num_devices=1)
    args = []
    for name, v in arrays.items():
        arrays[name] = v = np.ascontiguousarray(v)
        args.append(nc.dram_tensor(name, v.shape, mybir.dt.from_np(v.dtype), kind="ExternalInput").ap())
    args.append(nc.dram_tensor("out", (B, NPIX + 1, C), F32, kind="ExternalOutput").ap())
    tower(nc, *args)
    r = run_bass_kernel_spmd(nc, [arrays], core_ids=[0])
    return r.results[0]["out"]
```

```python
from contextlib import ExitStack

import numpy as np

import concourse.bass as bass
from concourse import mybir

ALU = mybir.AluOpType
ACT = mybir.ActivationFunctionType
AX = mybir.AxisListType
F32 = mybir.dt.float32
BF16 = mybir.dt.bfloat16
U32 = mybir.dt.uint32
I32 = mybir.dt.int32

P = 128
B, IMG, C = 4, 64, 64
NPIX = IMG * IMG
PAD = IMG + 2
PAIRS = B // 2
STEPS = 4
TILES = 2 * STEPS
W = STEPS * P
GROUPS = PAIRS * NPIX // W
GPP = GROUPS // PAIRS
ROWS_G = W // IMG
NT = GROUPS * TILES
E, HID = 64, 128
K2 = 2
TAPS = 9
ALPHA = float(np.float32(0.99))
DECAY = ALPHA ** P
EPS = 1e-5
ROW = C + 4
ONE, GAP, DEST = C, C + 1, C + 2
PICKS = K2 * (B * NPIX + 1)
MAX_LAG = 3
SPARE_BLOCKS = MAX_LAG * W * 2 // P + 1
REGION = 119
FULL = (REGION - SPARE_BLOCKS) * P
SPARES = K2 * ((GROUPS - MAX_LAG) * W * 2 + 1) // (FULL + 1)
assert (GROUPS - MAX_LAG) * W * 2 + 1 <= REGION * P - P
EXT = E + SPARES
NBLK = (PICKS + EXT * (P - 1)) // P
NBLK = -(-NBLK // 4) * 4
YROWS = K2 * P * NT + K2
ROUND = float(2 ** 23)
EMPTY = E * REGION + SPARES * SPARE_BLOCKS
SLOTS = (EMPTY + 1) * P
FAR = 4.0e6
assert max(SLOTS, YROWS) < FAR
WCOLS = HID + C
UB = 4
UNITS = NBLK // UB
RING = 4
LAPS = UNITS // RING

K_ID, K_MASK, K_TRI = 0, P, 2 * P
K_FIRST, K_KEEP = 3 * P, 3 * P + GROUPS
K_IOTA = K_KEEP + GROUPS
K_DEST = K_IOTA + E
K_VDEC = K_DEST + K2 * NT
K_QDEC = K_VDEC + 1
K_ROW1 = K_QDEC + 1
K_CDEST = K_ROW1 + 1
K_BLK = K_CDEST + K2
K_BASE = K_BLK + UB
K_SEL = K_BASE + EXT
K_EPS = K_SEL + P
K_COLS = K_EPS + 1


def constants():
    k = np.zeros((P, K_COLS), np.float64)
    i = np.arange(P)
    k[:, K_ID:K_ID + P] = np.eye(P)
    k[:, K_MASK:K_MASK + P] = (i[:, None] <= i[None, :]) / DECAY
    k[:, K_TRI:K_TRI + P] = i[:, None] < i[None, :]
    k[:, K_FIRST:K_FIRST + GROUPS] = np.arange(GROUPS) % GPP == 0
    k[:, K_KEEP:K_KEEP + GROUPS] = np.arange(GROUPS) % GPP != 0
    k[:, K_IOTA:K_IOTA + E] = np.arange(E)
    k[:, K_DEST:K_DEST + K2 * NT] = (np.arange(K2)[:, None] * P * NT + np.arange(NT)).reshape(1, -1) + i[:, None] * NT
    k[:, K_VDEC] = ALPHA ** -i.astype(np.float64)
    k[:, K_QDEC] = ALPHA ** i.astype(np.float64) * DECAY / np.sqrt(C)
    k[:, K_ROW1] = FAR * (i > 0)
    k[:, K_CDEST:K_CDEST + K2] = K2 * P * NT + np.arange(K2)
    k[:, K_BLK:K_BLK + UB] = UB * i[:, None] + np.arange(UB)
    k[:, K_BASE:K_BASE + EXT] = np.append(np.arange(E) * REGION, E * REGION + np.arange(SPARES) * SPARE_BLOCKS) * P
    k[96, K_SEL:K_SEL + P] = 1
    k[:, K_EPS] = EPS
    return k.astype(np.float32)


CLS = ("mean xc sq ss std rstd hn turned hnT qkv qkvb qk dot att h2 kk vv outer state0 state1 "
       "mean2 xc2 sq2 ss2 std2 rstd2 hn2 turned2 hn2T logit logitb top topi topf hot0 hot1 hots "
       "gap0 gap1 rows dests count pos0s pos1s pos posi").split()


def tower(nc, x, cls_rows, consts, bn, conv_w, conv_b, lin_w, lin_b, wqkv, bqkv_col, bqkv_row,
          wr, br_row, experts, out):
    with ExitStack() as ctx:
        def sb(name, shape, dt=F32):
            return ctx.enter_context(nc.sbuf_tensor(name, shape, dt))

        def psum(name):
            return ctx.enter_context(nc.psum_tensor(name, [P, 512], F32))

        def sem(name):
            return ctx.enter_context(nc.semaphore(name))

        slots = nc.dram_tensor("slot_rows", [SLOTS, ROW], F32, kind="Internal").ap()
        ybuf = nc.dram_tensor("gated_results", [YROWS, C], F32, kind="Internal").ap()

        blk_dram = nc.dram_tensor("block_table", [2, P, UB], I32, kind="Internal").ap()

        ps_conv = psum("ps_conv")
        ps_tok = psum("ps_tok")
        ps_turn = psum("ps_turn")
        ps_q = psum("ps_q")
        ps_k = psum("ps_k")
        ps_v = psum("ps_v")
        ps_p = psum("ps_p")
        ps_o = psum("ps_o")

        kc = sb("kc", [P, K_COLS])
        wall = sb("wall", [P, E * WCOLS])
        xs = wall[:, 0:PAIRS * 32 * P].rearrange("p (q j c) -> p q j c", q=PAIRS, j=32)
        img = sb("img", [P, PAIRS, PAD, PAD])
        h2 = sb("h2", [P, NT, C])
        bn_s = sb("bn_s", [P, 8])
        cw = sb("cw", [P, TAPS + 1])
        linT = sb("linT", [P, P])
        lb = sb("lb", [P, 2])
        wtap = sb("wtap", [P, TAPS, P])
        wq = sb("wq", [P, 3, P])
        bq = sb("bq", [P, 3])
        bqr = sb("bqr", [P, 3 * C])
        wrs = sb("wrs", [P, P])
        brr = sb("brr", [P, E])
        tri = sb("tri", [P, P], BF16)
        ones = sb("ones", [P, P], BF16)
        empty = sb("empty", [P, ROW])
        hT = sb("hT", [P, W])
        xc = sb("xc", [P, TILES, C])
        sq = sb("sq", [P, TILES, C])
        hn = sb("hn", [P, TILES, C])
        xc2 = sb("xc2", [P, TILES, C])
        sq2 = sb("sq2", [P, TILES, C])
        hn2 = sb("hn2", [P, TILES, C])
        hn2r = sb("hn2r", [P, TILES, C])
        ssum = sb("ssum", [P, 3, TILES])
        ssum2 = sb("ssum2", [P, 3, TILES])
        hnT = sb("hnT", [P, W])
        hn2T = sb("hn2T", [P, W])
        qT = sb("qT", [P, W])
        kT = sb("kT", [P, W])
        vT = sb("vT", [P, W])
        ktok = sb("ktok", [P, W])
        vtok = sb("vtok", [P, W])
        am = sb("am", [P, 2, W])
        state = sb("state", [P, STEPS + 1, P])
        state0 = sb("state0", [P, P])
        st_in = sb("st_in", [P, P])
        logit = sb("logit", [P, TILES, E])
        top = sb("top", [P, TILES, 8])
        topi = sb("topi", [P, TILES, 8], U32)
        topf = sb("topf", [P, K2, TILES])
        hot = sb("hot", [P, K2, TILES, E], BF16)
        hots = sb("hots", [P, TILES, E], BF16)
        tail = sb("tail", [P, K2, TILES, 4])
        rank = sb("rank", [P, TILES, E])
        pick = sb("pick", [P, K2, TILES, E])
        posf = sb("posf", [P, K2, TILES])
        posi = sb("posi", [P, K2 * TILES], U32)
        posi_last = sb("posi_last", [P, K2 * TILES], U32)
        rows = sb("rows", [P, K2, TILES, ROW])
        cnt = sb("cnt", [P, E])
        zero = sb("zero", [P, E])
        cl = sb("cl", [P, C])
        ch2 = sb("ch2", [P, C])
        cb = sb("cb", [P, 17, C])
        crow = sb("crow", [P, K2, ROW])
        ctop = sb("ctop", [P, 8])
        ctopi = sb("ctopi", [P, 8], U32)
        cs = sb("cs", [P, 16])
        cposi = sb("cposi", [P, K2], U32)
        chots = sb("chots", [P, E])
        ck2 = sb("ck2", [P, 2, P])
        blk_f = sb("blk_f", [P, 2, UB])
        blk_i = sb("blk_i", [P, 2, UB], I32)
        blk_row = sb("blk_row", [1, 2, P * UB], I32)
        pad_row = sb("pad_row", [1, EXT], I32)
        ext = sb("ext", [P, 7, EXT])
        blk_at = sb("blk_at", [P, 5, UB, EXT])
        move = sb("move", [P, 6, E])
        spare_at = sb("spare_at", [P, 3, SPARES, E])
        spare = img[:, :, :, :].rearrange("p a b c -> p (a b c)")
        at = [0]

        def reuse(n):
            at[0] += n
            return spare[:, at[0] - n:at[0]]
        xin = [reuse(UB * ROW).rearrange("p (k c) -> p k c", k=UB) for _ in range(RING)]
        ysb = [reuse(UB * C).rearrange("p (k c) -> p k c", k=UB) for _ in range(RING)]
        xT = [reuse(W) for _ in range(2)]
        hid = [reuse(W) for _ in range(2)]
        stage = [reuse(UB * WCOLS).rearrange("p (k c) -> p k c", k=UB) for _ in range(RING)]
        gate = [[reuse(2 * UB).rearrange("p (a k) -> p a k", a=2) for _ in range(RING)] for _ in range(3)]
        ydst = [sb(f"ydst{r}", [P, UB], U32) for r in range(RING)]
        FT = 16
        yin = [wall[:, i * K2 * FT * C:(i + 1) * K2 * FT * C].rearrange("p (k t c) -> p k t c", k=K2, t=FT)
               for i in range(4)]
        ycls = sb("ycls", [1, K2, C])
        osb = sb("osb", [1, C])

        ident = kc[:, K_ID:K_ID + P]

        def wide(ap, n=TILES):
            return ap.unsqueeze(2).to_broadcast([P, n, C])

        def all_tiles(ap):
            return ap.unsqueeze(1).to_broadcast([P, TILES, E])

        consts_in = sem("consts_in")
        x_in = [[sem(f"x_in{q}{half}") for half in range(2)] for q in range(PAIRS)]
        setup_v = sem("setup_v")
        bn_std = sem("bn_std")
        zeroed = sem("zeroed")
        bias_mm = sem("bias_mm")
        bias_ok = sem("bias_ok")
        turned_x = sem("turned_x")
        img_ok = sem("img_ok")
        filled = sem("filled")
        weights_in = sem("weights_in")
        cls_step = sem("cls_step")
        cls_sent = sem("cls_sent")
        s_conv = sem("s_conv")
        s_hT = sem("s_hT")
        s_htok = sem("s_htok")
        s_h = sem("s_h")
        s_ln1 = sem("s_ln1")
        s_sq1 = sem("s_sq1")
        s_turn1 = sem("s_turn1")
        s_hnT = sem("s_hnT")
        s_qmm = sem("s_qmm")
        s_kmm = sem("s_kmm")
        s_vmm = sem("s_vmm")
        s_q = sem("s_q")
        s_k = sem("s_k")
        s_v = sem("s_v")
        s_kturn = sem("s_kturn")
        s_vturn = sem("s_vturn")
        s_ktok = sem("s_ktok")
        s_vtok = sem("s_vtok")
        s_score = sem("s_score")
        s_am = sem("s_am")
        s_pmm = sem("s_pmm")
        s_stin = sem("s_stin")
        s_state = sem("s_state")
        s_omm = sem("s_omm")
        s_h2 = sem("s_h2")
        s_ln2 = sem("s_ln2")
        s_sq2 = sem("s_sq2")
        s_turn2 = sem("s_turn2")
        s_hn2T = sem("s_hn2T")
        s_hn2r = sem("s_hn2r")
        s_lmm = sem("s_lmm")
        s_logit = sem("s_logit")
        s_top = sem("s_top")
        s_topi = sem("s_topi")
        s_hot = sem("s_hot")
        s_tail = sem("s_tail")
        s_rank = sem("s_rank")
        s_count = sem("s_count")
        s_move = sem("s_move")
        s_pos = sem("s_pos")
        s_rows = sem("s_rows")
        s_sent = [sem(f"s_sent{s}") for s in range(STEPS)]
        s_blk = sem("s_blk")
        blk_out = sem("blk_out")
        blk_in_row = sem("blk_in_row")
        u_in = [sem(f"u_in{r}") for r in range(RING)]
        u_stage = sem("u_stage")
        u_turn = sem("u_turn")
        u_xT = sem("u_xT")
        u_hmm = sem("u_hmm")
        u_hid = sem("u_hid")
        u_ymm = sem("u_ymm")
        u_y = sem("u_y")
        u_dst = sem("u_dst")
        u_gap = sem("u_gap")
        u_exp = sem("u_exp")
        u_gate = sem("u_gate")
        u_sent = [sem(f"u_sent{r}") for r in range(RING)]
        y_in = [sem(f"y_in{r}") for r in range(4)]
        y_sum = sem("y_sum")
        cls_y = sem("cls_y")
        out_done = sem("out_done")

        POS, LN, TAIL = 4, 5, 3
        BLK, PADS = 20 + 4 + 3 + SPARES, 11 + SPARES
        SETUP_V = 5 + TAPS

        def later(g):
            return not (isinstance(g, int) and g == 0)

        def pipeline(eng, *stages, before_last=None):
            depth = max(lag for lag, _ in stages)
            for i in range(MAX_LAG + 1):
                for lag, f in stages:
                    if i >= lag:
                        f(i - lag)
            with eng.Fori(MAX_LAG + 1, GROUPS) as i:
                for lag, f in stages:
                    f(i - lag)
            if before_last:
                before_last()
            for i in range(GROUPS, GROUPS + MAX_LAG):
                for lag, f in stages:
                    if i - lag < GROUPS:
                        f(i - lag)

        def unit(n, r):
            return n * RING + r

        def older(n, r, by=2):
            return not isinstance(n, int) or unit(n, r) >= by

        def units(eng, *stages):
            def step(n, r):
                for lag, f in stages:
                    if r >= lag:
                        f(n, r - lag)
                    elif later(n):
                        f(n - 1, r - lag + RING)
            for r in range(RING):
                step(0, r)
            with eng.Fori(1, LAPS) as n:
                for r in range(RING):
                    step(n, r)
            for u in range(LAPS * RING, UNITS + max(lag for lag, _ in stages)):
                for lag, f in stages:
                    if u - lag < UNITS:
                        f(*divmod(u - lag, RING))

        def cls_after(eng, *names):
            eng.wait_ge(cls_step, max(CLS.index(n) for n in names) + 1)

        PADS_SP = 40

        def pad_extents(eng, lo, hi):
            at_once = 8
            regs = [eng.alloc_register(f"pad{k}") for k in range(at_once)]

            def pad(at, n):
                eng.load(regs[0:n], pad_row[0:1, bass.ds(at, n)])
                for k in range(n):
                    first = eng.snap(regs[k], min_val=0, max_val=SLOTS - P)
                    eng.dma_start(slots[bass.ds(first, P)], empty[:]).then_inc(filled, 16)
            with eng.Fori(0, (hi - lo) // at_once) as n:
                pad(n * at_once + lo, at_once)
            if (hi - lo) % at_once:
                pad(hi - (hi - lo) % at_once, (hi - lo) % at_once)

        block = ctx.enter_context(nc.Block())

        @block.sync
        def _(sp):
            loads = [(kc[:], consts), (cl[:], cls_rows), (bn_s[:, 0:4], bn), (cw[:, 0:TAPS], conv_w),
                     (cw[:, TAPS:TAPS + 1], conv_b), (linT[:], lin_w), (lb[:, 0:1], lin_b),
                     (wq[:], wqkv), (bq[:], bqkv_col), (bqr[:], bqkv_row), (wrs[:], wr), (brr[:], br_row)]
            for dst, src in loads:
                sp.dma_start(dst, src).then_inc(consts_in, 16)
            for q in range(PAIRS):
                for half in range(2):
                    j = slice(16 * half, 16 * half + 16)
                    for b in range(2):
                        sp.dma_start(xs[:, q, j, b * C:(b + 1) * C],
                                     x[2 * q + b].rearrange("(p j) c -> p j c", p=P)[:, j, :]
                                     ).then_inc(x_in[q][half], 16)
            sp.wait_ge(zeroed, 5)
            sp.dma_start(slots[EMPTY * P:SLOTS], empty[:]).then_inc(filled, 16)
            sp.wait_ge(turned_x, PAIRS * 8)
            sp.dma_start(wall[:], experts).then_inc(weights_in, 16)

            sp.wait_ge(s_blk, PADS)
            pad_extents(sp, 0, PADS_SP)
            sp.wait_ge(filled, 16 * (EXT + 1))
            sp.wait_ge(cls_sent, 32)
            for s in range(STEPS):
                sp.wait_ge(s_sent[s], GROUPS * 64)
            sp.wait_ge(blk_in_row, 16)
            by_block = slots.rearrange("(n p) c -> n p c", p=P)
            sp.wait_ge(weights_in, 16)
            blk_regs = [sp.alloc_register(f"block{k}") for k in range(UB)]

            def load_unit(n, r, old):
                u = unit(n, r)
                sp.load(blk_regs, blk_row[0:1, 1, bass.ds(u * UB, UB)])
                at = [sp.snap(blk_regs[k], min_val=0, max_val=EMPTY) for k in range(UB)]
                if old:
                    before = sp.snap(u - RING + 1)
                    sp.wait_ge(u_turn, before)
                    sp.wait_ge(u_dst, before)
                    sp.wait_ge(u_exp, before)
                for k in range(UB):
                    sp.dma_start(xin[r][:, k, :], by_block[bass.ds(at[k], 1)].rearrange("o p c -> p (o c)")
                                 ).then_inc(u_in[r], 16)
            for r in range(RING):
                load_unit(0, r, False)
            with sp.Fori(1, LAPS) as n:
                for r in range(RING):
                    load_unit(n, r, True)
            for r in range(UNITS % RING):
                load_unit(LAPS, r, True)
            for r in range(RING):
                sp.wait_ge(u_sent[r], (UNITS + RING - 1 - r) // RING * UB * 16)
            by_tile = ybuf[0:K2 * P * NT].rearrange("(k p t) c -> p k t c", k=K2, p=P)
            sp.dma_start(ycls[:], ybuf[K2 * P * NT:YROWS].unsqueeze(0)).then_inc(cls_y, 16)
            for n in range(NT // FT):
                if n >= 4:
                    sp.wait_ge(y_sum, 2 * (n - 3))
                sp.dma_start(yin[n % 4], by_tile[:, :, n * FT:(n + 1) * FT, :]).then_inc(y_in[n % 4], 16)
            sp.wait_ge(out_done, 16 * (B * NT // FT // 2 + B))

        @block.gpsimd
        def _(pool):
            cls_after(pool, "posi")
            for k in range(K2):
                nc.gpsimd.indirect_dma_start(slots, bass.IndirectOffsetOnAxis(cposi[0:2, k:k + 1], 0),
                                             crow[0:2, k, :], None, bounds_check=SLOTS - 1,
                                             oob_is_err=False).then_inc(cls_sent, 16)

            last_y = pool.alloc_register("last_y")
            pool.reg_mov(last_y, YROWS - 1)
            rows_wanted = pool.alloc_register("rows_wanted")
            pool.reg_mov(rows_wanted, 2)
            y_wanted = pool.alloc_register("y_wanted")
            pool.reg_mov(y_wanted, 1)

            def scatter(g, posi):
                for s in range(STEPS):
                    fixed = isinstance(g, int)
                    wanted = 2 * (STEPS * g + s + 1) if fixed else pool.snap(rows_wanted)
                    if s == 0:
                        pool.wait_ge(s_pos, POS * (g + 1))
                    pool.wait_ge(s_rows, wanted)
                    if not fixed:
                        pool.reg_add(rows_wanted, rows_wanted, 2)
                    for k in range(K2):
                        for b in range(2):
                            t = 2 * s + b
                            nc.gpsimd.indirect_dma_start(
                                slots, bass.IndirectOffsetOnAxis(posi[:, k * TILES + t:k * TILES + t + 1], 0),
                                rows[:, k, t, :], None).then_inc(s_sent[s], 16)

            with pool.Fori(0, GROUPS - 1) as g:
                scatter(g, posi)
            scatter(GROUPS - 1, posi_last)

            def send_unit(n, r):
                fixed = isinstance(n, int)
                wanted = n * RING + r + 1 if fixed else pool.snap(y_wanted)
                pool.wait_ge(u_dst, n * RING + r + 1)
                pool.wait_ge(u_y, wanted)
                if not fixed:
                    pool.reg_add(y_wanted, y_wanted, 1)
                for k in range(UB):
                    nc.gpsimd.indirect_dma_start(
                        ybuf, bass.IndirectOffsetOnAxis(ydst[r][:, k:k + 1], 0), ysb[r][:, k, :], None,
                        bounds_check=last_y, oob_is_err=False).then_inc(u_sent[r], 16)
            with pool.Fori(0, LAPS) as n:
                for r in range(RING):
                    send_unit(n, r)
            for r in range(UNITS % RING):
                send_unit(LAPS, r)

        @block.tensor
        def _(pe):
            pe.wait_ge(consts_in, 12 * 16)
            pe.matmul(ps_o[:, 0:1], linT[:], cw[:, TAPS:TAPS + 1], start=True, stop=True).then_inc(bias_mm, 1)
            def turn_images(q, banks):
                for n in range(8):
                    i = 8 * q + n
                    if n % 4 == 0:
                        pe.wait_ge(x_in[q][n // 4], 32)
                    if i >= 2:
                        pe.wait_ge(img_ok, i - 1)
                    bank = banks[i % 2]
                    for j in range(4):
                        m = pe.transpose(bank[:, j * P:(j + 1) * P], xs[:, q, 4 * n + j, :], ident)
                    m.then_inc(turned_x, 1)

            def rest_of_images(g):
                if isinstance(g, int) and g == 0:
                    turn_images(1, [ps_p, ps_o])

            cls_after(pe, "hn")
            pe.transpose(ps_turn[0:C, 0:P], cb[:, 3, :], ident).then_inc(cls_step, 1)
            cls_after(pe, "hnT")
            pe.matmul(ps_q[:, 0:3 * C], ck2[0:C, 0, :], wq[0:C, :, 0:C], start=True, stop=True
                      ).then_inc(cls_step, 1)
            cls_after(pe, "kk", "vv")
            pe.matmul(ps_k[:, 0:P], ck2[0:1, 0, :], ck2[0:1, 1, :], start=True, stop=True
                      ).then_inc(cls_step, 1)
            cls_after(pe, "hn2")
            pe.transpose(ps_turn[0:C, 0:P], cb[:, 11, :], ident).then_inc(cls_step, 1)
            cls_after(pe, "hn2T")
            pe.matmul(ps_q[:, 0:E], ck2[0:C, 0, :], wrs[0:C, 0:E], start=True, stop=True
                      ).then_inc(cls_step, 1)
            turn_images(0, [ps_conv, ps_tok])

            def taps(g):
                if later(g):
                    pe.wait_ge(s_hT, g)
                pair, y0 = (g // GPP, g % GPP * ROWS_G)
                for tap in range(TAPS):
                    dy, dx = divmod(tap, 3)
                    if isinstance(g, int):
                        view = img[:, pair, y0 + dy:y0 + dy + ROWS_G, dx:dx + IMG]
                    else:
                        row = pair * PAD + y0 + dy
                        view = img[:, :, :, :].rearrange("p a b c -> p (a b) c")[:, bass.ds(row, ROWS_G), dx:dx + IMG]
                    m = pe.matmul(ps_conv[:, :], wtap[:, tap, :], view, start=tap == 0, stop=tap == TAPS - 1,
                                  skip_group_check=True)
                m.then_inc(s_conv, 1)

            def turn_hn(g):
                pe.wait_ge(s_ln1, LN * (g + 1))
                if isinstance(g, int):
                    if g >= 2:
                        pe.wait_ge(s_hn2T, g - 1)
                else:
                    pe.wait_ge(s_hn2T, g - 1)
                for s in range(STEPS):
                    m = pe.transpose(ps_turn[:, s * P:(s + 1) * P],
                                     hn[:, 2 * s:2 * s + 2, :].rearrange("p t c -> p (t c)"), ident)
                m.then_inc(s_turn1, 1)

            def ranks(g):
                pe.wait_ge(s_hot, 3 * (g + 1))
                pe.wait_ge(s_state, 2 * STEPS * min_groups(g, 2))
                flat = hots[:].rearrange("p t e -> p (t e)")
                pe.matmul(ps_p[:, :], tri[:], flat, start=True, stop=False, skip_group_check=True)
                for k in range(1, TILES):
                    m = pe.matmul(ps_p[:, k * E:], ones[:], flat[:, 0:(TILES - k) * E], start=False,
                                  stop=k == TILES - 1, skip_group_check=True)
                pe.wait_ge(s_h2, min_groups(g, 2))
                for t in range(TILES):
                    m = pe.matmul(ps_o[:, 0:E], ones[:], hots[:, t, :], start=t == 0, stop=t == TILES - 1,
                                  skip_group_check=True)
                m.then_inc(s_rank, 1)

            def qkv(g):
                pe.wait_ge(s_hnT, g + 1)
                if not isinstance(g, int) or g >= 2:
                    pe.wait_ge(s_logit, g - 1)
                if later(g):
                    pe.wait_ge(s_am, 2 * g)
                    pe.wait_ge(s_vtok, g)
                for n, bank, done in ((1, ps_k, s_kmm), (2, ps_v, s_vmm), (0, ps_q, s_qmm)):
                    pe.matmul(bank[:, :], wq[:, n, :], hnT[:], start=True, stop=True).then_inc(done, 1)

            def turn_kv(g):
                pe.wait_ge(s_k, g + 1)
                pe.wait_ge(s_h, min_groups(g, 2))
                for s in range(STEPS):
                    m = pe.transpose(ps_tok[:, s * P:(s + 1) * P], kT[:, s * P:(s + 1) * P], ident)
                m.then_inc(s_kturn, 1)
                pe.wait_ge(s_v, g + 1)
                for s in range(STEPS):
                    m = pe.transpose(ps_v[:, s * P:(s + 1) * P], vT[:, s * P:(s + 1) * P], ident)
                m.then_inc(s_vturn, 1)

            def scores(g):
                pe.wait_ge(s_q, g + 1)
                for b, bank in ((0, ps_q), (1, ps_k)):
                    for s in range(STEPS):
                        m = pe.matmul(bank[:, s * P:(s + 1) * P], kT[b * C:(b + 1) * C, s * P:(s + 1) * P],
                                      qT[b * C:(b + 1) * C, s * P:(s + 1) * P], start=True, stop=True)
                    m.then_inc(s_score, 1)

            def products(g):
                pe.wait_ge(s_ktok, g + 1)
                pe.wait_ge(s_vtok, g + 1)
                if not isinstance(g, int) or g >= 2:
                    pe.wait_ge(s_pos, POS * (g - 2) + 1)
                for s in range(STEPS):
                    m = pe.matmul(ps_p[:, s * P:(s + 1) * P], ktok[:, s * P:(s + 1) * P],
                                  vtok[:, s * P:(s + 1) * P], start=True, stop=True)
                m.then_inc(s_pmm, 1)

            def attend(g):
                pe.wait_ge(s_am, 2 * (g + 1))
                if not isinstance(g, int) or g >= 2:
                    pe.wait_ge(s_count, g - 1)
                for s in range(STEPS):
                    c0 = s * P
                    for b in range(2):
                        pe.matmul(ps_o[:, c0 + b * C:c0 + (b + 1) * C], am[:, b, c0:c0 + P],
                                  vtok[:, c0 + b * C:c0 + (b + 1) * C], start=s == 0 and b == 0, stop=False,
                                  skip_group_check=True)
                pe.wait_ge(s_stin, 2 * (g + 1))
                pe.wait_ge(s_state, 2 * STEPS * g + 2 * (STEPS - 1))
                for s in range(STEPS):
                    c0 = s * P
                    m = pe.matmul(ps_o[:, c0:c0 + P], qT[:, c0:c0 + P], state[:, s, :], start=False,
                                  stop=s == STEPS - 1, skip_group_check=True)
                m.then_inc(s_omm, 1)

            def turn_hn2(g):
                pe.wait_ge(s_ln2, LN * (g + 1))
                pe.wait_ge(s_hnT, min_groups(g, 2))
                for s in range(STEPS):
                    m = pe.transpose(ps_turn[:, s * P:(s + 1) * P],
                                     hn2[:, 2 * s:2 * s + 2, :].rearrange("p t c -> p (t c)"), ident)
                m.then_inc(s_turn2, 1)

            def router(g):
                pe.wait_ge(s_hn2T, g + 1)
                pe.wait_ge(s_am, 2 * min_groups(g, 2))
                for s in range(STEPS):
                    m = pe.matmul(ps_q[:, s * P:(s + 1) * P], hn2T[:, s * P:(s + 1) * P], wrs[:],
                                  start=True, stop=True)
                m.then_inc(s_lmm, 1)

            def turn_h(g):
                pe.wait_ge(s_hT, g + 1)
                if not isinstance(g, int) or g >= 2:
                    pe.wait_ge(s_ktok, g - 1)
                for s in range(STEPS):
                    m = pe.transpose(ps_tok[:, s * P:(s + 1) * P], hT[:, s * P:(s + 1) * P], ident)
                m.then_inc(s_htok, 1)

            def min_groups(g, ahead):
                if isinstance(g, int):
                    return min(g + ahead, GROUPS)
                return g + ahead

            pe.wait_ge(bias_ok, 1)
            pe.wait_ge(img_ok, 8)
            cls_after(pe, "logitb", "state1")
            pe.wait_ge(setup_v, SETUP_V)
            pipeline(pe,
                     (0, taps), (3, ranks), (0, turn_h), (0, rest_of_images), (1, qkv), (1, turn_kv),
                     (1, scores), (2, turn_hn2), (1, products), (2, router), (1, attend), (0, turn_hn))

            def unit_turn(n, r):
                u = unit(n, r)
                pe.wait_ge(u_in[r], UB * 16 * (n + 1))
                if older(n, r):
                    pe.wait_ge(u_xT, u - 1)
                bank = (ps_conv, ps_tok)[r % 2]
                for k in range(UB):
                    m = pe.transpose(bank[0:ONE + 1, k * P:(k + 1) * P], xin[r][:, k, 0:ONE + 1], ident)
                m.then_inc(u_turn, 1)

            def unit_hidden(n, r):
                u = unit(n, r)
                pe.wait_ge(u_xT, u + 1)
                pe.wait_ge(u_stage, UB * (u + 1))
                if older(n, r):
                    pe.wait_ge(u_hid, u - 1)
                bank = (ps_q, ps_k)[r % 2]
                for k in range(UB):
                    m = pe.matmul(bank[:, k * P:(k + 1) * P], stage[r][0:ONE + 1, k, 0:HID],
                                  xT[r % 2][0:ONE + 1, k * P:(k + 1) * P], start=True, stop=True)
                m.then_inc(u_hmm, 1)

            def unit_out(n, r):
                u = unit(n, r)
                pe.wait_ge(u_hid, u + 1)
                if older(n, r):
                    pe.wait_ge(u_y, u - 1)
                bank = (ps_v, ps_p)[r % 2]
                pe.matmul(bank[:, 0:UB * C].rearrange("p (k c) -> p k c", k=UB), kc[:, K_SEL:K_SEL + P],
                          stage[r][:, :, 0:C], start=True, stop=False, skip_group_check=True)
                for k in range(UB):
                    m = pe.matmul(bank[:, k * C:(k + 1) * C], hid[r % 2][:, k * P:(k + 1) * P],
                                  stage[r][:, k, HID:WCOLS], start=False, stop=k == UB - 1,
                                  skip_group_check=True)
                m.then_inc(u_ymm, 1)

            units(pe, (0, unit_turn), (1, unit_hidden), (2, unit_out))


        @block.vector
        def _(v):
            for edge in (img[:, :, 0:PAD:PAD - 1, :], img[:, :, 1:PAD - 1, 0:1],
                         img[:, :, 1:PAD - 1, PAD - 1:PAD]):
                v.memset(edge, 0.0).then_inc(zeroed, 1)
            v.memset(empty[:], 0.0).then_inc(zeroed, 1)
            v.wait_ge(zeroed, 4)
            v.memset(empty[:, DEST:DEST + 1], FAR).then_inc(zeroed, 1)
            v.memset(state[:], 0.0).then_inc(zeroed, 1)
            v.memset(state0[:], 0.0).then_inc(zeroed, 1)
            v.memset(ones[:], 1.0).then_inc(zeroed, 1)
            v.memset(zero[:], 0.0).then_inc(zeroed, 1)
            v.memset(tail[:], 0.0).then_inc(zeroed, 1)
            v.memset(crow[:], 0.0).then_inc(zeroed, 1)
            v.wait_ge(zeroed, 11)
            v.memset(tail[:, :, :, 0:1], 1.0).then_inc(zeroed, 1)
            v.memset(crow[:, :, ONE:ONE + 1], 1.0).then_inc(zeroed, 1)
            v.wait_ge(consts_in, 12 * 16)
            v.wait_ge(bn_std, 1)
            v.reciprocal(bn_s[:, 4:5], bn_s[:, 4:5]).then_inc(setup_v, 1)
            v.wait_ge(setup_v, 1)
            v.tensor_tensor(bn_s[:, 5:6], bn_s[:, 4:5], bn_s[:, 0:1], ALU.mult).then_inc(setup_v, 1)
            v.wait_ge(setup_v, 2)
            v.tensor_tensor(bn_s[:, 6:7], bn_s[:, 5:6], bn_s[:, 2:3], ALU.mult).then_inc(setup_v, 1)
            v.wait_ge(setup_v, 3)
            v.tensor_tensor(bn_s[:, 7:8], bn_s[:, 1:2], bn_s[:, 6:7], ALU.subtract).then_inc(setup_v, 1)
            v.tensor_copy(tri[:], kc[:, K_TRI:K_TRI + P]).then_inc(setup_v, 1)
            for tap in range(TAPS):
                v.tensor_scalar(wtap[:, tap, :], linT[:], cw[:, tap:tap + 1], None, ALU.mult).then_inc(setup_v, 1)
            v.wait_ge(bias_mm, 1)
            v.tensor_tensor(lb[:, 1:2], ps_o[:, 0:1], lb[:, 0:1], ALU.add).then_inc(bias_ok, 1)

            def done(ins, name):
                assert name in CLS
                ins.then_inc(cls_step, 1)

            def norm_cls(src, o, s, tag):
                v.tensor_reduce(cs[:, s:s + 1], src, AX.X, ALU.add).then_inc(cls_step, 1)
                cls_after(v, "mean" + tag)
                v.scalar_tensor_tensor(cb[:, o, :], cs[:, s:s + 1].to_broadcast([P, C]), -1.0 / C, src,
                                       ALU.mult, ALU.add).then_inc(cls_step, 1)
                cls_after(v, "xc" + tag)
                v.tensor_tensor(cb[:, o + 1, :], cb[:, o, :], cb[:, o, :], ALU.mult).then_inc(cls_step, 1)
                cls_after(v, "sq" + tag)
                v.tensor_reduce(cs[:, s + 1:s + 2], cb[:, o + 1, :], AX.X, ALU.add).then_inc(cls_step, 1)
                cls_after(v, "std" + tag)
                v.reciprocal(cs[:, s + 2:s + 3], cs[:, s + 2:s + 3]).then_inc(cls_step, 1)
                cls_after(v, "rstd" + tag)
                v.tensor_scalar(cb[:, o + 2, :], cb[:, o, :], cs[:, s + 2:s + 3], None, ALU.mult
                                ).then_inc(cls_step, 1)

            norm_cls(cl[:], 1, 0, "")
            cls_after(v, "turned")
            v.tensor_copy(ck2[0:C, 0, :], ps_turn[0:C, 0:P]).then_inc(cls_step, 1)
            cls_after(v, "qkv")
            qkv_c = cb[:, 4:7, :].rearrange("p n c -> p (n c)")
            v.tensor_tensor(qkv_c, ps_q[:, 0:3 * C], bqr[:], ALU.add).then_inc(cls_step, 1)
            cls_after(v, "qkvb")
            v.tensor_tensor(cb[:, 7, :], cb[:, 4, :], cb[:, 5, :], ALU.mult).then_inc(cls_step, 1)
            cls_after(v, "qk")
            v.tensor_reduce(cs[:, 3:4], cb[:, 7, :], AX.X, ALU.add).then_inc(cls_step, 1)
            cls_after(v, "dot")
            v.tensor_scalar(cb[:, 8, :], cb[:, 6, :], cs[:, 3:4], float(1 / np.sqrt(C)), ALU.mult, ALU.mult
                            ).then_inc(cls_step, 1)
            cls_after(v, "att")
            v.tensor_tensor(ch2[:], cb[:, 8, :], cl[:], ALU.add).then_inc(cls_step, 1)
            v.tensor_copy(ck2[:, 0, :].rearrange("p (a c) -> p a c", a=2),
                          cb[:, 5, :].unsqueeze(1).to_broadcast([P, 2, C])).then_inc(cls_step, 1)
            v.tensor_copy(ck2[:, 1, :].rearrange("p (a c) -> p a c", a=2),
                          cb[:, 6, :].unsqueeze(1).to_broadcast([P, 2, C])).then_inc(cls_step, 1)
            cls_after(v, "outer")
            for b in range(2):
                d = slice(b * C, (b + 1) * C)
                v.tensor_scalar(state0[d, d], ps_k[d, d], ALPHA / DECAY, None, ALU.mult
                                ).then_inc(cls_step, 1)
            norm_cls(ch2[:], 9, 4, "2")
            cls_after(v, "turned2")
            v.tensor_copy(ck2[0:C, 0, :], ps_turn[0:C, 0:P]).then_inc(cls_step, 1)
            cls_after(v, "logit")
            v.tensor_tensor(cb[:, 12, :], ps_q[:, 0:E], brr[:], ALU.add).then_inc(cls_step, 1)
            cls_after(v, "logitb")
            v.max(ctop[:], cb[:, 12, :]).then_inc(cls_step, 1)
            cls_after(v, "top")
            v.max_index(ctopi[:], ctop[:], cb[:, 12, :]).then_inc(cls_step, 1)
            cls_after(v, "topi")
            v.tensor_copy(cs[:, 8:10], ctopi[:, 0:2]).then_inc(cls_step, 1)
            cls_after(v, "topf")
            for k in range(K2):
                v.tensor_scalar(cb[:, 13 + k, :], kc[:, K_IOTA:K_IOTA + E], cs[:, 8 + k:9 + k], None,
                                ALU.is_equal).then_inc(cls_step, 1)
            cls_after(v, "hot1")
            v.tensor_tensor(chots[:], cb[:, 13, :], cb[:, 14, :], ALU.add).then_inc(cls_step, 1)
            for k in range(K2):
                v.tensor_tensor(crow[:, k, GAP:GAP + 1], ctop[:, 1 - k:2 - k], ctop[:, k:k + 1], ALU.subtract
                                ).then_inc(cls_step, 1)
            v.tensor_copy(crow[:, :, 0:C], cb[:, 11, :].unsqueeze(1).to_broadcast([P, K2, C])
                          ).then_inc(cls_step, 1)
            v.tensor_copy(crow[:, :, DEST:DEST + 1], kc[:, K_CDEST:K_CDEST + K2].unsqueeze(2)
                          ).then_inc(cls_step, 1)
            cls_after(v, "hots")
            base = kc[:, K_BASE:K_BASE + E]
            v.tensor_tensor(cnt[:], chots[:], base, ALU.add).then_inc(cls_step, 1)
            for k in range(K2):
                v.tensor_tensor(cb[:, 15 + k, :], cb[:, 13 + k, :], base, ALU.mult
                                ).then_inc(cls_step, 1)
            cls_after(v, "pos1s")
            v.tensor_reduce(cs[:, 14:16], cb[:, 15:17, :], AX.X, ALU.add).then_inc(cls_step, 1)
            cls_after(v, "pos")
            v.tensor_scalar(cposi[:], cs[:, 14:16], kc[:, K_ROW1:K_ROW1 + 1], None, ALU.add
                            ).then_inc(cls_step, 1)
            cls_after(v, "posi")

            def slots_of(g):
                def p(n):
                    v.wait_ge(s_pos, POS * g + n)
                v.wait_ge(s_rank, g + 1)
                if later(g):
                    p(0)
                    v.wait_ge(s_count, g)
                v.tensor_tensor(rank[:], ps_p[:, :].rearrange("p (t e) -> p t e", e=E), all_tiles(cnt[:]),
                                ALU.add).then_inc(s_pos, 1)
                p(1)
                v.tensor_tensor(pick[:], hot[:], rank[:].unsqueeze(1).to_broadcast([P, K2, TILES, E]),
                                ALU.mult).then_inc(s_pos, 1)
                v.tensor_tensor(cnt[:], cnt[:], ps_o[:, 0:E], ALU.add).then_inc(s_count, 1)
                p(2)
                v.tensor_reduce(posf[:], pick[:], AX.X, ALU.add).then_inc(s_pos, 1)
                p(3)
                last = isinstance(g, int) and g == GROUPS - 1
                if later(g) and not last:
                    for s in range(STEPS):
                        v.wait_ge(s_sent[s], 64 * g)
                v.tensor_copy((posi_last if last else posi)[:], posf[:].rearrange("p k t -> p (k t)")).then_inc(s_pos, 1)

            def center(g, xc_, sums, s_ln):
                src = h2[:, bass.ds(g * TILES, TILES), :]
                v.tensor_reduce(sums[:, 0, :], src, AX.X, ALU.add).then_inc(s_ln, 1)
                v.wait_ge(s_ln, LN * g + 1)
                v.scalar_tensor_tensor(xc_[:], wide(sums[:, 0, :]), -1.0 / C, src, ALU.mult, ALU.add
                                       ).then_inc(s_ln, 1)

            def variance(g, sq_, sums, s_ln, s_sq):
                v.wait_ge(s_sq, 2 * g + 1)
                v.tensor_reduce(sums[:, 1, :], sq_[:], AX.X, ALU.add).then_inc(s_ln, 1)

            def scaled(g, xc_, out_, sums, s_ln, s_sq, s_turn):
                v.wait_ge(s_sq, 2 * g + 2)
                v.reciprocal(sums[:, 2, :], sums[:, 2, :]).then_inc(s_ln, 1)
                v.wait_ge(s_ln, LN * g + 4)
                if later(g):
                    v.wait_ge(s_turn, g)
                v.tensor_tensor(out_[:], xc_[:], wide(sums[:, 2, :]), ALU.mult).then_inc(s_ln, 1)

            def center1(g):
                v.wait_ge(s_h, g + 1)
                if later(g):
                    v.wait_ge(s_ln1, LN * g)
                center(g, xc, ssum, s_ln1)

            def variance1(g):
                variance(g, sq, ssum, s_ln1, s_sq1)

            def scaled1(g):
                scaled(g, xc, hn, ssum, s_ln1, s_sq1, s_turn1)

            def center2(g):
                v.wait_ge(s_h2, g + 1)
                if later(g):
                    v.wait_ge(s_ln2, LN * g)
                center(g, xc2, ssum2, s_ln2)

            def variance2(g):
                variance(g, sq2, ssum2, s_ln2, s_sq2)

            def scaled2(g):
                if later(g):
                    v.wait_ge(s_hn2r, g)
                scaled(g, xc2, hn2, ssum2, s_ln2, s_sq2, s_turn2)

            def masked(g):
                if later(g):
                    v.wait_ge(s_omm, g)
                for b, bank in ((0, ps_q), (1, ps_k)):
                    v.wait_ge(s_score, 2 * g + b + 1)
                    v.tensor_tensor(am[:, b, :].rearrange("p (s i) -> p s i", s=STEPS),
                                    bank[:, :].rearrange("p (s i) -> p s i", s=STEPS),
                                    kc[:, K_MASK:K_MASK + P].unsqueeze(1).to_broadcast([P, STEPS, P]),
                                    ALU.mult).then_inc(s_am, 1)

            def states(g):
                if later(g):
                    v.wait_ge(s_omm, g)
                    v.wait_ge(s_state, 2 * STEPS * g)
                col = (lambda o: kc[:, o + g:o + g + 1]) if isinstance(g, int) else \
                    (lambda o: kc[:, bass.ds(g + o, 1)])
                v.tensor_scalar(st_in[:], state0[:], col(K_FIRST), None, ALU.mult).then_inc(s_stin, 1)
                v.wait_ge(s_stin, 2 * g + 1)
                v.scalar_tensor_tensor(state[:, 0, :], state[:, STEPS, :], col(K_KEEP), st_in[:], ALU.mult,
                                       ALU.add).then_inc(s_stin, 1)
                v.wait_ge(s_stin, 2 * g + 2)
                v.wait_ge(s_pmm, g + 1)
                for s in range(STEPS):
                    if s:
                        v.wait_ge(s_state, 2 * STEPS * g + 2 * s)
                    for b in range(2):
                        d = slice(b * C, (b + 1) * C)
                        v.scalar_tensor_tensor(state[d, s + 1, d], state[d, s, d], DECAY,
                                               ps_p[d, s * P + b * C:s * P + (b + 1) * C], ALU.mult, ALU.add
                                               ).then_inc(s_state, 1)

            def logits(g):
                v.wait_ge(s_lmm, g + 1)
                if later(g):
                    v.wait_ge(s_topi, TILES * g)
                v.tensor_tensor(logit[:], ps_q[:, :].rearrange("p (t e) -> p t e", e=E), all_tiles(brr[:]),
                                ALU.add).then_inc(s_logit, 1)

            def tops(g):
                if later(g):
                    v.wait_ge(s_rows, 2 * STEPS * g)
                v.wait_ge(s_logit, g + 1)
                dest = kc[:, K_DEST:K_DEST + K2 * NT].rearrange("p (k t) -> p k t", k=K2)
                v.tensor_copy(tail[:, :, :, 2:3], dest[:, :, bass.ds(g * TILES, TILES)].unsqueeze(3)
                              ).then_inc(s_tail, 1)
                for t in range(TILES):
                    v.max(top[:, t, :], logit[:, t, :]).then_inc(s_top, 1)
                v.wait_ge(s_top, TILES * (g + 1))
                for k in range(K2):
                    v.tensor_tensor(tail[:, k, :, 1:2], top[:, :, 1 - k:2 - k], top[:, :, k:k + 1], ALU.subtract
                                    ).then_inc(s_tail, 1)

            def one_hots(g):
                for t in range(TILES):
                    v.max_index(topi[:, t, :], top[:, t, :], logit[:, t, :]).then_inc(s_topi, 1)
                v.wait_ge(s_topi, TILES * (g + 1))
                v.tensor_copy(topf[:], topi[:, :, 0:K2].rearrange("p t k -> p k t")).then_inc(s_hot, 1)
                v.wait_ge(s_hot, 3 * g + 1)
                if later(g):
                    v.wait_ge(s_pos, POS * g)
                    v.wait_ge(s_rank, g)
                v.tensor_tensor(hot[:], kc[:, K_IOTA:K_IOTA + E].unsqueeze(1).unsqueeze(1).to_broadcast([P, K2, TILES, E]),
                                topf[:].unsqueeze(3).to_broadcast([P, K2, TILES, E]), ALU.is_equal
                                ).then_inc(s_hot, 1)
                v.wait_ge(s_hot, 3 * g + 2)
                v.tensor_tensor(hots[:], hot[:, 0], hot[:, 1], ALU.add).then_inc(s_hot, 1)

            def residual(g):
                v.wait_ge(s_omm, g + 1)
                part = h2[:, bass.ds(g * TILES, TILES), :]
                v.scalar_tensor_tensor(part, ps_o[:, :].rearrange("p (t c) -> p t c", c=C),
                                       kc[:, K_QDEC:K_QDEC + 1], part, ALU.mult, ALU.add).then_inc(s_h2, 1)

            moved, order, to, stayed, dist, gone = (move[:, k, :] for k in range(6))

            def move_on():
                def m(n):
                    v.wait_ge(s_move, n)
                v.wait_ge(s_count, GROUPS - MAX_LAG)
                v.scalar_tensor_tensor(moved, cnt[:], float(-FULL), base, ALU.add, ALU.is_gt).then_inc(s_move, 1)
                v.tensor_copy(stayed, cnt[:]).then_inc(s_move, 1)
                m(1)
                v.tensor_tensor_scan(order, zero[:], moved, 0.0, ALU.add, ALU.add).then_inc(s_move, 1)
                m(3)
                v.tensor_scalar(to, order, float(SPARE_BLOCKS * P), float((E * REGION - SPARE_BLOCKS) * P),
                                ALU.mult, ALU.add).then_inc(s_move, 1)
                m(4)
                v.tensor_tensor(dist, to, cnt[:], ALU.subtract).then_inc(s_move, 1)
                m(5)
                v.tensor_tensor(gone, dist, moved, ALU.mult).then_inc(s_move, 1)
                m(6)
                v.tensor_tensor(cnt[:], cnt[:], gone, ALU.add).then_inc(s_move, 1)
                m(7)

            v.wait_ge(zeroed, 13)
            pipeline(v, (2, center2), (3, tops), (2, variance2), (3, one_hots), (2, scaled2), (3, slots_of),
                     (0, center1), (1, masked), (0, variance1), (1, states), (0, scaled1), (2, logits),
                     (1, residual), before_last=move_on)

            def b(n):
                v.wait_ge(s_blk, n)
            v.wait_ge(s_count, GROUPS)
            count, blocks_, ends, starts, shift, rounded, owner = (ext[:, k, :] for k in range(7))
            mine_of, used_of, owner_of = (spare_at[:, k] for k in range(3))
            ext_base = kc[:, K_BASE:K_BASE + EXT]

            def over_spares(ap):
                return ap.unsqueeze(1).to_broadcast([P, SPARES, E])
            v.tensor_tensor(dist, stayed, cnt[:], ALU.subtract).then_inc(s_blk, 1)
            for k in range(SPARES):
                v.scalar_tensor_tensor(mine_of[:, k, :], order, float(k + 1), moved, ALU.is_equal, ALU.mult
                                       ).then_inc(s_blk, 1)
            v.tensor_tensor(gone, cnt[:], to, ALU.subtract).then_inc(s_blk, 1)
            b(1)
            v.tensor_tensor(dist, dist, moved, ALU.mult).then_inc(s_blk, 1)
            v.tensor_tensor(rounded[:, 0:E], cnt[:], base, ALU.subtract).then_inc(s_blk, 1)
            b(4)
            v.tensor_tensor(used_of, mine_of, over_spares(gone), ALU.mult).then_inc(s_blk, 1)
            v.tensor_tensor(owner_of, mine_of, over_spares(kc[:, K_IOTA:K_IOTA + E]), ALU.mult
                            ).then_inc(s_blk, 1)
            b(6)
            v.tensor_tensor(count[:, 0:E], rounded[:, 0:E], dist, ALU.add).then_inc(s_blk, 1)
            b(7)
            v.tensor_reduce(count[:, E:EXT], used_of, AX.X, ALU.add).then_inc(s_blk, 1)
            b(8)
            v.tensor_reduce(owner[:, E:EXT], owner_of, AX.X, ALU.add).then_inc(s_blk, 1)
            v.tensor_copy(owner[:, 0:E], kc[:, K_IOTA:K_IOTA + E]).then_inc(s_blk, 1)
            b(10)
            v.tensor_tensor(pad_row[:], count[0:1, :], ext_base[0:1, :], ALU.add).then_inc(s_blk, 1)
            v.tensor_scalar(rounded, count, 1.0 / P, 0.5 - 0.5 / P, ALU.mult, ALU.add).then_inc(s_blk, 1)
            b(14)
            v.tensor_scalar(rounded, rounded, ROUND, None, ALU.add).then_inc(s_blk, 1)
            b(15)
            v.tensor_scalar(blocks_, rounded, ROUND, None, ALU.subtract).then_inc(s_blk, 1)
            b(16)
            v.tensor_tensor_scan(ends, zero[:, 0:1].to_broadcast([P, EXT]), blocks_, 0.0, ALU.add, ALU.add
                                 ).then_inc(s_blk, 1)
            b(17)
            v.tensor_tensor(starts, ends, blocks_, ALU.subtract).then_inc(s_blk, 1)
            b(18)
            v.scalar_tensor_tensor(shift, ext_base, 1.0 / P, starts, ALU.mult, ALU.subtract).then_inc(s_blk, 1)

            def by_block(ap):
                return ap.unsqueeze(1).to_broadcast([P, UB, EXT])
            this = kc[:, K_BLK:K_BLK + UB].unsqueeze(2).to_broadcast([P, UB, EXT])
            begun, mine, at_e, at_b, row_b = (blk_at[:, k] for k in range(5))
            v.tensor_tensor(begun, by_block(starts), this, ALU.is_le).then_inc(s_blk, 1)
            v.tensor_tensor(mine, by_block(ends), this, ALU.is_gt).then_inc(s_blk, 1)
            b(21)
            v.tensor_tensor(mine, mine, begun, ALU.mult).then_inc(s_blk, 1)
            v.tensor_tensor(row_b, by_block(shift), this, ALU.add).then_inc(s_blk, 1)
            b(23)
            v.tensor_tensor(at_e, mine, by_block(owner), ALU.mult).then_inc(s_blk, 1)
            v.scalar_tensor_tensor(at_b, row_b, float(-EMPTY), mine, ALU.add, ALU.mult).then_inc(s_blk, 1)
            b(24)
            v.tensor_reduce(blk_f[:, 0, :], at_e, AX.X, ALU.add).then_inc(s_blk, 1)
            b(25)
            v.tensor_reduce(blk_f[:, 1, :], at_b, AX.X, ALU.add).then_inc(s_blk, 1)
            b(26)
            v.tensor_copy(blk_i[:, 0, :], blk_f[:, 0, :]).then_inc(s_blk, 1)
            b(27)
            v.tensor_scalar(blk_i[:, 1, :], blk_f[:, 1, :], float(EMPTY), None, ALU.add).then_inc(s_blk, 1)
            v.wait_ge(blk_in_row, 16)
            v.wait_ge(weights_in, 16)

            regs = [v.alloc_register(f"expert{k}") for k in range(UB)]

            def stage_unit(n, r):
                u = unit(n, r)
                v.load(regs, blk_row[0:1, 0, bass.ds(u * UB, UB)])
                if older(n, r, RING):
                    v.wait_ge(u_ymm, u - RING + 1)
                for k in range(UB):
                    e = v.snap(regs[k], min_val=0, max_val=E - 1)
                    v.tensor_copy(stage[r][:, k, :], wall[:, bass.ds(e * WCOLS, WCOLS)]).then_inc(u_stage, 1)

            def dest_unit(n, r):
                v.wait_ge(u_in[r], UB * 16 * (n + 1))
                if later(n):
                    v.wait_ge(u_sent[r], UB * 16 * n)
                v.tensor_copy(ydst[r][:].unsqueeze(2), xin[r][:, :, DEST:DEST + 1]).then_inc(u_dst, 1)
                d = xin[r][:, :, GAP]
                v.tensor_scalar(gate[0][r][:, 0, :], d, 0.0, -1.0, ALU.max, ALU.mult).then_inc(u_gap, 1)
                v.scalar_tensor_tensor(gate[0][r][:, 1, :], d, -1.0, d, ALU.mult, ALU.min).then_inc(u_gap, 1)

            def gated_unit(n, r):
                u = unit(n, r)
                v.wait_ge(u_exp, u + 1)
                g1, g2 = gate[1][r], gate[2][r]
                v.tensor_scalar(g2[:, 1, :], g1[:, 1, :], 1.0, None, ALU.add).then_inc(u_gate, 1)
                v.wait_ge(u_gate, 3 * u + 1)
                v.reciprocal(g2[:, 0, :], g2[:, 1, :]).then_inc(u_gate, 1)
                v.wait_ge(u_gate, 3 * u + 2)
                v.tensor_tensor(g1[:, 1, :], g2[:, 0, :], g1[:, 0, :], ALU.mult).then_inc(u_gate, 1)
                v.wait_ge(u_gate, 3 * u + 3)
                v.wait_ge(u_ymm, u + 1)
                v.tensor_tensor(ysb[r], (ps_v, ps_p)[r % 2][:, 0:UB * C].rearrange("p (k c) -> p k c", k=UB),
                                wide(g1[:, 1, :], UB), ALU.mult).then_inc(u_y, 1)

            units(v, (0, stage_unit), (0, dest_unit), (2, gated_unit))

            v.wait_ge(cls_y, 16)
            v.tensor_tensor(osb[:], ch2[0:1, :], ycls[:, 0, :], ALU.add).then_inc(cls_y, 1)
            v.wait_ge(cls_y, 17)
            v.tensor_tensor(osb[:], osb[:], ycls[:, 1, :], ALU.add).then_inc(cls_y, 1)
            for n in range(NT // FT):
                v.wait_ge(y_in[n % 4], 16 * (n // 4 + 1))
                part = h2[:, n * FT:(n + 1) * FT, :]
                v.tensor_tensor(part, part, yin[n % 4][:, 0], ALU.add).then_inc(y_sum, 1)
                v.wait_ge(y_sum, 2 * n + 1)
                v.tensor_tensor(part, part, yin[n % 4][:, 1], ALU.add).then_inc(y_sum, 1)

        @block.scalar
        def _(act):
            act.wait_ge(consts_in, 12 * 16)
            act.activation(bn_s[:, 4:5], bn_s[:, 3:4], ACT.Sqrt, bias=kc[:, K_EPS:K_EPS + 1]).then_inc(bn_std, 1)
            for s, tag in ((0, ""), (4, "2")):
                cls_after(act, "ss" + tag)
                act.activation(cs[:, s + 2:s + 3], cs[:, s + 1:s + 2], ACT.Sqrt, scale=1.0 / C,
                               bias=kc[:, K_EPS:K_EPS + 1]).then_inc(cls_step, 1)
            act.wait_ge(zeroed, 4)
            act.wait_ge(setup_v, 4)

            def images_back(q, banks):
                for i in range(8 * q, 8 * q + 8):
                    act.wait_ge(turned_x, i + 1)
                    n = i % 8
                    inner = img[:, q, 1:1 + IMG, 1:1 + IMG].rearrange("p y (x j) -> p y x j", j=32)
                    act.activation(inner[:, :, :, 4 * n:4 * n + 4],
                                   banks[i % 2][:, :].rearrange("p (j y x) -> p y x j", j=4, x=2),
                                   ACT.Identity, bias=bn_s[:, 7:8], scale=bn_s[:, 5:6]).then_inc(img_ok, 1)
            images_back(0, [ps_conv, ps_tok])

            def rest_of_images(g):
                if isinstance(g, int) and g == 0:
                    images_back(1, [ps_p, ps_o])


            def hn_back(g):
                act.wait_ge(s_turn1, g + 1)
                if later(g):
                    act.wait_ge(s_vmm, g)
                act.copy(hnT[:], ps_turn[:, :]).then_inc(s_hnT, 1)

            def qkv_bias(g):
                for n, bank, dst, mm, done in ((1, ps_k, kT, s_kmm, s_k), (2, ps_v, vT, s_vmm, s_v),
                                               (0, ps_q, qT, s_qmm, s_q)):
                    act.wait_ge(mm, g + 1)
                    if later(g):
                        if n == 0:
                            act.wait_ge(s_omm, g)
                        elif n == 1:
                            act.wait_ge(s_score, 2 * g)
                        else:
                            act.wait_ge(s_vturn, g)
                    act.activation(dst[:], bank[:, :], ACT.Identity, bias=bq[:, n:n + 1]).then_inc(done, 1)

            def square2(g):
                act.wait_ge(s_ln2, LN * g + 2)
                act.activation(sq2[:], xc2[:], ACT.Square).then_inc(s_sq2, 1)
                act.wait_ge(s_ln2, LN * g + 3)
                act.activation(ssum2[:, 2, :], ssum2[:, 1, :], ACT.Sqrt, scale=1.0 / C,
                               bias=kc[:, K_EPS:K_EPS + 1]).then_inc(s_sq2, 1)

            def kv_tokens(g):
                if later(g):
                    act.wait_ge(s_omm, g)
                act.wait_ge(s_kturn, g + 1)
                act.copy(ktok[:], ps_tok[:, :]).then_inc(s_ktok, 1)
                act.wait_ge(s_vturn, g + 1)
                act.activation(vtok[:], ps_v[:, :], ACT.Identity, scale=kc[:, K_VDEC:K_VDEC + 1]
                               ).then_inc(s_vtok, 1)

            def hn2_back(g):
                act.wait_ge(s_turn2, g + 1)
                if later(g):
                    act.wait_ge(s_lmm, g)
                act.copy(hn2T[:], ps_turn[:, :]).then_inc(s_hn2T, 1)

            def hn2_keep(g):
                act.wait_ge(s_ln2, LN * (g + 1))
                if later(g):
                    act.wait_ge(s_rows, 2 * STEPS * g)
                act.copy(hn2r[:], hn2[:]).then_inc(s_hn2r, 1)

            def fill_rows(g):
                act.wait_ge(s_tail, TAIL * (g + 1))
                act.wait_ge(s_hn2r, g + 1)
                for s in range(STEPS):
                    if later(g):
                        act.wait_ge(s_sent[s], 64 * g)
                    t = slice(2 * s, 2 * s + 2)
                    act.copy(rows[:, :, t, 0:C], hn2r[:, t, :].unsqueeze(1).to_broadcast([P, K2, 2, C])
                             ).then_inc(s_rows, 1)
                    act.copy(rows[:, :, t, C:ROW], tail[:, :, t, :]).then_inc(s_rows, 1)

            def h_bias(g):
                act.wait_ge(s_conv, g + 1)
                if later(g):
                    act.wait_ge(s_htok, g)
                act.activation(hT[:], ps_conv[:, :], ACT.Identity, bias=lb[:, 1:2]).then_inc(s_hT, 1)

            def h_back(g):
                act.wait_ge(s_htok, g + 1)
                act.copy(h2[:, bass.ds(g * TILES, TILES), :].rearrange("p t c -> p (t c)"), ps_tok[:, :]
                         ).then_inc(s_h, 1)

            def square1(g):
                act.wait_ge(s_ln1, LN * g + 2)
                act.activation(sq[:], xc[:], ACT.Square).then_inc(s_sq1, 1)
                act.wait_ge(s_ln1, LN * g + 3)
                act.activation(ssum[:, 2, :], ssum[:, 1, :], ACT.Sqrt, scale=1.0 / C,
                               bias=kc[:, K_EPS:K_EPS + 1]).then_inc(s_sq1, 1)

            act.wait_ge(bias_ok, 1)
            pipeline(act, (2, square2), (3, fill_rows), (0, h_bias), (0, h_back), (0, rest_of_images),
                     (1, qkv_bias), (1, kv_tokens), (2, hn2_back), (0, square1), (2, hn2_keep), (0, hn_back))

            def turned_unit(n, r):
                u = unit(n, r)
                act.wait_ge(u_gap, 2 * (u + 1))
                act.activation(gate[1][r], gate[0][r], ACT.Exp).then_inc(u_exp, 1)
                act.wait_ge(u_turn, u + 1)
                if older(n, r):
                    act.wait_ge(u_hmm, u - 1)
                act.copy(xT[r % 2][0:ONE + 1, :], (ps_conv, ps_tok)[r % 2][0:ONE + 1, :]).then_inc(u_xT, 1)

            def hidden_unit(n, r):
                u = unit(n, r)
                act.wait_ge(u_hmm, u + 1)
                if older(n, r):
                    act.wait_ge(u_ymm, u - 1)
                act.activation(hid[r % 2], (ps_q, ps_k)[r % 2][:, :], ACT.Relu).then_inc(u_hid, 1)

            act.wait_ge(s_blk, PADS)
            pad_extents(act, PADS_SP, EXT)
            act.wait_ge(s_blk, BLK)
            act.dma_start(blk_dram.rearrange("a p k -> p a k"), blk_i[:]).then_inc(blk_out, 16)
            act.wait_ge(blk_out, 16)
            act.dma_start(blk_row[:], blk_dram.rearrange("a p k -> a (p k)").unsqueeze(0)).then_inc(blk_in_row, 16)

            units(act, (0, turned_unit), (1, hidden_unit))

            act.wait_ge(cls_y, 18)
            for b in range(B):
                act.dma_start(out[b, 0:1, :], osb[:]).then_inc(out_done, 16)
            CH = FT // 2
            for n in range(NT // FT):
                act.wait_ge(y_sum, 2 * (n + 1))
                q, c0 = divmod(n * CH, NPIX // P)
                for b in range(2):
                    dst = out[2 * q + b, 1 + c0 * P:1 + (c0 + CH) * P, :].rearrange("(t p) c -> p t c", p=P)
                    src = h2[:, n * FT:(n + 1) * FT, :].rearrange("p (t b) c -> p t b c", b=2)[:, :, b, :]
                    act.dma_start(dst, src).then_inc(out_done, 16)


def kernel(**inputs):
    import concourse.bacc as bacc
    from concourse.bass_utils import run_bass_kernel_spmd

    a = {n: np.asarray(v) for n, v in inputs.items()}

    def twice(v):
        return np.ascontiguousarray(np.concatenate([v, v], 0))

    def rows(v):
        return np.ascontiguousarray(np.broadcast_to(v.reshape(1, -1), (P, v.size)))

    def blocks(m):
        d = np.zeros((P, P), m.dtype)
        d[:C, :C] = m
        d[C:, C:] = m
        return d

    wqkv = a["L0_attn_Wqkv"]
    pack = np.zeros((P, E, WCOLS), np.float32)
    pack[:C, :, :HID] = a["L0_ffn_W1"].transpose(1, 0, 2)
    pack[ONE, :, :HID] = a["L0_ffn_b1"]
    pack[96, :, :C] = a["L0_ffn_b2"]
    pack[:, :, HID:] = a["L0_ffn_W2"].transpose(1, 0, 2)
    arrays = {
        "x": a["x"].reshape(B, NPIX, C),
        "cls_rows": rows(a["cls_tok"]),
        "consts": constants(),
        "bn": twice(np.stack([a["L0_tok_bn_gamma"], a["L0_tok_bn_beta"], a["L0_tok_bn_mean"], a["L0_tok_bn_var"]], 1)),
        "conv_w": twice(a["L0_tok_conv_w"].reshape(C, TAPS)),
        "conv_b": twice(a["L0_tok_conv_b"].reshape(C, 1)),
        "lin_w": blocks(a["L0_tok_lin_w"].T),
        "lin_b": twice(a["L0_tok_lin_b"].reshape(C, 1)),
        "wqkv": np.stack([blocks(wqkv[:, n * C:(n + 1) * C]) for n in range(3)], 1),
        "bqkv_col": twice(a["L0_attn_bqkv"].reshape(3, C).T),
        "bqkv_row": rows(a["L0_attn_bqkv"]),
        "wr": blocks(a["L0_ffn_Wr"]),
        "br_row": rows(a["L0_ffn_br"]),
        "experts": pack.reshape(P, E * WCOLS),
    }
    nc = bacc.Bacc("TRN2", target_bir_lowering=False, num_devices=1)
    args = []
    for name, v in arrays.items():
        arrays[name] = v = np.ascontiguousarray(v)
        args.append(nc.dram_tensor(name, v.shape, mybir.dt.from_np(v.dtype), kind="ExternalInput").ap())
    args.append(nc.dram_tensor("out", (B, NPIX + 1, C), F32, kind="ExternalOutput").ap())
    tower(nc, *args)
    r = run_bass_kernel_spmd(nc, [arrays], core_ids=[0])
    return r.results[0]["out"]
```

```python
from contextlib import ExitStack

import numpy as np

import concourse.bass as bass
from concourse import mybir

ALU = mybir.AluOpType
ACT = mybir.ActivationFunctionType
AX = mybir.AxisListType
F32 = mybir.dt.float32
BF16 = mybir.dt.bfloat16
U32 = mybir.dt.uint32
I32 = mybir.dt.int32

P = 128
B, IMG, C = 4, 64, 64
NPIX = IMG * IMG
PAD = IMG + 2
PAIRS = B // 2
STEPS = 4
TILES = 2 * STEPS
W = STEPS * P
GROUPS = PAIRS * NPIX // W
GPP = GROUPS // PAIRS
ROWS_G = W // IMG
NT = GROUPS * TILES
E, HID = 64, 128
K2 = 2
TAPS = 9
PARTS = 4
EARLY = 3
ALPHA = float(np.float32(0.99))
DECAY = ALPHA ** P
EPS = 1e-5
ROW = C + 4
ONE, GAP, DEST = C, C + 1, C + 2
PICKS = K2 * (B * NPIX + 1)
MAX_LAG = 3
LATE = MAX_LAG + 1
SPARE_BLOCKS = LATE * W * 2 // P + 1
REGION = 119
FULL = (REGION - SPARE_BLOCKS) * P
SPARES = K2 * ((GROUPS - LATE) * W * 2 + 1) // (FULL + 1)
assert (GROUPS - LATE) * W * 2 + 1 <= REGION * P - P
EXT = E + SPARES
NBLK = (PICKS + EXT * (P - 1)) // P
NBLK = -(-NBLK // 4) * 4
YROWS = K2 * P * NT + K2
ROUND = float(2 ** 23)
EMPTY = E * REGION + SPARES * SPARE_BLOCKS
SLOTS = (EMPTY + 1) * P
FAR = 4.0e6
assert max(SLOTS, YROWS) < FAR
WCOLS = HID + C
UB = 4
UNITS = NBLK // UB
RING = 4
LAPS = UNITS // RING

K_ID, K_MASK, K_TRI = 0, P, 2 * P
K_FIRST, K_KEEP = 3 * P, 3 * P + GROUPS
K_IOTA = K_KEEP + GROUPS
K_DEST = K_IOTA + E
K_VDEC = K_DEST + K2 * NT
K_QDEC = K_VDEC + 1
K_ROW1 = K_QDEC + 1
K_CDEST = K_ROW1 + 1
K_BLK = K_CDEST + K2
K_BASE = K_BLK + UB
K_EPS = K_BASE + EXT
K_COLS = K_EPS + 1


def constants():
    k = np.zeros((P, K_COLS), np.float64)
    i = np.arange(P)
    k[:, K_ID:K_ID + P] = np.eye(P)
    k[:, K_MASK:K_MASK + P] = (i[:, None] <= i[None, :]) / DECAY
    k[:, K_TRI:K_TRI + P] = i[:, None] < i[None, :]
    k[:, K_FIRST:K_FIRST + GROUPS] = np.arange(GROUPS) % GPP == 0
    k[:, K_KEEP:K_KEEP + GROUPS] = np.arange(GROUPS) % GPP != 0
    k[:, K_IOTA:K_IOTA + E] = np.arange(E)
    t = np.arange(NT)
    first = (t // (2 * NPIX // P) * 2 + t % 2) * NPIX + t % (2 * NPIX // P) // 2 * P
    k[:, K_DEST:K_DEST + K2 * NT] = (np.arange(K2)[:, None] * B * NPIX + first).reshape(1, -1) + i[:, None]
    k[:, K_VDEC] = ALPHA ** -i.astype(np.float64)
    k[:, K_QDEC] = ALPHA ** i.astype(np.float64) * DECAY / np.sqrt(C)
    k[:, K_ROW1] = FAR * (i > 0)
    k[:, K_CDEST:K_CDEST + K2] = K2 * P * NT + np.arange(K2)
    k[:, K_BLK:K_BLK + UB] = UB * i[:, None] + np.arange(UB)
    k[:, K_BASE:K_BASE + EXT] = np.append(np.arange(E) * REGION, E * REGION + np.arange(SPARES) * SPARE_BLOCKS) * P
    k[:, K_EPS] = EPS
    return k.astype(np.float32)


CLS = ("mean xc sq ss std rstd hn turned hnT qkv qkvb qk dot att h2 kk vv outer state0 state1 "
       "mean2 xc2 sq2 ss2 std2 rstd2 hn2 turned2 hn2T logit logitb top topi topf hot0 hot1 hots "
       "gap0 gap1 rows dests count pos0s pos1s pos posi").split()


def tower(nc, x, cls_rows, consts, bn, conv_w, conv_b, lin_w, lin_b, wqkv, bqkv_col, bqkv_row,
          wr, br_row, experts, b2_row, out):
    with ExitStack() as ctx:
        def sb(name, shape, dt=F32):
            return ctx.enter_context(nc.sbuf_tensor(name, shape, dt))

        def psum(name):
            return ctx.enter_context(nc.psum_tensor(name, [P, 512], F32))

        def sem(name):
            return ctx.enter_context(nc.semaphore(name))

        slots = nc.dram_tensor("slot_rows", [SLOTS, ROW], F32, kind="Internal").ap()
        ybuf = nc.dram_tensor("gated_results", [YROWS, C], F32, kind="Internal").ap()

        h_dram = nc.dram_tensor("residual", [B, NPIX, C], F32, kind="Internal").ap()
        blk_dram = nc.dram_tensor("block_table", [2, P, UB], I32, kind="Internal").ap()

        ps_conv = psum("ps_conv")
        ps_tok = psum("ps_tok")
        ps_turn = psum("ps_turn")
        ps_q = psum("ps_q")
        ps_k = psum("ps_k")
        ps_v = psum("ps_v")
        ps_p = psum("ps_p")
        ps_o = psum("ps_o")

        kc = sb("kc", [P, K_COLS])
        wall = sb("wall", [P, E * WCOLS])
        xs = wall[:, 0:PAIRS * NPIX].rearrange("p (q y x) -> p q y x", q=PAIRS, x=IMG)
        img = sb("img", [P, PAIRS, PAD, PAD])
        early = sb("early", [P, W])
        h2 = sb("h2", [P, NT, C])
        bn_s = sb("bn_s", [P, 8])
        cw = sb("cw", [P, TAPS + 1])
        linT = sb("linT", [P, P])
        lb = sb("lb", [P, 2])
        wtap = sb("wtap", [P, TAPS - EARLY, P])
        wq = sb("wq", [P, 3, P])
        bq = sb("bq", [P, 3])
        bqr = sb("bqr", [P, 3 * C])
        wrs = sb("wrs", [P, P])
        brr = sb("brr", [P, E])
        tri = sb("tri", [P, P], BF16)
        ones = sb("ones", [P, P], BF16)
        empty = sb("empty", [P, ROW])
        work = sb("work", [P, 8, W])
        hT, hnT, hn2T, qT, kT, vT, ktok, vtok = (work[:, n, :] for n in range(8))
        b2s = work[:].rearrange("p n w -> p (n w)")
        xc = sb("xc", [P, TILES, C])
        sq = sb("sq", [P, TILES, C])
        hn = sb("hn", [P, TILES, C])
        xc2 = sb("xc2", [P, TILES, C])
        sq2 = sb("sq2", [P, TILES, C])
        hn2 = sb("hn2", [P, TILES, C])
        hn2r = sb("hn2r", [P, TILES, C])
        ssum = sb("ssum", [P, 3, TILES])
        ssum2 = sb("ssum2", [P, 3, TILES])
        am = sb("am", [P, 2, W])
        state = sb("state", [P, STEPS + 1, P])
        state0 = sb("state0", [P, P])
        st_in = sb("st_in", [P, P])
        logit = sb("logit", [P, TILES, E])
        top = sb("top", [P, TILES, 8])
        topi = sb("topi", [P, TILES, 8], U32)
        topf = sb("topf", [P, K2, TILES])
        hot = sb("hot", [P, K2, TILES, E], BF16)
        hots = sb("hots", [P, TILES, E], BF16)
        tail = sb("tail", [P, K2, TILES, 4])
        rank = sb("rank", [P, TILES, E])
        pick = sb("pick", [P, K2, TILES, E])
        posf = sb("posf", [P, K2, TILES])
        posi = sb("posi", [P, K2 * TILES], U32)
        posi_last = sb("posi_last", [P, K2 * TILES], U32)
        rows = sb("rows", [P, K2, TILES, ROW])
        cnt = sb("cnt", [P, E])
        zero = sb("zero", [P, E])
        cl = sb("cl", [P, C])
        ch2 = sb("ch2", [P, C])
        cb = sb("cb", [P, 17, C])
        crow = sb("crow", [P, K2, ROW])
        ctop = sb("ctop", [P, 8])
        ctopi = sb("ctopi", [P, 8], U32)
        cs = sb("cs", [P, 16])
        cposi = sb("cposi", [P, K2], U32)
        chots = sb("chots", [P, E])
        ck2 = sb("ck2", [P, 2, P])
        blk_f = sb("blk_f", [P, 2, UB])
        blk_i = sb("blk_i", [P, 2, UB], I32)
        blk_row = sb("blk_row", [1, 2, P * UB], I32)
        pad_row = sb("pad_row", [1, EXT], I32)
        ext = sb("ext", [P, 7, EXT])
        blk_at = sb("blk_at", [P, 5, UB, EXT])
        move = sb("move", [P, 6, E])
        spare_at = sb("spare_at", [P, 3, SPARES, E])
        spare = img[:, :, :, :].rearrange("p a b c -> p (a b c)")
        at = [0]

        def reuse(n):
            at[0] += n
            return spare[:, at[0] - n:at[0]]
        xin = [reuse(UB * ROW).rearrange("p (k c) -> p k c", k=UB) for _ in range(RING)]
        ysb = [reuse(UB * C).rearrange("p (k c) -> p k c", k=UB) for _ in range(RING)]
        xT = [reuse(W) for _ in range(2)]
        hid = [reuse(W) for _ in range(2)]
        b2u = [reuse(UB * C).rearrange("p (k c) -> p k c", k=UB) for _ in range(RING)]
        stage = [reuse(UB * WCOLS).rearrange("p (k c) -> p k c", k=UB) for _ in range(RING)]
        gate = [[reuse(2 * UB).rearrange("p (a k) -> p a k", a=2) for _ in range(RING)] for _ in range(3)]
        ydst = [sb(f"ydst{r}", [P, UB], U32) for r in range(RING)]
        FT = 16
        RUN = NPIX // P
        h_run = h2[:].rearrange("p (b j) c -> p b j c", b=B)
        yin = [wall[:, i * K2 * FT * C:(i + 1) * K2 * FT * C].rearrange("p (k t c) -> p k t c", k=K2, t=FT)
               for i in range(4)]
        ycls = sb("ycls", [1, K2, C])
        osb = sb("osb", [1, C])

        ident = kc[:, K_ID:K_ID + P]

        def wide(ap, n=TILES):
            return ap.unsqueeze(2).to_broadcast([P, n, C])

        def all_tiles(ap):
            return ap.unsqueeze(1).to_broadcast([P, TILES, E])

        consts_in = sem("consts_in")
        x_in = [[sem(f"x_in{q}{n}") for n in range(PARTS)] for q in range(PAIRS)]
        setup_v = sem("setup_v")
        bn_std = sem("bn_std")
        zeroed = sem("zeroed")
        bias_mm = sem("bias_mm")
        bias_ok = sem("bias_ok")
        img_ok = sem("img_ok")
        filled = sem("filled")
        filled_pool = sem("filled_pool")
        weights_in = sem("weights_in")
        cls_step = sem("cls_step")
        cls_sent = sem("cls_sent")
        s_conv = sem("s_conv")
        s_hT = sem("s_hT")
        s_early = sem("s_early")
        s_htok = sem("s_htok")
        s_h = sem("s_h")
        s_ln1 = sem("s_ln1")
        s_sq1 = sem("s_sq1")
        s_turn1 = sem("s_turn1")
        s_hnT = sem("s_hnT")
        s_qmm = sem("s_qmm")
        s_kmm = sem("s_kmm")
        s_vmm = sem("s_vmm")
        s_q = sem("s_q")
        s_k = sem("s_k")
        s_v = sem("s_v")
        s_kturn = sem("s_kturn")
        s_vturn = sem("s_vturn")
        s_ktok = sem("s_ktok")
        s_vtok = sem("s_vtok")
        s_score = sem("s_score")
        s_am = sem("s_am")
        s_pmm = sem("s_pmm")
        s_stin = sem("s_stin")
        s_state = sem("s_state")
        s_omm = sem("s_omm")
        s_h2 = sem("s_h2")
        s_ln2 = sem("s_ln2")
        s_sq2 = sem("s_sq2")
        s_turn2 = sem("s_turn2")
        s_hn2T = sem("s_hn2T")
        s_hn2r = sem("s_hn2r")
        s_lmm = sem("s_lmm")
        s_logit = sem("s_logit")
        s_top = sem("s_top")
        s_topi = sem("s_topi")
        s_hot = sem("s_hot")
        s_tail = sem("s_tail")
        s_rank = sem("s_rank")
        s_count = sem("s_count")
        s_move = sem("s_move")
        s_pos = sem("s_pos")
        s_rows = sem("s_rows")
        s_sent = [sem(f"s_sent{s}") for s in range(STEPS)]
        s_blk = sem("s_blk")
        blk_out = sem("blk_out")
        blk_in_row = sem("blk_in_row")
        u_in = [sem(f"u_in{r}") for r in range(RING)]
        u_stage = sem("u_stage")
        u_b2 = sem("u_b2")
        u_sum = sem("u_sum")
        u_turn = sem("u_turn")
        u_xT = sem("u_xT")
        u_hmm = sem("u_hmm")
        u_hid = sem("u_hid")
        u_ymm = sem("u_ymm")
        u_y = sem("u_y")
        u_dst = sem("u_dst")
        u_gap = sem("u_gap")
        u_exp = sem("u_exp")
        u_gate = sem("u_gate")
        u_sent = [sem(f"u_sent{r}") for r in range(RING)]
        y_in = [sem(f"y_in{r}") for r in range(4)]
        y_sum = sem("y_sum")
        cls_y = sem("cls_y")
        h_out = sem("h_out")
        h_in = sem("h_in")
        out_done = sem("out_done")

        POS, LN, SQ, TAIL = 4, 4, TILES + 1, 3
        BLK, PADS = 20 + 4 + 3 + SPARES, 11 + SPARES
        SETUP_V = 5 + TAPS - EARLY

        def tap_view(g, tap):
            pair, y0 = (g // GPP, g % GPP * ROWS_G)
            dy, dx = divmod(tap, 3)
            if isinstance(g, int):
                return img[:, pair, y0 + dy:y0 + dy + ROWS_G, dx:dx + IMG]
            row = pair * PAD + y0 + dy
            return img[:, :, :, :].rearrange("p a b c -> p (a b) c")[:, bass.ds(row, ROWS_G), dx:dx + IMG]

        early_rows = early[:].rearrange("p (y x) -> p y x", x=IMG)

        def later(g):
            return not (isinstance(g, int) and g == 0)

        def pipeline(eng, *stages, before_last=None):
            def step(i):
                for lag, f in stages:
                    if 0 <= i - lag < GROUPS:
                        f(i - lag)
            for i in range(-1, MAX_LAG + 1):
                step(i)
            with eng.Fori(MAX_LAG + 1, GROUPS - 1) as i:
                for lag, f in stages:
                    f(i - lag)
            if before_last:
                before_last()
            for i in range(GROUPS - 1, GROUPS + MAX_LAG):
                step(i)

        def unit(n, r):
            return n * RING + r

        def older(n, r, by=2):
            return not isinstance(n, int) or unit(n, r) >= by

        def units(eng, *stages):
            def step(n, r):
                for lag, f in stages:
                    if r >= lag:
                        f(n, r - lag)
                    elif later(n):
                        f(n - 1, r - lag + RING)
            for r in range(RING):
                step(0, r)
            with eng.Fori(1, LAPS) as n:
                for r in range(RING):
                    step(n, r)
            for u in range(LAPS * RING, UNITS + max(lag for lag, _ in stages)):
                for lag, f in stages:
                    if u - lag < UNITS:
                        f(*divmod(u - lag, RING))

        def cls_after(eng, *names):
            eng.wait_ge(cls_step, max(CLS.index(n) for n in names) + 1)

        PADS_SP, PADS_ACT = 34, 58

        def pad_extents(eng, lo, hi, done):
            at_once = 8
            regs = [eng.alloc_register(f"pad{lo}_{k}") for k in range(at_once)]

            def pad(at, n):
                eng.load(regs[0:n], pad_row[0:1, bass.ds(at, n)])
                for k in range(n):
                    first = eng.snap(regs[k], min_val=0, max_val=SLOTS - P)
                    eng.dma_start(slots[bass.ds(first, P)], empty[:]).then_inc(done, 16)
            if hi - lo >= at_once:
                with eng.Fori(0, (hi - lo) // at_once) as n:
                    pad(n * at_once + lo, at_once)
            if (hi - lo) % at_once:
                pad(hi - (hi - lo) % at_once, (hi - lo) % at_once)

        block = ctx.enter_context(nc.Block())

        @block.sync
        def _(sp):
            loads = [(kc[:], consts), (cl[:], cls_rows), (bn_s[:, 0:4], bn), (cw[:, 0:TAPS], conv_w),
                     (cw[:, TAPS:TAPS + 1], conv_b), (linT[:], lin_w), (lb[:, 0:1], lin_b),
                     (wq[:], wqkv), (bq[:], bqkv_col), (bqr[:], bqkv_row), (wrs[:], wr), (brr[:], br_row)]
            for dst, src in loads:
                sp.dma_start(dst, src).then_inc(consts_in, 16)
            for q in range(PAIRS):
                for n in range(PARTS):
                    y = slice(n * IMG // PARTS, (n + 1) * IMG // PARTS)
                    sp.dma_start(xs[:, q, y, :], x[q].rearrange("p (y x) -> p y x", x=IMG)[:, y, :]
                                 ).then_inc(x_in[q][n], 16)
            sp.wait_ge(zeroed, 5)
            sp.dma_start(slots[EMPTY * P:SLOTS], empty[:]).then_inc(filled, 16)
            sp.wait_ge(img_ok, PAIRS * PARTS)
            sp.dma_start(wall[:], experts).then_inc(weights_in, 16)

            sp.wait_ge(s_rank, GROUPS)
            sp.dma_start(b2s[:, 0:E * C], b2_row.to_broadcast([P, E * C])).then_inc(weights_in, 16)
            sp.wait_ge(s_blk, PADS)
            pad_extents(sp, 0, PADS_SP, filled)
            sp.wait_ge(filled, 16 * (PADS_ACT + 1))
            sp.wait_ge(filled_pool, 16 * (EXT - PADS_ACT))
            sp.wait_ge(cls_sent, 32)
            for s in range(STEPS):
                sp.wait_ge(s_sent[s], GROUPS * 64)
            sp.wait_ge(blk_in_row, 16)
            by_block = slots.rearrange("(n p) c -> n p c", p=P)
            blk_regs = [sp.alloc_register(f"block{k}") for k in range(UB)]

            def load_unit(n, r, old):
                u = unit(n, r)
                sp.load(blk_regs, blk_row[0:1, 1, bass.ds(u * UB, UB)])
                at = [sp.snap(blk_regs[k], min_val=0, max_val=EMPTY) for k in range(UB)]
                if old:
                    before = sp.snap(u - RING + 1)
                    sp.wait_ge(u_turn, before)
                    sp.wait_ge(u_dst, before)
                    sp.wait_ge(u_exp, before)
                for k in range(UB):
                    sp.dma_start(xin[r][:, k, :], by_block[bass.ds(at[k], 1)].rearrange("o p c -> p (o c)")
                                 ).then_inc(u_in[r], 16)
            for r in range(RING):
                load_unit(0, r, False)
            by_chunk = h2[:].rearrange("p (q t b) c -> p q t b c", q=PAIRS, b=2)
            sp.wait_ge(s_h2, GROUPS)
            for b in range(B):
                for r in range(RING):
                    load_unit(1 + b, r, True)
                    t = slice(r * RUN // RING, (r + 1) * RUN // RING)
                    sp.dma_start(h_dram[b].rearrange("(t p) c -> p t c", p=P)[:, t, :],
                                 by_chunk[:, b // 2, t, b % 2, :]).then_inc(h_out, 16)
            sp.wait_ge(h_out, B * RING * 16)
            sp.wait_ge(s_ln2, LN * GROUPS)
            for b in range(B):
                for r in range(RING):
                    load_unit(1 + B + b, r, True)
                    j = slice(r * RUN // RING, (r + 1) * RUN // RING)
                    sp.dma_start(h_run[:, b, j, :], h_dram[b].rearrange("(p j) c -> p j c", p=P)[:, j, :]
                                 ).then_inc(h_in, 16)
            with sp.Fori(1 + 2 * B, LAPS) as n:
                for r in range(RING):
                    load_unit(n, r, True)
            for r in range(UNITS % RING):
                load_unit(LAPS, r, True)
            for r in range(RING):
                sp.wait_ge(u_sent[r], (UNITS + RING - 1 - r) // RING * UB * 16)
            by_run = ybuf[0:K2 * B * NPIX].rearrange("(k b p j) c -> b p k j c", k=K2, b=B, p=P)
            sp.dma_start(ycls[:], ybuf[K2 * P * NT:YROWS].unsqueeze(0)).then_inc(cls_y, 16)
            for n in range(NT // FT):
                if n >= 4:
                    sp.wait_ge(y_sum, 2 * (n - 3))
                sp.dma_start(yin[n % 4], by_run[n * FT // RUN][:, :, n * FT % RUN:n * FT % RUN + FT, :]).then_inc(y_in[n % 4], 16)
            sp.wait_ge(out_done, 16 * (NT // FT + B))

        @block.gpsimd
        def _(pool):
            cls_after(pool, "posi")
            for k in range(K2):
                nc.gpsimd.indirect_dma_start(slots, bass.IndirectOffsetOnAxis(cposi[0:2, k:k + 1], 0),
                                             crow[0:2, k, :], None, bounds_check=SLOTS - 1,
                                             oob_is_err=False).then_inc(cls_sent, 16)

            last_y = pool.alloc_register("last_y")
            pool.reg_mov(last_y, YROWS - 1)
            rows_wanted = pool.alloc_register("rows_wanted")
            pool.reg_mov(rows_wanted, 2)
            y_wanted = pool.alloc_register("y_wanted")
            pool.reg_mov(y_wanted, 1)

            def scatter(g, posi):
                for s in range(STEPS):
                    fixed = isinstance(g, int)
                    wanted = 2 * (STEPS * g + s + 1) if fixed else pool.snap(rows_wanted)
                    if s == 0:
                        pool.wait_ge(s_pos, POS * (g + 1))
                    pool.wait_ge(s_rows, wanted)
                    if not fixed:
                        pool.reg_add(rows_wanted, rows_wanted, 2)
                    for k in range(K2):
                        for b in range(2):
                            t = 2 * s + b
                            nc.gpsimd.indirect_dma_start(
                                slots, bass.IndirectOffsetOnAxis(posi[:, k * TILES + t:k * TILES + t + 1], 0),
                                rows[:, k, t, :], None).then_inc(s_sent[s], 16)

            with pool.Fori(0, GROUPS - 1) as g:
                scatter(g, posi)
            scatter(GROUPS - 1, posi_last)
            pool.wait_ge(s_blk, PADS)
            pad_extents(pool, PADS_ACT, EXT, filled_pool)

            def send_unit(n, r):
                fixed = isinstance(n, int)
                wanted = n * RING + r + 1 if fixed else pool.snap(y_wanted)
                pool.wait_ge(u_dst, n * RING + r + 1)
                pool.wait_ge(u_y, wanted)
                if not fixed:
                    pool.reg_add(y_wanted, y_wanted, 1)
                for k in range(UB):
                    nc.gpsimd.indirect_dma_start(
                        ybuf, bass.IndirectOffsetOnAxis(ydst[r][:, k:k + 1], 0), ysb[r][:, k, :], None,
                        bounds_check=last_y, oob_is_err=False).then_inc(u_sent[r], 16)
            with pool.Fori(0, LAPS) as n:
                for r in range(RING):
                    send_unit(n, r)
            for r in range(UNITS % RING):
                send_unit(LAPS, r)

        @block.tensor
        def _(pe):
            pe.wait_ge(consts_in, 12 * 16)
            pe.matmul(ps_o[:, 0:1], linT[:], cw[:, TAPS:TAPS + 1], start=True, stop=True).then_inc(bias_mm, 1)
            cls_after(pe, "hn")
            pe.transpose(ps_turn[0:C, 0:P], cb[:, 3, :], ident).then_inc(cls_step, 1)
            cls_after(pe, "hnT")
            pe.matmul(ps_q[:, 0:3 * C], ck2[0:C, 0, :], wq[0:C, :, 0:C], start=True, stop=True
                      ).then_inc(cls_step, 1)
            cls_after(pe, "kk", "vv")
            pe.matmul(ps_k[:, 0:P], ck2[0:1, 0, :], ck2[0:1, 1, :], start=True, stop=True
                      ).then_inc(cls_step, 1)
            cls_after(pe, "hn2")
            pe.transpose(ps_turn[0:C, 0:P], cb[:, 11, :], ident).then_inc(cls_step, 1)
            cls_after(pe, "hn2T")
            pe.matmul(ps_q[:, 0:E], ck2[0:C, 0, :], wrs[0:C, 0:E], start=True, stop=True
                      ).then_inc(cls_step, 1)
            def taps(g):
                if later(g):
                    pe.wait_ge(s_hT, g)
                for tap in range(EARLY, TAPS):
                    pe.matmul(ps_conv[:, :], wtap[:, tap - EARLY, :], tap_view(g, tap), start=tap == EARLY,
                              stop=False, skip_group_check=True)
                pe.wait_ge(s_early, EARLY * (g + 1))
                m = pe.matmul(ps_conv[:, :], linT[:], early[:], start=False, stop=True, skip_group_check=True)
                m.then_inc(s_conv, 1)

            def turn_hn(g):
                pe.wait_ge(s_ln1, LN * (g + 1))
                if isinstance(g, int):
                    if g >= 2:
                        pe.wait_ge(s_hn2T, g - 1)
                else:
                    pe.wait_ge(s_hn2T, g - 1)
                for s in range(STEPS):
                    m = pe.transpose(ps_turn[:, s * P:(s + 1) * P],
                                     hn[:, 2 * s:2 * s + 2, :].rearrange("p t c -> p (t c)"), ident)
                m.then_inc(s_turn1, 1)

            def ranks(g):
                pe.wait_ge(s_hot, 3 * (g + 1))
                pe.wait_ge(s_state, 2 * STEPS * min_groups(g, 2))
                flat = hots[:].rearrange("p t e -> p (t e)")
                pe.matmul(ps_p[:, :], tri[:], flat, start=True, stop=False, skip_group_check=True)
                for k in range(1, TILES):
                    m = pe.matmul(ps_p[:, k * E:], ones[:], flat[:, 0:(TILES - k) * E], start=False,
                                  stop=k == TILES - 1, skip_group_check=True)
                pe.wait_ge(s_h2, min_groups(g, 2))
                for t in range(TILES):
                    m = pe.matmul(ps_o[:, 0:E], ones[:], hots[:, t, :], start=t == 0, stop=t == TILES - 1,
                                  skip_group_check=True)
                m.then_inc(s_rank, 1)

            def kv(g):
                pe.wait_ge(s_hnT, g + 1)
                if later(g):
                    pe.wait_ge(s_am, 2 * g)
                    pe.wait_ge(s_vtok, g)
                for n, bank, done in ((1, ps_k, s_kmm), (2, ps_v, s_vmm)):
                    pe.matmul(bank[:, :], wq[:, n, :], hnT[:], start=True, stop=True).then_inc(done, 1)

            def q(g):
                if not isinstance(g, int) or g >= 2:
                    pe.wait_ge(s_logit, g - 1)
                pe.matmul(ps_q[:, :], wq[:, 0, :], hnT[:], start=True, stop=True).then_inc(s_qmm, 1)

            def turn_kv(g):
                pe.wait_ge(s_v, g + 1)
                for s in range(STEPS):
                    m = pe.transpose(ps_v[:, s * P:(s + 1) * P], vT[:, s * P:(s + 1) * P], ident)
                m.then_inc(s_vturn, 1)
                pe.wait_ge(s_k, g + 1)
                pe.wait_ge(s_h, min_groups(g, 2))
                for s in range(STEPS):
                    m = pe.transpose(ps_tok[:, s * P:(s + 1) * P], kT[:, s * P:(s + 1) * P], ident)
                m.then_inc(s_kturn, 1)

            def scores(b, bank):
                def product(g):
                    pe.wait_ge(s_q, g + 1)
                    for s in range(STEPS):
                        m = pe.matmul(bank[:, s * P:(s + 1) * P], kT[b * C:(b + 1) * C, s * P:(s + 1) * P],
                                      qT[b * C:(b + 1) * C, s * P:(s + 1) * P], start=True, stop=True)
                    m.then_inc(s_score, 1)
                return product

            def products(g):
                pe.wait_ge(s_ktok, g + 1)
                pe.wait_ge(s_vtok, g + 1)
                if not isinstance(g, int) or g >= 2:
                    pe.wait_ge(s_pos, POS * (g - 2) + 1)
                for s in range(STEPS):
                    m = pe.matmul(ps_p[:, s * P:(s + 1) * P], ktok[:, s * P:(s + 1) * P],
                                  vtok[:, s * P:(s + 1) * P], start=True, stop=True)
                m.then_inc(s_pmm, 1)

            def attend(g):
                pe.wait_ge(s_am, 2 * (g + 1))
                if not isinstance(g, int) or g >= 2:
                    pe.wait_ge(s_count, g - 1)
                for s in range(STEPS):
                    c0 = s * P
                    for b in range(2):
                        pe.matmul(ps_o[:, c0 + b * C:c0 + (b + 1) * C], am[:, b, c0:c0 + P],
                                  vtok[:, c0 + b * C:c0 + (b + 1) * C], start=s == 0 and b == 0, stop=False,
                                  skip_group_check=True)
                pe.wait_ge(s_stin, 2 * (g + 1))
                pe.wait_ge(s_state, 2 * STEPS * g + 2 * (STEPS - 1))
                for s in range(STEPS):
                    c0 = s * P
                    m = pe.matmul(ps_o[:, c0:c0 + P], qT[:, c0:c0 + P], state[:, s, :], start=False,
                                  stop=s == STEPS - 1, skip_group_check=True)
                m.then_inc(s_omm, 1)

            def turn_hn2(g):
                pe.wait_ge(s_ln2, LN * (g + 1))
                pe.wait_ge(s_hnT, min_groups(g, 2))
                for s in range(STEPS):
                    m = pe.transpose(ps_turn[:, s * P:(s + 1) * P],
                                     hn2[:, 2 * s:2 * s + 2, :].rearrange("p t c -> p (t c)"), ident)
                m.then_inc(s_turn2, 1)

            def router(g):
                pe.wait_ge(s_hn2T, g + 1)
                pe.wait_ge(s_am, 2 * min_groups(g, 2))
                for s in range(STEPS):
                    m = pe.matmul(ps_q[:, s * P:(s + 1) * P], hn2T[:, s * P:(s + 1) * P], wrs[:],
                                  start=True, stop=True)
                m.then_inc(s_lmm, 1)

            def turn_h(g):
                pe.wait_ge(s_hT, g + 1)
                if not isinstance(g, int) or g >= 2:
                    pe.wait_ge(s_ktok, g - 1)
                for s in range(STEPS):
                    m = pe.transpose(ps_tok[:, s * P:(s + 1) * P], hT[:, s * P:(s + 1) * P], ident)
                m.then_inc(s_htok, 1)

            def min_groups(g, ahead):
                if isinstance(g, int):
                    return min(g + ahead, GROUPS)
                return g + ahead

            pe.wait_ge(bias_ok, 1)
            pe.wait_ge(img_ok, PARTS)
            cls_after(pe, "logitb", "state1")
            pe.wait_ge(setup_v, SETUP_V)
            pipeline(pe,
                     (0, taps), (1, kv), (0, turn_h), (1, q), (1, turn_kv),
                     (1, scores(0, ps_q)), (3, ranks), (1, scores(1, ps_k)), (2, turn_hn2), (1, products),
                     (2, router), (1, attend), (0, turn_hn))

            def unit_turn(n, r):
                u = unit(n, r)
                pe.wait_ge(u_in[r], UB * 16 * (n + 1))
                if older(n, r):
                    pe.wait_ge(u_xT, u - 1)
                bank = (ps_conv, ps_tok)[r % 2]
                for k in range(UB):
                    m = pe.transpose(bank[0:ONE + 1, k * P:(k + 1) * P], xin[r][:, k, 0:ONE + 1], ident)
                m.then_inc(u_turn, 1)

            def unit_hidden(n, r):
                u = unit(n, r)
                pe.wait_ge(u_xT, u + 1)
                pe.wait_ge(u_stage, UB * (u + 1))
                if older(n, r):
                    pe.wait_ge(u_hid, u - 1)
                bank = (ps_q, ps_k)[r % 2]
                for k in range(UB):
                    m = pe.matmul(bank[:, k * P:(k + 1) * P], stage[r][0:ONE + 1, k, 0:HID],
                                  xT[r % 2][0:ONE + 1, k * P:(k + 1) * P], start=True, stop=True)
                m.then_inc(u_hmm, 1)

            def unit_out(n, r):
                u = unit(n, r)
                pe.wait_ge(u_hid, u + 1)
                if older(n, r):
                    pe.wait_ge(u_y, u - 1)
                bank = (ps_v, ps_p)[r % 2]
                for k in range(UB):
                    m = pe.matmul(bank[:, k * C:(k + 1) * C], hid[r % 2][:, k * P:(k + 1) * P],
                                  stage[r][:, k, HID:WCOLS], start=True, stop=True)
                m.then_inc(u_ymm, 1)

            units(pe, (0, unit_turn), (1, unit_hidden), (2, unit_out))


        @block.vector
        def _(v):
            for edge in (img[:, :, 0:PAD:PAD - 1, :], img[:, :, 1:PAD - 1, 0:1],
                         img[:, :, 1:PAD - 1, PAD - 1:PAD]):
                v.memset(edge, 0.0).then_inc(zeroed, 1)
            v.memset(empty[:], 0.0).then_inc(zeroed, 1)
            v.wait_ge(zeroed, 4)
            v.memset(empty[:, DEST:DEST + 1], FAR).then_inc(zeroed, 1)
            v.memset(state[:], 0.0).then_inc(zeroed, 1)
            v.memset(state0[:], 0.0).then_inc(zeroed, 1)
            v.memset(ones[:], 1.0).then_inc(zeroed, 1)
            v.memset(zero[:], 0.0).then_inc(zeroed, 1)
            v.memset(tail[:], 0.0).then_inc(zeroed, 1)
            v.memset(crow[:], 0.0).then_inc(zeroed, 1)
            v.wait_ge(zeroed, 11)
            v.memset(tail[:, :, :, 0:1], 1.0).then_inc(zeroed, 1)
            v.memset(crow[:, :, ONE:ONE + 1], 1.0).then_inc(zeroed, 1)
            v.wait_ge(consts_in, 12 * 16)
            v.wait_ge(bn_std, 1)
            v.reciprocal(bn_s[:, 4:5], bn_s[:, 4:5]).then_inc(setup_v, 1)
            v.wait_ge(setup_v, 1)
            v.tensor_tensor(bn_s[:, 5:6], bn_s[:, 4:5], bn_s[:, 0:1], ALU.mult).then_inc(setup_v, 1)
            v.wait_ge(setup_v, 2)
            v.tensor_tensor(bn_s[:, 6:7], bn_s[:, 5:6], bn_s[:, 2:3], ALU.mult).then_inc(setup_v, 1)
            v.wait_ge(setup_v, 3)
            v.tensor_tensor(bn_s[:, 7:8], bn_s[:, 1:2], bn_s[:, 6:7], ALU.subtract).then_inc(setup_v, 1)
            v.tensor_copy(tri[:], kc[:, K_TRI:K_TRI + P]).then_inc(setup_v, 1)
            for tap in range(EARLY, TAPS):
                v.tensor_scalar(wtap[:, tap - EARLY, :], linT[:], cw[:, tap:tap + 1], None, ALU.mult).then_inc(setup_v, 1)
            v.wait_ge(bias_mm, 1)
            v.tensor_tensor(lb[:, 1:2], ps_o[:, 0:1], lb[:, 0:1], ALU.add).then_inc(bias_ok, 1)

            def done(ins, name):
                assert name in CLS
                ins.then_inc(cls_step, 1)

            def norm_cls(src, o, s, tag):
                v.tensor_reduce(cs[:, s:s + 1], src, AX.X, ALU.add).then_inc(cls_step, 1)
                cls_after(v, "mean" + tag)
                v.scalar_tensor_tensor(cb[:, o, :], cs[:, s:s + 1].to_broadcast([P, C]), -1.0 / C, src,
                                       ALU.mult, ALU.add).then_inc(cls_step, 1)
                cls_after(v, "xc" + tag)
                v.tensor_tensor(cb[:, o + 1, :], cb[:, o, :], cb[:, o, :], ALU.mult).then_inc(cls_step, 1)
                cls_after(v, "sq" + tag)
                v.tensor_reduce(cs[:, s + 1:s + 2], cb[:, o + 1, :], AX.X, ALU.add).then_inc(cls_step, 1)
                cls_after(v, "std" + tag)
                v.reciprocal(cs[:, s + 2:s + 3], cs[:, s + 2:s + 3]).then_inc(cls_step, 1)
                cls_after(v, "rstd" + tag)
                v.tensor_scalar(cb[:, o + 2, :], cb[:, o, :], cs[:, s + 2:s + 3], None, ALU.mult
                                ).then_inc(cls_step, 1)

            norm_cls(cl[:], 1, 0, "")
            cls_after(v, "turned")
            v.tensor_copy(ck2[0:C, 0, :], ps_turn[0:C, 0:P]).then_inc(cls_step, 1)
            cls_after(v, "qkv")
            qkv_c = cb[:, 4:7, :].rearrange("p n c -> p (n c)")
            v.tensor_tensor(qkv_c, ps_q[:, 0:3 * C], bqr[:], ALU.add).then_inc(cls_step, 1)
            cls_after(v, "qkvb")
            v.tensor_tensor(cb[:, 7, :], cb[:, 4, :], cb[:, 5, :], ALU.mult).then_inc(cls_step, 1)
            cls_after(v, "qk")
            v.tensor_reduce(cs[:, 3:4], cb[:, 7, :], AX.X, ALU.add).then_inc(cls_step, 1)
            cls_after(v, "dot")
            v.tensor_scalar(cb[:, 8, :], cb[:, 6, :], cs[:, 3:4], float(1 / np.sqrt(C)), ALU.mult, ALU.mult
                            ).then_inc(cls_step, 1)
            cls_after(v, "att")
            v.tensor_tensor(ch2[:], cb[:, 8, :], cl[:], ALU.add).then_inc(cls_step, 1)
            v.tensor_copy(ck2[:, 0, :].rearrange("p (a c) -> p a c", a=2),
                          cb[:, 5, :].unsqueeze(1).to_broadcast([P, 2, C])).then_inc(cls_step, 1)
            v.tensor_copy(ck2[:, 1, :].rearrange("p (a c) -> p a c", a=2),
                          cb[:, 6, :].unsqueeze(1).to_broadcast([P, 2, C])).then_inc(cls_step, 1)
            cls_after(v, "outer")
            for b in range(2):
                d = slice(b * C, (b + 1) * C)
                v.tensor_scalar(state0[d, d], ps_k[d, d], ALPHA / DECAY, None, ALU.mult
                                ).then_inc(cls_step, 1)
            norm_cls(ch2[:], 9, 4, "2")
            cls_after(v, "turned2")
            v.tensor_copy(ck2[0:C, 0, :], ps_turn[0:C, 0:P]).then_inc(cls_step, 1)
            cls_after(v, "logit")
            v.tensor_tensor(cb[:, 12, :], ps_q[:, 0:E], brr[:], ALU.add).then_inc(cls_step, 1)
            cls_after(v, "logitb")
            v.max(ctop[:], cb[:, 12, :]).then_inc(cls_step, 1)
            cls_after(v, "top")
            v.max_index(ctopi[:], ctop[:], cb[:, 12, :]).then_inc(cls_step, 1)
            cls_after(v, "topi")
            v.tensor_copy(cs[:, 8:10], ctopi[:, 0:2]).then_inc(cls_step, 1)
            cls_after(v, "topf")
            for k in range(K2):
                v.tensor_scalar(cb[:, 13 + k, :], kc[:, K_IOTA:K_IOTA + E], cs[:, 8 + k:9 + k], None,
                                ALU.is_equal).then_inc(cls_step, 1)
            cls_after(v, "hot1")
            v.tensor_tensor(chots[:], cb[:, 13, :], cb[:, 14, :], ALU.add).then_inc(cls_step, 1)
            for k in range(K2):
                v.tensor_tensor(crow[:, k, GAP:GAP + 1], ctop[:, 1 - k:2 - k], ctop[:, k:k + 1], ALU.subtract
                                ).then_inc(cls_step, 1)
            v.tensor_copy(crow[:, :, 0:C], cb[:, 11, :].unsqueeze(1).to_broadcast([P, K2, C])
                          ).then_inc(cls_step, 1)
            v.tensor_copy(crow[:, :, DEST:DEST + 1], kc[:, K_CDEST:K_CDEST + K2].unsqueeze(2)
                          ).then_inc(cls_step, 1)
            cls_after(v, "hots")
            base = kc[:, K_BASE:K_BASE + E]
            v.tensor_tensor(cnt[:], chots[:], base, ALU.add).then_inc(cls_step, 1)
            for k in range(K2):
                v.tensor_tensor(cb[:, 15 + k, :], cb[:, 13 + k, :], base, ALU.mult
                                ).then_inc(cls_step, 1)
            cls_after(v, "pos1s")
            v.tensor_reduce(cs[:, 14:16], cb[:, 15:17, :], AX.X, ALU.add).then_inc(cls_step, 1)
            cls_after(v, "pos")
            v.tensor_scalar(cposi[:], cs[:, 14:16], kc[:, K_ROW1:K_ROW1 + 1], None, ALU.add
                            ).then_inc(cls_step, 1)
            cls_after(v, "posi")

            def ranked(g):
                v.wait_ge(s_rank, g + 1)
                if later(g):
                    v.wait_ge(s_pos, POS * g)
                    v.wait_ge(s_count, g)
                v.tensor_tensor(rank[:], ps_p[:, :].rearrange("p (t e) -> p t e", e=E), all_tiles(cnt[:]),
                                ALU.add).then_inc(s_pos, 1)

            def counted(g):
                v.wait_ge(s_pos, POS * g + 1)
                v.tensor_tensor(cnt[:], cnt[:], ps_o[:, 0:E], ALU.add).then_inc(s_count, 1)
                if isinstance(g, int) and g == GROUPS - 1:
                    v.wait_ge(s_count, GROUPS)
                    padding()

            moved, order, to, stayed, dist, gone = (move[:, k, :] for k in range(6))
            def b(n):
                v.wait_ge(s_blk, n)
            count, blocks_, ends, starts, shift, rounded, owner = (ext[:, k, :] for k in range(7))
            mine_of, used_of, owner_of = (spare_at[:, k] for k in range(3))
            ext_base = kc[:, K_BASE:K_BASE + EXT]

            def over_spares(ap):
                return ap.unsqueeze(1).to_broadcast([P, SPARES, E])

            def padding():
                v.tensor_tensor(dist, stayed, cnt[:], ALU.subtract).then_inc(s_blk, 1)
                for k in range(SPARES):
                    v.scalar_tensor_tensor(mine_of[:, k, :], order, float(k + 1), moved, ALU.is_equal, ALU.mult
                                           ).then_inc(s_blk, 1)
                v.tensor_tensor(gone, cnt[:], to, ALU.subtract).then_inc(s_blk, 1)
                b(1)
                v.tensor_tensor(dist, dist, moved, ALU.mult).then_inc(s_blk, 1)
                v.tensor_tensor(rounded[:, 0:E], cnt[:], base, ALU.subtract).then_inc(s_blk, 1)
                b(4)
                v.tensor_tensor(used_of, mine_of, over_spares(gone), ALU.mult).then_inc(s_blk, 1)
                v.tensor_tensor(owner_of, mine_of, over_spares(kc[:, K_IOTA:K_IOTA + E]), ALU.mult
                                ).then_inc(s_blk, 1)
                b(6)
                v.tensor_tensor(count[:, 0:E], rounded[:, 0:E], dist, ALU.add).then_inc(s_blk, 1)
                b(7)
                v.tensor_reduce(count[:, E:EXT], used_of, AX.X, ALU.add).then_inc(s_blk, 1)
                b(8)
                v.tensor_reduce(owner[:, E:EXT], owner_of, AX.X, ALU.add).then_inc(s_blk, 1)
                v.tensor_copy(owner[:, 0:E], kc[:, K_IOTA:K_IOTA + E]).then_inc(s_blk, 1)
                b(10)
                v.tensor_tensor(pad_row[:], count[0:1, :], ext_base[0:1, :], ALU.add).then_inc(s_blk, 1)

            def picked(g):
                v.wait_ge(s_pos, POS * g + 1)
                v.tensor_tensor(pick[:], hot[:], rank[:].unsqueeze(1).to_broadcast([P, K2, TILES, E]),
                                ALU.mult).then_inc(s_pos, 1)

            def slots_summed(g):
                v.wait_ge(s_pos, POS * g + 2)
                v.tensor_reduce(posf[:], pick[:], AX.X, ALU.add).then_inc(s_pos, 1)

            def slots_out(g):
                v.wait_ge(s_pos, POS * g + 3)
                last = isinstance(g, int) and g == GROUPS - 1
                if later(g) and not last:
                    for s in range(STEPS):
                        v.wait_ge(s_sent[s], 64 * g)
                v.tensor_copy((posi_last if last else posi)[:], posf[:].rearrange("p k t -> p (k t)")).then_inc(s_pos, 1)

            def sums1(g):
                v.wait_ge(s_h, g + 1)
                if later(g):
                    v.wait_ge(s_ln1, LN * g)
                v.tensor_reduce(ssum[:, 0, :], h2[:, bass.ds(g * TILES, TILES), :], AX.X, ALU.add
                                ).then_inc(s_ln1, 1)

            def sums2(g):
                v.wait_ge(s_h2, g + 1)
                if later(g):
                    v.wait_ge(s_ln2, LN * g)
                v.tensor_reduce(ssum2[:, 0, :], h2[:, bass.ds(g * TILES, TILES), :], AX.X, ALU.add
                                ).then_inc(s_ln2, 1)

            def center(g, xc_, sums, s_ln):
                v.wait_ge(s_ln, LN * g + 1)
                v.scalar_tensor_tensor(xc_[:], wide(sums[:, 0, :]), -1.0 / C, h2[:, bass.ds(g * TILES, TILES), :],
                                       ALU.mult, ALU.add).then_inc(s_ln, 1)

            def roots(g, sums, s_ln, s_sq):
                v.wait_ge(s_sq, SQ * (g + 1))
                v.reciprocal(sums[:, 2, :], sums[:, 2, :]).then_inc(s_ln, 1)

            def scaled(g, xc_, out_, sums, s_ln, s_turn):
                v.wait_ge(s_ln, LN * g + 3)
                if later(g):
                    v.wait_ge(s_turn, g)
                v.tensor_tensor(out_[:], xc_[:], wide(sums[:, 2, :]), ALU.mult).then_inc(s_ln, 1)

            def center1(g):
                center(g, xc, ssum, s_ln1)

            def center2(g):
                center(g, xc2, ssum2, s_ln2)

            def roots1(g):
                roots(g, ssum, s_ln1, s_sq1)

            def roots2(g):
                roots(g, ssum2, s_ln2, s_sq2)

            def scaled1(g):
                scaled(g, xc, hn, ssum, s_ln1, s_turn1)

            def scaled2(g):
                if later(g):
                    v.wait_ge(s_hn2r, g)
                scaled(g, xc2, hn2, ssum2, s_ln2, s_turn2)

            def masked(b):
                def mask(g):
                    if later(g):
                        v.wait_ge(s_omm, g)
                    v.wait_ge(s_score, 2 * g + b + 1)
                    v.tensor_tensor(am[:, b, :].rearrange("p (s i) -> p s i", s=STEPS),
                                    (ps_q, ps_k)[b][:, :].rearrange("p (s i) -> p s i", s=STEPS),
                                    kc[:, K_MASK:K_MASK + P].unsqueeze(1).to_broadcast([P, STEPS, P]),
                                    ALU.mult).then_inc(s_am, 1)
                return mask

            def early_taps(lo, hi):
                def add(g):
                    for tap in range(lo, hi):
                        v.wait_ge(s_early, EARLY * g + tap)
                        v.scalar_tensor_tensor(early_rows, tap_view(g, tap), cw[:, tap:tap + 1], early_rows,
                                               ALU.mult, ALU.add).then_inc(s_early, 1)
                return add

            def group_column(g, at):
                return kc[:, at + g:at + g + 1] if isinstance(g, int) else kc[:, bass.ds(g + at, 1)]

            def first_state(g):
                v.tensor_scalar(st_in[:], state0[:], group_column(g, K_FIRST), None, ALU.mult).then_inc(s_stin, 1)

            def carried(g):
                if later(g):
                    v.wait_ge(s_omm, g)
                    v.wait_ge(s_state, 2 * STEPS * g)
                v.wait_ge(s_stin, 2 * g + 1)
                v.scalar_tensor_tensor(state[:, 0, :], state[:, STEPS, :], group_column(g, K_KEEP), st_in[:],
                                       ALU.mult, ALU.add).then_inc(s_stin, 1)

            def states(lo, hi):
                def add(g):
                    v.wait_ge(s_stin, 2 * g + 2)
                    v.wait_ge(s_pmm, g + 1)
                    for s in range(lo, hi):
                        if s:
                            v.wait_ge(s_state, 2 * STEPS * g + 2 * s)
                        for b in range(2):
                            d = slice(b * C, (b + 1) * C)
                            v.scalar_tensor_tensor(state[d, s + 1, d], state[d, s, d], DECAY,
                                                   ps_p[d, s * P + b * C:s * P + (b + 1) * C], ALU.mult, ALU.add
                                                   ).then_inc(s_state, 1)
                return add

            def logits(g):
                v.wait_ge(s_lmm, g + 1)
                if later(g):
                    v.wait_ge(s_topi, TILES * g)
                v.tensor_tensor(logit[:], ps_q[:, :].rearrange("p (t e) -> p t e", e=E), all_tiles(brr[:]),
                                ALU.add).then_inc(s_logit, 1)

            def destinations(g):
                if later(g):
                    v.wait_ge(s_rows, 2 * STEPS * g)
                v.wait_ge(s_logit, g + 1)
                dest = kc[:, K_DEST:K_DEST + K2 * NT].rearrange("p (k t) -> p k t", k=K2)
                v.tensor_copy(tail[:, :, :, 2:3], dest[:, :, bass.ds(g * TILES, TILES)].unsqueeze(3)
                              ).then_inc(s_tail, 1)

            def tops(g):
                for t in range(TILES):
                    v.max(top[:, t, :], logit[:, t, :]).then_inc(s_top, 1)

            def gaps(g):
                v.wait_ge(s_top, TILES * (g + 1))
                for k in range(K2):
                    v.tensor_tensor(tail[:, k, :, 1:2], top[:, :, 1 - k:2 - k], top[:, :, k:k + 1], ALU.subtract
                                    ).then_inc(s_tail, 1)

            def indices(g):
                for t in range(TILES):
                    v.max_index(topi[:, t, :], top[:, t, :], logit[:, t, :]).then_inc(s_topi, 1)

            def indices_float(g):
                v.wait_ge(s_topi, TILES * (g + 1))
                v.tensor_copy(topf[:], topi[:, :, 0:K2].rearrange("p t k -> p k t")).then_inc(s_hot, 1)

            def one_hots(g):
                v.wait_ge(s_hot, 3 * g + 1)
                if later(g):
                    v.wait_ge(s_pos, POS * g)
                    v.wait_ge(s_rank, g)
                v.tensor_tensor(hot[:], kc[:, K_IOTA:K_IOTA + E].unsqueeze(1).unsqueeze(1).to_broadcast([P, K2, TILES, E]),
                                topf[:].unsqueeze(3).to_broadcast([P, K2, TILES, E]), ALU.is_equal
                                ).then_inc(s_hot, 1)

            def both_hots(g):
                v.wait_ge(s_hot, 3 * g + 2)
                v.tensor_tensor(hots[:], hot[:, 0], hot[:, 1], ALU.add).then_inc(s_hot, 1)

            def residual(g):
                v.wait_ge(s_omm, g + 1)
                part = h2[:, bass.ds(g * TILES, TILES), :]
                v.scalar_tensor_tensor(part, ps_o[:, :].rearrange("p (t c) -> p t c", c=C),
                                       kc[:, K_QDEC:K_QDEC + 1], part, ALU.mult, ALU.add).then_inc(s_h2, 1)


            def move_on():
                def m(n):
                    v.wait_ge(s_move, n)
                v.wait_ge(s_count, GROUPS - LATE)
                v.scalar_tensor_tensor(moved, cnt[:], float(-FULL), base, ALU.add, ALU.is_gt).then_inc(s_move, 1)
                v.tensor_copy(stayed, cnt[:]).then_inc(s_move, 1)
                m(1)
                v.tensor_tensor_scan(order, zero[:], moved, 0.0, ALU.add, ALU.add).then_inc(s_move, 1)
                m(3)
                v.tensor_scalar(to, order, float(SPARE_BLOCKS * P), float((E * REGION - SPARE_BLOCKS) * P),
                                ALU.mult, ALU.add).then_inc(s_move, 1)
                m(4)
                v.tensor_tensor(dist, to, cnt[:], ALU.subtract).then_inc(s_move, 1)
                m(5)
                v.tensor_tensor(gone, dist, moved, ALU.mult).then_inc(s_move, 1)
                m(6)
                v.tensor_tensor(cnt[:], cnt[:], gone, ALU.add).then_inc(s_move, 1)
                m(7)

            v.wait_ge(zeroed, 13)
            v.wait_ge(img_ok, PARTS)
            pipeline(v, (2, sums2), (2, center2), (3, destinations), (3, tops), (3, gaps), (3, indices),
                     (2, roots2), (3, indices_float), (2, scaled2), (3, one_hots), (3, both_hots),
                     (0, sums1), (1, first_state), (0, center1),
                     (1, masked(0)), (1, carried), (3, ranked), (1, masked(1)), (3, counted), (-1, early_taps(1, 2)),
                     (1, states(0, 2)), (2, logits), (0, roots1),
                     (1, states(2, STEPS)), (0, scaled1), (3, picked), (1, residual), (3, slots_summed),
                     (-1, early_taps(2, EARLY)), (3, slots_out), before_last=move_on)

            v.wait_ge(s_count, GROUPS)
            v.tensor_scalar(rounded, count, 1.0 / P, 0.5 - 0.5 / P, ALU.mult, ALU.add).then_inc(s_blk, 1)
            b(14)
            v.tensor_scalar(rounded, rounded, ROUND, None, ALU.add).then_inc(s_blk, 1)
            b(15)
            v.tensor_scalar(blocks_, rounded, ROUND, None, ALU.subtract).then_inc(s_blk, 1)
            b(16)
            v.tensor_tensor_scan(ends, zero[:, 0:1].to_broadcast([P, EXT]), blocks_, 0.0, ALU.add, ALU.add
                                 ).then_inc(s_blk, 1)
            b(17)
            v.tensor_tensor(starts, ends, blocks_, ALU.subtract).then_inc(s_blk, 1)
            b(18)
            v.scalar_tensor_tensor(shift, ext_base, 1.0 / P, starts, ALU.mult, ALU.subtract).then_inc(s_blk, 1)

            def by_block(ap):
                return ap.unsqueeze(1).to_broadcast([P, UB, EXT])
            this = kc[:, K_BLK:K_BLK + UB].unsqueeze(2).to_broadcast([P, UB, EXT])
            begun, mine, at_e, at_b, row_b = (blk_at[:, k] for k in range(5))
            v.tensor_tensor(begun, by_block(starts), this, ALU.is_le).then_inc(s_blk, 1)
            v.tensor_tensor(mine, by_block(ends), this, ALU.is_gt).then_inc(s_blk, 1)
            b(21)
            v.tensor_tensor(mine, mine, begun, ALU.mult).then_inc(s_blk, 1)
            v.tensor_tensor(row_b, by_block(shift), this, ALU.add).then_inc(s_blk, 1)
            b(23)
            v.tensor_tensor(at_e, mine, by_block(owner), ALU.mult).then_inc(s_blk, 1)
            v.scalar_tensor_tensor(at_b, row_b, float(-EMPTY), mine, ALU.add, ALU.mult).then_inc(s_blk, 1)
            b(24)
            v.tensor_reduce(blk_f[:, 0, :], at_e, AX.X, ALU.add).then_inc(s_blk, 1)
            b(25)
            v.tensor_reduce(blk_f[:, 1, :], at_b, AX.X, ALU.add).then_inc(s_blk, 1)
            b(26)
            v.tensor_copy(blk_i[:, 0, :], blk_f[:, 0, :]).then_inc(s_blk, 1)
            b(27)
            v.tensor_scalar(blk_i[:, 1, :], blk_f[:, 1, :], float(EMPTY), None, ALU.add).then_inc(s_blk, 1)
            v.wait_ge(blk_in_row, 16)
            v.wait_ge(weights_in, 32)

            regs = [v.alloc_register(f"expert{k}") for k in range(UB)]

            def stage_unit(n, r):
                u = unit(n, r)
                v.load(regs, blk_row[0:1, 0, bass.ds(u * UB, UB)])
                if older(n, r, RING):
                    v.wait_ge(u_ymm, u - RING + 1)
                for k in range(UB):
                    e = v.snap(regs[k], min_val=0, max_val=E - 1)
                    v.tensor_copy(b2u[r][:, k, :], b2s[:, bass.ds(e * C, C)]).then_inc(u_b2, 1)
                    v.tensor_copy(stage[r][:, k, :], wall[:, bass.ds(e * WCOLS, WCOLS)]).then_inc(u_stage, 1)

            def dest_unit(n, r):
                v.wait_ge(u_in[r], UB * 16 * (n + 1))
                if later(n):
                    v.wait_ge(u_sent[r], UB * 16 * n)
                v.tensor_copy(ydst[r][:].unsqueeze(2), xin[r][:, :, DEST:DEST + 1]).then_inc(u_dst, 1)
                d = xin[r][:, :, GAP]
                v.tensor_scalar(gate[0][r][:, 0, :], d, 0.0, -1.0, ALU.max, ALU.mult).then_inc(u_gap, 1)
                v.scalar_tensor_tensor(gate[0][r][:, 1, :], d, -1.0, d, ALU.mult, ALU.min).then_inc(u_gap, 1)

            def gated_unit(n, r):
                u = unit(n, r)
                v.wait_ge(u_exp, u + 1)
                g1, g2 = gate[1][r], gate[2][r]
                v.tensor_scalar(g2[:, 1, :], g1[:, 1, :], 1.0, None, ALU.add).then_inc(u_gate, 1)
                v.wait_ge(u_gate, 3 * u + 1)
                v.reciprocal(g2[:, 0, :], g2[:, 1, :]).then_inc(u_gate, 1)
                v.wait_ge(u_gate, 3 * u + 2)
                v.tensor_tensor(g1[:, 1, :], g2[:, 0, :], g1[:, 0, :], ALU.mult).then_inc(u_gate, 1)
                v.wait_ge(u_ymm, u + 1)
                v.tensor_tensor(b2u[r], (ps_v, ps_p)[r % 2][:, 0:UB * C].rearrange("p (k c) -> p k c", k=UB),
                                b2u[r], ALU.add).then_inc(u_sum, 1)
                v.wait_ge(u_gate, 3 * u + 3)
                v.wait_ge(u_sum, u + 1)
                v.tensor_tensor(ysb[r], b2u[r], wide(g1[:, 1, :], UB), ALU.mult).then_inc(u_y, 1)

            units(v, (0, stage_unit), (0, dest_unit), (2, gated_unit))

            v.wait_ge(h_in, B * RING * 16)
            v.wait_ge(cls_y, 16)
            v.tensor_tensor(osb[:], ch2[0:1, :], ycls[:, 0, :], ALU.add).then_inc(cls_y, 1)
            v.wait_ge(cls_y, 17)
            v.tensor_tensor(osb[:], osb[:], ycls[:, 1, :], ALU.add).then_inc(cls_y, 1)
            for n in range(NT // FT):
                v.wait_ge(y_in[n % 4], 16 * (n // 4 + 1))
                part = h2[:, n * FT:(n + 1) * FT, :]
                v.tensor_tensor(part, part, yin[n % 4][:, 0], ALU.add).then_inc(y_sum, 1)
                v.wait_ge(y_sum, 2 * n + 1)
                v.tensor_tensor(part, part, yin[n % 4][:, 1], ALU.add).then_inc(y_sum, 1)

        @block.scalar
        def _(act):
            act.wait_ge(consts_in, 12 * 16)
            act.activation(bn_s[:, 4:5], bn_s[:, 3:4], ACT.Sqrt, bias=kc[:, K_EPS:K_EPS + 1]).then_inc(bn_std, 1)
            def cls_std(s, tag):
                cls_after(act, "ss" + tag)
                act.activation(cs[:, s + 2:s + 3], cs[:, s + 1:s + 2], ACT.Sqrt, scale=1.0 / C,
                               bias=kc[:, K_EPS:K_EPS + 1]).then_inc(cls_step, 1)
            cls_std(0, "")
            act.wait_ge(zeroed, 4)
            act.wait_ge(setup_v, 4)

            def normalise(q):
                for n in range(PARTS):
                    act.wait_ge(x_in[q][n], 16)
                    y = slice(n * IMG // PARTS, (n + 1) * IMG // PARTS)
                    act.activation(img[:, q, 1:1 + IMG, 1:1 + IMG][:, y, :], xs[:, q, y, :], ACT.Identity,
                                   bias=bn_s[:, 7:8], scale=bn_s[:, 5:6]).then_inc(img_ok, 1)
            normalise(0)
            cls_std(4, "2")

            def rest_of_images(g):
                if isinstance(g, int) and g == 0:
                    normalise(1)

            def hn_back(g):
                act.wait_ge(s_turn1, g + 1)
                if later(g):
                    act.wait_ge(s_vmm, g)
                act.copy(hnT[:], ps_turn[:, :]).then_inc(s_hnT, 1)

            def with_bias(g, n, bank, dst, mm, done):
                act.wait_ge(mm, g + 1)
                act.activation(dst[:], bank[:, :], ACT.Identity, bias=bq[:, n:n + 1]).then_inc(done, 1)

            def kv_back(g):
                if later(g):
                    act.wait_ge(s_score, 2 * g)
                with_bias(g, 1, ps_k, kT, s_kmm, s_k)
                if later(g):
                    act.wait_ge(s_vturn, g)
                with_bias(g, 2, ps_v, vT, s_vmm, s_v)

            def q_back(g):
                if later(g):
                    act.wait_ge(s_omm, g)
                with_bias(g, 0, ps_q, qT, s_qmm, s_q)

            def squares(g, xc_, sq_, sums, s_sq):
                for t in range(TILES):
                    act.activation(sq_[:, t, :], xc_[:, t, :], ACT.Square, accum_out=sums[:, 1, t:t + 1]
                                   ).then_inc(s_sq, 1)
                act.wait_ge(s_sq, SQ * g + TILES)

            def square2(g):
                act.wait_ge(s_ln2, LN * g + 2)
                squares(g, xc2, sq2, ssum2, s_sq2)
                act.activation(ssum2[:, 2, :], ssum2[:, 1, :], ACT.Sqrt, scale=1.0 / C,
                               bias=kc[:, K_EPS:K_EPS + 1]).then_inc(s_sq2, 1)

            def kv_tokens(g):
                if later(g):
                    act.wait_ge(s_omm, g)
                act.wait_ge(s_vturn, g + 1)
                act.activation(vtok[:], ps_v[:, :], ACT.Identity, scale=kc[:, K_VDEC:K_VDEC + 1]
                               ).then_inc(s_vtok, 1)
                act.wait_ge(s_kturn, g + 1)
                act.copy(ktok[:], ps_tok[:, :]).then_inc(s_ktok, 1)

            def hn2_back(g):
                act.wait_ge(s_turn2, g + 1)
                if later(g):
                    act.wait_ge(s_lmm, g)
                act.copy(hn2T[:], ps_turn[:, :]).then_inc(s_hn2T, 1)

            def hn2_keep(g):
                act.wait_ge(s_ln2, LN * (g + 1))
                if later(g):
                    act.wait_ge(s_rows, 2 * STEPS * g)
                act.copy(hn2r[:], hn2[:]).then_inc(s_hn2r, 1)

            def fill_rows(g):
                act.wait_ge(s_tail, TAIL * (g + 1))
                act.wait_ge(s_hn2r, g + 1)
                for s in range(STEPS):
                    if later(g):
                        act.wait_ge(s_sent[s], 64 * g)
                    t = slice(2 * s, 2 * s + 2)
                    act.copy(rows[:, :, t, 0:C], hn2r[:, t, :].unsqueeze(1).to_broadcast([P, K2, 2, C])
                             ).then_inc(s_rows, 1)
                    act.copy(rows[:, :, t, C:ROW], tail[:, :, t, :]).then_inc(s_rows, 1)

            def h_bias(g):
                act.wait_ge(s_conv, g + 1)
                if later(g):
                    act.wait_ge(s_htok, g)
                act.activation(hT[:], ps_conv[:, :], ACT.Identity, bias=lb[:, 1:2]).then_inc(s_hT, 1)

            def first_tap(g):
                if later(g):
                    act.wait_ge(s_conv, g)
                if isinstance(g, int):
                    act.wait_ge(img_ok, PARTS if g < 2 else PAIRS * PARTS)
                act.activation(early_rows, tap_view(g, 0), ACT.Copy, scale=cw[:, 0:1]).then_inc(s_early, 1)

            def h_back(g):
                act.wait_ge(s_htok, g + 1)
                act.copy(h2[:, bass.ds(g * TILES, TILES), :].rearrange("p t c -> p (t c)"), ps_tok[:, :]
                         ).then_inc(s_h, 1)

            def square1(g):
                act.wait_ge(s_ln1, LN * g + 2)
                squares(g, xc, sq, ssum, s_sq1)
                act.activation(ssum[:, 2, :], ssum[:, 1, :], ACT.Sqrt, scale=1.0 / C,
                               bias=kc[:, K_EPS:K_EPS + 1]).then_inc(s_sq1, 1)

            act.wait_ge(bias_ok, 1)
            pipeline(act, (2, square2), (0, h_bias), (1, kv_back), (0, h_back), (1, q_back), (-1, first_tap),
                     (1, kv_tokens), (2, hn2_back), (0, square1), (3, fill_rows),
                     (2, hn2_keep), (0, hn_back), (0, rest_of_images))

            def turned_unit(n, r):
                u = unit(n, r)
                act.wait_ge(u_gap, 2 * (u + 1))
                act.activation(gate[1][r], gate[0][r], ACT.Exp).then_inc(u_exp, 1)
                act.wait_ge(u_turn, u + 1)
                if older(n, r):
                    act.wait_ge(u_hmm, u - 1)
                act.copy(xT[r % 2][0:ONE + 1, :], (ps_conv, ps_tok)[r % 2][0:ONE + 1, :]).then_inc(u_xT, 1)

            def hidden_unit(n, r):
                u = unit(n, r)
                act.wait_ge(u_hmm, u + 1)
                if older(n, r):
                    act.wait_ge(u_ymm, u - 1)
                act.activation(hid[r % 2], (ps_q, ps_k)[r % 2][:, :], ACT.Relu).then_inc(u_hid, 1)

            act.wait_ge(s_blk, PADS)
            pad_extents(act, PADS_SP, PADS_SP + 8, filled)
            act.wait_ge(s_blk, BLK)
            act.dma_start(blk_dram.rearrange("a p k -> p a k"), blk_i[:]).then_inc(blk_out, 16)
            pad_extents(act, PADS_SP + 8, PADS_ACT, filled)
            act.wait_ge(blk_out, 16)
            act.dma_start(blk_row[:], blk_dram.rearrange("a p k -> a (p k)").unsqueeze(0)).then_inc(blk_in_row, 16)

            units(act, (0, turned_unit), (1, hidden_unit))

            act.wait_ge(cls_y, 18)
            for b in range(B):
                act.dma_start(out[b, 0:1, :], osb[:]).then_inc(out_done, 16)
            for n in range(NT // FT):
                act.wait_ge(y_sum, 2 * (n + 1))
                b, j = divmod(n * FT, RUN)
                act.dma_start(out[b, 1:1 + NPIX, :].rearrange("(p j) c -> p j c", p=P)[:, j:j + FT, :],
                              h_run[:, b, j:j + FT, :]).then_inc(out_done, 16)


def kernel(**inputs):
    import concourse.bacc as bacc
    from concourse.bass_utils import run_bass_kernel_spmd

    a = {n: np.asarray(v) for n, v in inputs.items()}

    def twice(v):
        return np.ascontiguousarray(np.concatenate([v, v], 0))

    def rows(v):
        return np.ascontiguousarray(np.broadcast_to(v.reshape(1, -1), (P, v.size)))

    def blocks(m):
        d = np.zeros((P, P), m.dtype)
        d[:C, :C] = m
        d[C:, C:] = m
        return d

    wqkv = a["L0_attn_Wqkv"]
    pack = np.zeros((P, E, WCOLS), np.float32)
    pack[:C, :, :HID] = a["L0_ffn_W1"].transpose(1, 0, 2)
    pack[ONE, :, :HID] = a["L0_ffn_b1"]
    pack[:, :, HID:] = a["L0_ffn_W2"].transpose(1, 0, 2)
    arrays = {
        "x": a["x"].reshape(PAIRS, 2, NPIX, C).transpose(0, 1, 3, 2).reshape(PAIRS, P, NPIX),
        "cls_rows": rows(a["cls_tok"]),
        "consts": constants(),
        "bn": twice(np.stack([a["L0_tok_bn_gamma"], a["L0_tok_bn_beta"], a["L0_tok_bn_mean"], a["L0_tok_bn_var"]], 1)),
        "conv_w": twice(a["L0_tok_conv_w"].reshape(C, TAPS)),
        "conv_b": twice(a["L0_tok_conv_b"].reshape(C, 1)),
        "lin_w": blocks(a["L0_tok_lin_w"].T),
        "lin_b": twice(a["L0_tok_lin_b"].reshape(C, 1)),
        "wqkv": np.stack([blocks(wqkv[:, n * C:(n + 1) * C]) for n in range(3)], 1),
        "bqkv_col": twice(a["L0_attn_bqkv"].reshape(3, C).T),
        "bqkv_row": rows(a["L0_attn_bqkv"]),
        "wr": blocks(a["L0_ffn_Wr"]),
        "br_row": rows(a["L0_ffn_br"]),
        "experts": pack.reshape(P, E * WCOLS),
        "b2_row": a["L0_ffn_b2"].reshape(1, E * C),
    }
    nc = bacc.Bacc("TRN2", target_bir_lowering=False, num_devices=1)
    args = []
    for name, v in arrays.items():
        arrays[name] = v = np.ascontiguousarray(v)
        args.append(nc.dram_tensor(name, v.shape, mybir.dt.from_np(v.dtype), kind="ExternalInput").ap())
    args.append(nc.dram_tensor("out", (B, NPIX + 1, C), F32, kind="ExternalOutput").ap())
    tower(nc, *args)
    r = run_bass_kernel_spmd(nc, [arrays], core_ids=[0])
    return r.results[0]["out"]
```
